# Optimizing a Trainium2 kernel written in Bass

```python
import numpy as np
import jax
import jax.numpy as jnp

def _softmax(x, axis=-1):
    return jax.nn.softmax(x, axis=axis)

def _gelu(x):
    return jax.nn.gelu(x, approximate=True)

def _silu(x):
    return jax.nn.silu(x)

def _sigmoid(x):
    return jax.nn.sigmoid(x)

def _layernorm(x, axis=-1, eps=1e-05):
    m = jnp.mean(x, axis=axis, keepdims=True)
    v = jnp.var(x, axis=axis, keepdims=True)
    return (x - m) / jnp.sqrt(v + eps)

def _scatter_add(tgt, idx, src, axis=0):
    return tgt.at[idx].add(src)

def _segment_sum(src, seg, n):
    return jax.ops.segment_sum(src, seg, n)
kernel_name = 'mk_vit_tower_d2_tok_img256_r4_9b9c5b'

def setup_inputs(seed: int=0):
    np.random.seed(seed)
    _w = jnp.asarray

    def _rec_inputs():
        import jax
        import jax.numpy as jnp
        _rk = jax.random.key(seed)
        x = -0.000928989 + 1.00043 * jax.random.normal(jax.random.fold_in(_rk, 1), (64, 64, 64, 1), jnp.float32)
        return x
    x = _rec_inputs()

    def _L0_tok_setup():
        import jax, jax.numpy as jnp
        import numpy as np
        B, S, D_A, D_V, D_U, L, M1, M2 = (16, 64, 3, 32, 1, 4, 12, 12)
        MID = 4 * D_U

        def conv1x1(x, w, b):
            return jnp.einsum('bixy,oi->boxy', x, w) + b[None, :, None, None]

        def fourier_layer(x, fw_i):
            Bm, C, M, N = x.shape
            x_ft = jnp.fft.rfft2(x, s=(M, N), norm='ortho')
            w_lo = fw_i[0, ..., 0] + 1j * fw_i[0, ..., 1]
            w_hi = fw_i[1, ..., 0] + 1j * fw_i[1, ..., 1]
            lo = jnp.einsum('bixy,ioxy->boxy', x_ft[:, :, :M1, :M2], w_lo)
            hi = jnp.einsum('bixy,ioxy->boxy', x_ft[:, :, -M1:, :M2], w_hi)
            out_ft = jnp.zeros(x_ft.shape, dtype=x_ft.dtype)
            out_ft = out_ft.at[:, :, :M1, :M2].set(lo)
            out_ft = out_ft.at[:, :, -M1:, :M2].set(hi)
            return jnp.fft.irfft2(out_ft, s=(M, N), norm='ortho')

        def make_grid(b, sx, sy):
            gx = jnp.broadcast_to(jnp.linspace(0.0, 1.0, sx)[None, :, None], (b, sx, sy))
            gy = jnp.broadcast_to(jnp.linspace(0.0, 1.0, sy)[None, None, :], (b, sx, sy))
            return jnp.stack([gx, gy], axis=-1)
        key = jax.random.key(seed)
        ks = jax.random.split(key, 12)
        sc_v = 1.0 / np.sqrt(D_V)
        inp = {'x': jax.random.normal(ks[0], (B, S, S, D_A - 2), dtype=jnp.float32), 'p_w': jax.random.normal(ks[1], (D_V, D_A), dtype=jnp.float32) / np.sqrt(D_A), 'p_b': jnp.zeros((D_V,), dtype=jnp.float32), 'fw': jax.random.normal(ks[2], (L, 2, D_V, D_V, M1, M2, 2), dtype=jnp.float32) * sc_v, 'w1_w': jax.random.normal(ks[3], (L, D_V, D_V), dtype=jnp.float32) * sc_v, 'w1_b': jnp.zeros((L, D_V), dtype=jnp.float32), 'w2_w': jax.random.normal(ks[4], (L, D_V, D_V), dtype=jnp.float32) * sc_v, 'w2_b': jnp.zeros((L, D_V), dtype=jnp.float32), 'q1_w': jax.random.normal(ks[5], (MID, D_V), dtype=jnp.float32) * sc_v, 'q1_b': jnp.zeros((MID,), dtype=jnp.float32), 'q2_w': jax.random.normal(ks[6], (D_U, MID), dtype=jnp.float32) / np.sqrt(MID), 'q2_b': jnp.zeros((D_U,), dtype=jnp.float32)}
        return inp
    _L0_tok_all = _L0_tok_setup()
    _L0_tok_in = {k: v for k, v in _L0_tok_all.items() if k in ('p_w', 'p_b', 'fw', 'w1_w', 'w1_b', 'w2_w', 'w2_b', 'q1_w', 'q1_b', 'q2_w', 'q2_b')}
    del _L0_tok_all

    def _L0_attn_setup():
        import jax, jax.numpy as jnp
        import numpy as np
        GAMMA = 0.96875
        ROPE_THETA = 10000.0

        def _rope(x):
            B, S, d = x.shape
            inv_freq = 1.0 / ROPE_THETA ** (jnp.arange(0, d, 2, dtype=jnp.float32) / d)
            angles = jnp.arange(S, dtype=jnp.float32)[:, None] * inv_freq[None, :]
            cos = jnp.cos(angles).astype(x.dtype)
            sin = jnp.sin(angles).astype(x.dtype)
            xs = x.reshape(B, S, d // 2, 2)
            x0, x1 = (xs[..., 0], xs[..., 1])
            out = jnp.stack([x0 * cos - x1 * sin, x1 * cos + x0 * sin], axis=-1)
            return out.reshape(B, S, d)

        def _decay_mask(S, dtype):
            n = jnp.arange(S)[:, None]
            m = jnp.arange(S)[None, :]
            diff = n - m
            D = jnp.exp(jnp.maximum(diff, 0).astype(jnp.float32) * np.log(GAMMA))
            return jnp.where(diff >= 0, D, 0.0).astype(dtype)
        key = jax.random.key(seed)
        k1, k2, k3, k4 = jax.random.split(key, 4)
        H = 64
        X = jax.random.normal(k1, (4, 2048, H), dtype=jnp.float32)
        W_Q = jax.random.normal(k2, (H, H), dtype=jnp.float32) / H
        W_K = jax.random.normal(k3, (H, H), dtype=jnp.float32) / H
        W_V = jax.random.normal(k4, (H, H), dtype=jnp.float32) / H
        return {'X': X, 'W_Q': W_Q, 'W_K': W_K, 'W_V': W_V}
    _L0_attn_all = _L0_attn_setup()
    _L0_attn_in = {k: v for k, v in _L0_attn_all.items() if k in ('W_Q', 'W_K', 'W_V')}
    del _L0_attn_all

    def _L0_ffn_setup():
        import jax, jax.numpy as jnp
        import numpy as np
        B, T, D, H, E = (16, 1024, 64, 128, 8)
        key = jax.random.key(seed)
        ks = jax.random.split(key, 5)
        x = jax.random.normal(ks[0], (B, T, D), dtype=jnp.float32)
        gate_w = jax.random.normal(ks[1], (D, E), dtype=jnp.float32) * 0.02
        gate_b = jnp.zeros((E,), dtype=jnp.float32)
        W1 = jax.random.normal(ks[2], (E, D, H), dtype=jnp.float32) * 0.02
        b1 = jnp.zeros((E, H), dtype=jnp.float32)
        W2 = jax.random.normal(ks[3], (E, H, D), dtype=jnp.float32) * 0.02
        b2 = jnp.zeros((E, D), dtype=jnp.float32)
        return {'x': x, 'gate_w': gate_w, 'gate_b': gate_b, 'W1': W1, 'b1': b1, 'W2': W2, 'b2': b2}
    _L0_ffn_all = _L0_ffn_setup()
    _L0_ffn_in = {k: v for k, v in _L0_ffn_all.items() if k in ('gate_w', 'gate_b', 'W1', 'b1', 'W2', 'b2')}
    del _L0_ffn_all

    def _L1_attn_setup():
        import jax, jax.numpy as jnp
        import numpy as np
        B, L, D = (4, 1024, 64)
        key = jax.random.key(seed)
        kx, kq, kk, kv, ko = jax.random.split(key, 5)
        std = 0.02
        return {'x': jax.random.normal(kx, (B, L, D), dtype=jnp.float32), 'Wq': std * jax.random.normal(kq, (D, D), dtype=jnp.float32), 'Wk': std * jax.random.normal(kk, (D, D), dtype=jnp.float32), 'Wv': std * jax.random.normal(kv, (D, D), dtype=jnp.float32), 'Wo': std * jax.random.normal(ko, (D, D), dtype=jnp.float32)}
    _L1_attn_all = _L1_attn_setup()
    _L1_attn_in = {k: v for k, v in _L1_attn_all.items() if k in ('Wq', 'Wk', 'Wv', 'Wo')}
    del _L1_attn_all

    def _L1_ffn_setup():
        import jax, jax.numpy as jnp
        import numpy as np
        NUM_EXPERTS = 8
        TOP_K = 2
        B, S, D = (8, 2048, 64)

        def _moe(tokens, router_w, w1, b1, w2, b2):
            N = tokens.shape[0]
            E = router_w.shape[0]
            logits = tokens.astype(jnp.float32) @ router_w.astype(jnp.float32).T
            probs = jax.nn.softmax(logits, axis=-1)
            rw, re = jax.lax.top_k(probs, TOP_K)
            if TOP_K > 1:
                rw = rw / jnp.maximum(rw.sum(-1, keepdims=True), 1e-12)
            rw = rw.astype(tokens.dtype)
            combine = jnp.zeros((N, E), tokens.dtype).at[jnp.arange(N)[:, None], re].set(rw)
            out = tokens
            for e in range(E):
                h = jax.nn.gelu(tokens @ w1[e] + b1[e], approximate=False)
                y = h @ w2[e] + b2[e]
                out = out + combine[:, e:e + 1] * y
            return out
        key = jax.random.key(seed)
        ks = jax.random.split(key, 4)
        scale = 1.0 / np.sqrt(D).astype(np.float32)
        return {'input_embeddings': jax.random.normal(ks[0], (B, S, D), jnp.float32), 'router_w': jax.random.normal(ks[1], (NUM_EXPERTS, D), jnp.float32) * scale, 'w1': jax.random.normal(ks[2], (NUM_EXPERTS, D, D), jnp.float32) * scale, 'b1': jnp.zeros((NUM_EXPERTS, D), jnp.float32), 'w2': jax.random.normal(ks[3], (NUM_EXPERTS, D, D), jnp.float32) * scale, 'b2': jnp.zeros((NUM_EXPERTS, D), jnp.float32)}
    _L1_ffn_all = _L1_ffn_setup()
    _L1_ffn_in = {k: v for k, v in _L1_ffn_all.items() if k in ('router_w', 'w1', 'b1', 'w2', 'b2')}
    del _L1_ffn_all
    return {'x': x, 'L0_tok_p_w': _L0_tok_in['p_w'], 'L0_tok_p_b': _L0_tok_in['p_b'], 'L0_tok_fw': _L0_tok_in['fw'], 'L0_tok_w1_w': _L0_tok_in['w1_w'], 'L0_tok_w1_b': _L0_tok_in['w1_b'], 'L0_tok_w2_w': _L0_tok_in['w2_w'], 'L0_tok_w2_b': _L0_tok_in['w2_b'], 'L0_tok_q1_w': _L0_tok_in['q1_w'], 'L0_tok_q1_b': _L0_tok_in['q1_b'], 'L0_tok_q2_w': _L0_tok_in['q2_w'], 'L0_tok_q2_b': _L0_tok_in['q2_b'], 'L0_attn_W_Q': _L0_attn_in['W_Q'], 'L0_attn_W_K': _L0_attn_in['W_K'], 'L0_attn_W_V': _L0_attn_in['W_V'], 'L0_ffn_gate_w': _L0_ffn_in['gate_w'], 'L0_ffn_gate_b': _L0_ffn_in['gate_b'], 'L0_ffn_W1': _L0_ffn_in['W1'], 'L0_ffn_b1': _L0_ffn_in['b1'], 'L0_ffn_W2': _L0_ffn_in['W2'], 'L0_ffn_b2': _L0_ffn_in['b2'], 'L1_attn_Wq': _L1_attn_in['Wq'], 'L1_attn_Wk': _L1_attn_in['Wk'], 'L1_attn_Wv': _L1_attn_in['Wv'], 'L1_attn_Wo': _L1_attn_in['Wo'], 'L1_ffn_router_w': _L1_ffn_in['router_w'], 'L1_ffn_w1': _L1_ffn_in['w1'], 'L1_ffn_b1': _L1_ffn_in['b1'], 'L1_ffn_w2': _L1_ffn_in['w2'], 'L1_ffn_b2': _L1_ffn_in['b2']}

def reference(x, L0_tok_p_w, L0_tok_p_b, L0_tok_fw, L0_tok_w1_w, L0_tok_w1_b, L0_tok_w2_w, L0_tok_w2_b, L0_tok_q1_w, L0_tok_q1_b, L0_tok_q2_w, L0_tok_q2_b, L0_attn_W_Q, L0_attn_W_K, L0_attn_W_V, L0_ffn_gate_w, L0_ffn_gate_b, L0_ffn_W1, L0_ffn_b1, L0_ffn_W2, L0_ffn_b2, L1_attn_Wq, L1_attn_Wk, L1_attn_Wv, L1_attn_Wo, L1_ffn_router_w, L1_ffn_w1, L1_ffn_b1, L1_ffn_w2, L1_ffn_b2):
    import jax
    import jax.numpy as jnp

    def _L0_tok_ref(x, p_w, p_b, fw, w1_w, w1_b, w2_w, w2_b, q1_w, q1_b, q2_w, q2_b):
        import jax, jax.numpy as jnp
        import numpy as np
        B, S, D_A, D_V, D_U, L, M1, M2 = (16, 64, 3, 32, 1, 4, 12, 12)
        MID = 4 * D_U

        def conv1x1(x, w, b):
            return jnp.einsum('bixy,oi->boxy', x, w) + b[None, :, None, None]

        def fourier_layer(x, fw_i):
            Bm, C, M, N = x.shape
            x_ft = jnp.fft.rfft2(x, s=(M, N), norm='ortho')
            w_lo = fw_i[0, ..., 0] + 1j * fw_i[0, ..., 1]
            w_hi = fw_i[1, ..., 0] + 1j * fw_i[1, ..., 1]
            lo = jnp.einsum('bixy,ioxy->boxy', x_ft[:, :, :M1, :M2], w_lo)
            hi = jnp.einsum('bixy,ioxy->boxy', x_ft[:, :, -M1:, :M2], w_hi)
            out_ft = jnp.zeros(x_ft.shape, dtype=x_ft.dtype)
            out_ft = out_ft.at[:, :, :M1, :M2].set(lo)
            out_ft = out_ft.at[:, :, -M1:, :M2].set(hi)
            return jnp.fft.irfft2(out_ft, s=(M, N), norm='ortho')

        def make_grid(b, sx, sy):
            gx = jnp.broadcast_to(jnp.linspace(0.0, 1.0, sx)[None, :, None], (b, sx, sy))
            gy = jnp.broadcast_to(jnp.linspace(0.0, 1.0, sy)[None, None, :], (b, sx, sy))
            return jnp.stack([gx, gy], axis=-1)
        b, sx, sy = (x.shape[0], x.shape[1], x.shape[2])
        grid = make_grid(b, sx, sy)
        h = jnp.concatenate([x, grid], axis=-1)
        h = jnp.transpose(h, (0, 3, 1, 2))
        h = conv1x1(h, p_w, p_b)
        for i in range(L):
            x1 = fourier_layer(h, fw[i])
            x1 = jax.nn.relu(conv1x1(x1, w1_w[i], w1_b[i]))
            x1 = conv1x1(x1, w2_w[i], w2_b[i])
            h = h + x1
        h = conv1x1(h, q1_w, q1_b)
        h = jax.nn.relu(h)
        h = conv1x1(h, q2_w, q2_b)
        return jnp.squeeze(h)

    def _L0_attn_ref(X, W_Q, W_K, W_V):
        import jax, jax.numpy as jnp
        import numpy as np
        GAMMA = 0.96875
        ROPE_THETA = 10000.0

        def _rope(x):
            B, S, d = x.shape
            inv_freq = 1.0 / ROPE_THETA ** (jnp.arange(0, d, 2, dtype=jnp.float32) / d)
            angles = jnp.arange(S, dtype=jnp.float32)[:, None] * inv_freq[None, :]
            cos = jnp.cos(angles).astype(x.dtype)
            sin = jnp.sin(angles).astype(x.dtype)
            xs = x.reshape(B, S, d // 2, 2)
            x0, x1 = (xs[..., 0], xs[..., 1])
            out = jnp.stack([x0 * cos - x1 * sin, x1 * cos + x0 * sin], axis=-1)
            return out.reshape(B, S, d)

        def _decay_mask(S, dtype):
            n = jnp.arange(S)[:, None]
            m = jnp.arange(S)[None, :]
            diff = n - m
            D = jnp.exp(jnp.maximum(diff, 0).astype(jnp.float32) * np.log(GAMMA))
            return jnp.where(diff >= 0, D, 0.0).astype(dtype)
        B, S, _ = X.shape
        D = _decay_mask(S, X.dtype)
        Q = _rope(X @ W_Q)
        K = _rope(X @ W_K)
        V = X @ W_V
        ret = jnp.einsum('bqd,bkd->bqk', Q, K) * D[None]
        return ret @ V

    def _L0_ffn_ref(x, gate_w, gate_b, W1, b1, W2, b2):
        import jax, jax.numpy as jnp
        import numpy as np
        B, T, D, H, E = (16, 1024, 64, 128, 8)
        Bb, Tt, Dd = x.shape
        Ee = gate_w.shape[1]
        xf = x.reshape(-1, Dd)
        N = xf.shape[0]
        logits = xf @ gate_w + gate_b
        probs = jax.nn.softmax(logits, axis=-1)
        top2_vals, top2_idx = jax.lax.top_k(probs, 2)
        cw = jnp.zeros((N, Ee), dtype=xf.dtype).at[jnp.arange(N)[:, None], top2_idx].add(top2_vals)

        def step(acc, params):
            w1, bb1, w2, bb2, we = params
            h = jax.nn.gelu(xf @ w1 + bb1, approximate=False)
            y = h @ w2 + bb2
            return (acc + we[:, None] * y, None)
        out, _ = jax.lax.scan(step, jnp.zeros_like(xf), (W1, b1, W2, b2, cw.T))
        return out.reshape(Bb, Tt, Dd)

    def _L1_attn_ref(x, Wq, Wk, Wv, Wo):
        import jax, jax.numpy as jnp
        import numpy as np
        B, L, D = (4, 1024, 64)
        q = x @ Wq.T
        k = x @ Wk.T
        v = x @ Wv.T
        logits = jnp.einsum('bld,bmd->blm', q, k)
        Lq = x.shape[1]
        causal_mask = jnp.triu(jnp.ones((Lq, Lq), dtype=bool), k=1)
        logits = jnp.where(causal_mask[None], jnp.asarray(0.0, logits.dtype), logits)
        attn = jax.nn.relu(logits)
        row_counts = jnp.maximum(jnp.arange(Lq, dtype=attn.dtype), 1.0)
        attn = attn / row_counts[None, :, None]
        ctx = jnp.einsum('blm,bmd->bld', attn, v)
        return ctx @ Wo.T

    def _L1_ffn_ref(input_embeddings, router_w, w1, b1, w2, b2):
        import jax, jax.numpy as jnp
        import numpy as np
        NUM_EXPERTS = 8
        TOP_K = 2
        B, S, D = (8, 2048, 64)

        def _moe(tokens, router_w, w1, b1, w2, b2):
            N = tokens.shape[0]
            E = router_w.shape[0]
            logits = tokens.astype(jnp.float32) @ router_w.astype(jnp.float32).T
            probs = jax.nn.softmax(logits, axis=-1)
            rw, re = jax.lax.top_k(probs, TOP_K)
            if TOP_K > 1:
                rw = rw / jnp.maximum(rw.sum(-1, keepdims=True), 1e-12)
            rw = rw.astype(tokens.dtype)
            combine = jnp.zeros((N, E), tokens.dtype).at[jnp.arange(N)[:, None], re].set(rw)
            out = tokens
            for e in range(E):
                h = jax.nn.gelu(tokens @ w1[e] + b1[e], approximate=False)
                y = h @ w2[e] + b2[e]
                out = out + combine[:, e:e + 1] * y
            return out
        b, s, d = input_embeddings.shape
        tokens = input_embeddings.reshape(b * s, d)
        return _moe(tokens, router_w, w1, b1, w2, b2).reshape(b, s, d)
    h = _L0_tok_ref(x, L0_tok_p_w, L0_tok_p_b, L0_tok_fw, L0_tok_w1_w, L0_tok_w1_b, L0_tok_w2_w, L0_tok_w2_b, L0_tok_q1_w, L0_tok_q1_b, L0_tok_q2_w, L0_tok_q2_b)
    h = h + _L0_attn_ref(_layernorm(h, axis=-1), L0_attn_W_Q, L0_attn_W_K, L0_attn_W_V)
    h = h + _L0_ffn_ref(_layernorm(h, axis=-1), L0_ffn_gate_w, L0_ffn_gate_b, L0_ffn_W1, L0_ffn_b1, L0_ffn_W2, L0_ffn_b2)
    h = h + _L1_attn_ref(_layernorm(h, axis=-1), L1_attn_Wq, L1_attn_Wk, L1_attn_Wv, L1_attn_Wo)
    h = h + _L1_ffn_ref(_layernorm(h, axis=-1), L1_ffn_router_w, L1_ffn_w1, L1_ffn_b1, L1_ffn_w2, L1_ffn_b2)
    return h

_drawn_inputs = setup_inputs


def setup_inputs(seed=0):
    import zlib

    import numpy as np

    out = dict(_drawn_inputs(seed))
    spreads = {'L0_tok_p_b': (0.0, 0.1),
     'L0_tok_w1_b': (0.0, 0.1),
     'L0_tok_w2_b': (0.0, 0.1),
     'L0_tok_q1_b': (0.0, 0.1),
     'L0_ffn_gate_b': (0.0, 0.1),
     'L0_ffn_b1': (0.0, 0.401),
     'L0_ffn_b2': (0.0, 0.1),
     'L1_ffn_b1': (0.0, 0.417),
     'L1_ffn_b2': (0.0, 0.1)}
    factors = {'L0_ffn_W1': 2.872,
     'L0_ffn_W2': 2.829,
     'L1_attn_Wq': 5.807,
     'L1_attn_Wk': 6.055,
     'L1_attn_Wv': 4.956,
     'L1_attn_Wo': 5.476}
    for name, (base, spread) in spreads.items():
        noise = np.random.default_rng([zlib.crc32(name.encode()), seed]).standard_normal(out[name].shape)
        drawn = base * np.exp(spread * noise) if base else spread * noise
        out[name] = jnp.asarray(drawn.astype(out[name].dtype))
    for name, factor in factors.items():
        out[name] = (out[name] * factor).astype(out[name].dtype)
    return out
```

```python
import concourse.bass as bass
from concourse import mybir
from contextlib import ExitStack
import numpy as np

B, S, C, L, M, MID = 64, 64, 32, 4, 12, 4
KX = 2 * M
NC_, BH, BQ = 8, 2, 4
CH = BH * BQ
NB = B // BQ
OG = 8
O4, Y32 = 4, 32
COLS = BQ * BH * S
SPEC = B * M
HALF = SPEC // 2
UNITS = NC_ * OG


def dft_constants():
    n = np.arange(S)
    kx = np.concatenate([np.arange(M), np.arange(S - M, S)])
    ky = np.arange(M)
    rt = np.sqrt(S)
    wx = 2 * np.pi * np.outer(kx, n) / S
    wy = 2 * np.pi * np.outer(ky, n) / S
    cx, sx, cy, sy = np.cos(wx) / rt, np.sin(wx) / rt, np.cos(wy) / rt, np.sin(wy) / rt
    twice = np.where(ky == 0, 1.0, 2.0)[:, None]
    inv_x = np.zeros((BH, 2, 2, M, 2, BH, S))
    fwd_x = np.zeros((BH, S, 2, BH, 2, 2, M))
    for b in range(BH):
        for g in range(2):
            c, s = cx[g * M:(g + 1) * M], sx[g * M:(g + 1) * M]
            inv_x[b, g, 0, :, 0, b], inv_x[b, g, 1, :, 0, b] = c, -s
            inv_x[b, g, 0, :, 1, b], inv_x[b, g, 1, :, 1, b] = s, c
            fwd_x[b, :, 0, b, g, 0], fwd_x[b, :, 1, b, g, 0] = c.T, s.T
            fwd_x[b, :, 0, b, g, 1], fwd_x[b, :, 1, b, g, 1] = -s.T, c.T
    inv_y = np.zeros((128, 2, O4, Y32))
    fwd_y = np.zeros((O4, Y32, 2, 2, O4, M))
    for o in range(O4):
        for h in range(2):
            y = slice(h * Y32, (h + 1) * Y32)
            inv_y[o * M:(o + 1) * M, h, o] = (twice * cy)[:, y]
            inv_y[64 + o * M:64 + (o + 1) * M, h, o] = -(twice * sy)[:, y]
            fwd_y[o, :, h, 0, o] = cy[:, y].T
            fwd_y[o, :, h, 1, o] = -sy[:, y].T
    first_y = np.concatenate([cy.T, -sy.T], 1)
    line = np.linspace(0.0, 1.0, S)
    grids = []
    for image in (np.broadcast_to(line[:, None], (S, S)), np.broadcast_to(line[None, :], (S, S))):
        f = (cx - 1j * sx) @ image @ (cy - 1j * sy).T
        f = f.reshape(2, M, M)
        grids.append(np.stack([f.real, f.imag], 1).reshape(4 * M, M))
    grid_spec = np.broadcast_to(np.stack(grids, 1)[:, :, None, :, None], (4 * M, 2, NB, M, BQ)).reshape(4 * M, 2, SPEC)
    gl = np.ones((3, 2, MID, Y32))
    gl[1] = line.reshape(2, 1, Y32)
    gr = np.ones((3, S))
    gr[0] = line
    eye = np.zeros((O4, Y32, MID, Y32))
    eye[:, np.arange(Y32), :, np.arange(Y32)] = 1.0
    pick = np.zeros((S, 2, MID, Y32))
    for h in range(2):
        for y in range(Y32):
            pick[h * Y32 + y, h, :, y] = 1.0
    sign = np.ones((128, 1))
    for g in range(2):
        sign[64 * g + 32:64 * g + 64] = -1.0
    f = lambda a, *s: np.ascontiguousarray(a.reshape(*s), dtype=np.float32)
    out = {
        "inv_x": f(T_SCALE * inv_x, 96, 2 * BH * S), "fwd_x": f(fwd_x / G_SCALE, 128, 2 * 96), "first_y": f(G_SCALE * first_y, S, 2 * M),
        "grid_spec": f(grid_spec, 48, 2 * SPEC), "grid_l": f(H_SCALE * gl, 3, 256), "grid_r": f(gr, 3, S),
        "eye": f(Q_SCALE * eye, 128, 128), "pick": f(H_SCALE * pick, S, 256), "sign": f(sign, 128, 1),
    }
    for name, a, shape in (("inv_y", U_SCALE * inv_y, (128, 256)), ("fwd_y", F_SCALE * fwd_y, (128, 192))):
        hi = a.reshape(shape).astype(np.float16)
        lo = (a.reshape(shape) - hi.astype(np.float64)).astype(np.float16)
        out[name + "_h"], out[name + "_l"] = hi, lo
    return out

T_SCALE, U_SCALE, F_SCALE, Q_SCALE = 4.0, 8.0, 8.0, 16.0
R_SCALE = T_SCALE * U_SCALE
G_SCALE = R_SCALE * F_SCALE
H_SCALE = R_SCALE * Q_SCALE
CREDIT = 8


def wait_apart(eng, sem, value, stood):
    eng.wait_ge(sem, value)
    eng.sem_inc(stood, 1)


def fno(nc, d, out):
    f32, f16 = mybir.dt.float32, mybir.dt.float16
    ALU, ACT = mybir.AluOpType, mybir.ActivationFunctionType
    ctx = ExitStack()
    with ctx:
        sb = lambda n, s, t=f32: ctx.enter_context(nc.sbuf_tensor(n, s, t))
        sem = lambda n: ctx.enter_context(nc.semaphore(n))
        bank = [ctx.enter_context(nc.psum_tensor(f"bank{i}", [128, 512], f32)) for i in range(8)]
        Yd = nc.dram_tensor("y_spectrum", (4, M, C, NB, M * BQ), f32, kind="Internal").ap()
        Sd = nc.dram_tensor("r_spectrum", (4, M, C, NB, M * BQ), f32, kind="Internal").ap()
        Yd48 = Yd.rearrange("q x o b n -> (q x) o b n")
        Sd48 = Sd.rearrange("q x o b n -> (q x) o b n")

        inv_x, fwd_x = sb("inv_x_sb", [96, 2, 128]), sb("fwd_x_sb", [128, 2, 96])
        inv_y = [sb(f"inv_y{i}", [128, 2, 128], f16) for i in "hl"]
        fwd_y = [sb(f"fwd_y{i}", [128, 2, 96], f16) for i in "hl"]
        eye, sign = sb("eye_sb", [128, 128]), sb("sign_sb", [128, 1])
        q1a, bias_s, bias_1 = sb("q1a_sb", [33, 128]), sb("bias_s_sb", [32, 5]), sb("bias_1_sb", [32, 4])
        bias_s64, bias_1_64 = sb("bias_s64", [32, 4]), sb("bias_1_64", [32, 4])
        Sp = sb("S_spec", [128, M, NB, M, BQ])
        Wm = sb("W_modes", [128, M, M, 64])
        acc = sb("head_acc", [128, NC_, 2, COLS])
        w_in, w_1 = sb("w_in", [128, 128]), sb("w_1", [128, 128])
        w2e = sb("w2_exp", [32, OG, 128])
        q_tmp = sb("q_tmp", [128, 4, 128])
        q_st = [sb(f"q_st{i}", [128, OG, 128], f16) for i in "hl"]
        sd = sb("sd_ring", [128, 3, SPEC])
        ym = sb("ym_ring", [128, 2, M // 2, B])
        y1 = sb("y1_ring", [128, 2, NB, M, BQ])
        yin = sb("yin", [96, 2, 16, M, BQ])
        t1 = [sb(f"t1{i}", [128, 2, COLS], f16) for i in "hl"]
        r = [sb(f"r{i}", [128, 2, 2, COLS], f16) for i in "hl"]
        gs = sb("gs", [128, 2, BQ, 2, 48])
        ss = sb("ss", [96, 2, 16, M, BQ])
        tok = sb("tok", [128, 32, 64])
        q2s, q2b, q2c = sb("q2s_sb", [128, 1]), sb("q2b_sb", [128, 1]), sb("q2c", [128, Y32])
        xT = Wm[0:64].rearrange("p x k o -> p (x k o)")[:, 0:4096]
        pro = lambda a, b, p=128: Wm[0:p].rearrange("p x k o -> p (x k o)")[:, a:b]
        g0 = pro(4096, 4864).rearrange("p (t r k) -> p t r k", t=32, r=2)
        pick, kb = pro(4864, 5120, 64), pro(5120, 5376, 64)
        grid_l, gl, grid_r = pro(5376, 5632, 3), pro(5632, 5888, 3), pro(5888, 5952, 3)
        pexp, p12, first_y, g2 = pro(5952, 6016, 33), pro(6016, 6019, 33), pro(6080, 6104, 64), pro(6144, 6272)

        ld = sem("constants_loaded")
        zero = sem("zeroed")
        pre = sem("first_spectrum_stored")
        p_pe, p_ev = sem("prologue_product"), sem("prologue_evacuated")
        wl, w2l = sem("layer_weights_loaded"), sem("w2_expanded_loaded")
        wm_l, wm_s = sem("mode_weights_loaded"), sem("mode_weights_signed")
        sd_l = [sem(f"slab_loaded{i}") for i in range(3)]
        pe_w2, ev_w2 = sem("w2_mixed"), sem("S_updated")
        pe_mix, ev_a, ev_b = sem("modes_mixed"), sem("mixed_evac_g0"), sem("mixed_evac_g1")
        pe_w1, ev_w1, ev_db = sem("w1_mixed"), sem("y1_evacuated"), sem("y1_biased")
        bs_done = sem("S_biased")
        y_st = [sem(f"y_stored{i}") for i in range(2)]
        pe_qb, ev_qt, ev_qh, ev_ql = sem("q_built"), sem("q_masked"), sem("q_high"), sem("q_low")
        yin_l = [sem(f"yin_loaded{i}") for i in range(2)]
        pe_t, ev_th, ev_tl = sem("t1_product"), sem("t1_high"), sem("t1_low")
        pe_u, ev_rh, ev_rl = sem("u_product"), sem("r_high"), sem("r_low")
        pe_q, ev_q = sem("q_product"), sem("q_added")
        pe_g, ev_g = sem("g_product"), sem("g_evacuated")
        pe_s, ev_s = sem("s_product"), sem("s_evacuated")
        s_out = [sem(f"s_stored{i}") for i in range(2)]
        relu_d, pe_f, ev_f, q2_d = sem("head_relu"), sem("head_product"), sem("tok_ready"), sem("q2_ready")
        stood = sem("wait_stood_apart")
        LOADS = ["inv_x", "fwd_x", "inv_y_h", "inv_y_l", "fwd_y_h", "fwd_y_l", "eye", "sign", "q1a", "bias_s", "bias_1",
                 "xT", "pick", "grid_l", "grid_r", "pexp", "p12", "first_y", "q2s", "q2b"]
        dst = {"inv_x": inv_x[:].rearrange("p a b -> p (a b)"), "fwd_x": fwd_x[:].rearrange("p a b -> p (a b)"),
               "inv_y_h": inv_y[0][:].rearrange("p a b -> p (a b)"), "inv_y_l": inv_y[1][:].rearrange("p a b -> p (a b)"),
               "fwd_y_h": fwd_y[0][:].rearrange("p a b -> p (a b)"), "fwd_y_l": fwd_y[1][:].rearrange("p a b -> p (a b)"),
               "eye": eye[:], "sign": sign[:], "q1a": q1a[:], "bias_s": bias_s[:], "bias_1": bias_1[:], "xT": xT,
               "pick": pick, "grid_l": grid_l, "grid_r": grid_r, "pexp": pexp, "p12": p12, "first_y": first_y,
               "q2s": q2s[:], "q2b": q2b[:]}
        LOADED = 16 * len(LOADS)
        all_images = nc.Block()
        block = all_images.__enter__()

        @block.sync
        def _(sp):
            for n in LOADS:
                sp.dma_start(dst[n], d[n]).then_inc(ld, 16)
            sp.sem_inc(s_out[0], CREDIT)
            sp.sem_inc(s_out[1], CREDIT)
            sp.dma_start(Sd48[:, 1:3].rearrange("p o b n -> p o (b n)"), d["grid_spec"].rearrange("p (o n) -> p o n", o=2)).then_inc(pre, 16)
            sp.wait_ge(zero, 1)
            for o in range(3, C, M):
                n = min(M, C - o)
                sp.dma_start(Sd48[:, o:o + n].rearrange("p o b n -> p o (b n)"),
                             Sp[0:48, 0:n].rearrange("p x b k q -> p x (b k q)")).then_inc(pre, 16)
            sp.wait_ge(p_ev, 3)
            for bh in range(BH):
                sp.dma_start(Sd48[:, 0].rearrange("p (c h) n -> p c h n", h=BH)[:, :, bh],
                             ss[48 * bh:48 * bh + 48].rearrange("p a o k q -> p (a o) (k q)")[:, 0:NC_]).then_inc(pre, 16)
            sp.wait_ge(pre, 16 * 6)
            with sp.Fori(0, L) as l:
                sp.wait_ge(pe_s, l * UNITS + CREDIT)
                sp.dma_start(w_in[:], d["w_in"][bass.ds(l * 128, 128), :]).then_inc(wl, 16)
                sp.dma_start(w_1[:], d["w_1"][bass.ds(l * 128, 128), :]).then_inc(wl, 16)
                sp.dma_start(w2e[:].rearrange("p a b -> p (a b)"), d["w2e"][bass.ds(l * 32, 32), :]).then_inc(w2l, 16)
                sp.wait_ge(s_out[0], l * NC_ * 32 + CREDIT)
                sp.wait_ge(s_out[1], l * NC_ * 32 + CREDIT)

                def store_y(x):
                    wait_apart(sp, ev_w1, l * 2 * M + 2 * x + 2, stood)
                    if x == 0:
                        sp.wait_ge(ev_db, l + 1)
                    for q in range(4):
                        sp.dma_start(Yd[q, x].rearrange("o b n -> o (b n)"),
                                     y1[32 * q:32 * q + 32, x % 2].rearrange("p b k q -> p (b k q)")).then_inc(y_st[x % 2], 16)

                for x in range(M):
                    sp.wait_ge(pe_w2, l * 2 * M + 2 * (x - 3) + 2 + CREDIT)
                    for q in range(4):
                        sp.dma_start(sd[32 * q:32 * q + 32, x % 3], Sd[q, x].rearrange("o b n -> o (b n)")).then_inc(sd_l[x % 3], 16)
                    if x >= 4:
                        store_y(x - 4)
                for x in range(M - 4, M):
                    store_y(x)
                sp.wait_ge(y_st[0], (l + 1) * 6 * 64)
                sp.wait_ge(y_st[1], (l + 1) * 6 * 64)

                def load_yin(c, h):
                    for bh in range(BH):
                        sp.dma_start(yin[48 * bh:48 * bh + 48, h].rearrange("p o k q -> p o (k q)"),
                                     Yd48[:, 16 * h:16 * h + 16, bass.ds(c * BH + bh, 1), :].rearrange("p o b n -> p o (b n)")).then_inc(yin_l[h], 16)

                def store_s(c, h, k):
                    sp.wait_ge(ev_s, l * UNITS + k)
                    for bh in range(BH):
                        sp.dma_start(Sd48[:, 16 * h:16 * h + 16, bass.ds(c * BH + bh, 1), :].rearrange("p o b n -> p o (b n)"),
                                     ss[48 * bh:48 * bh + 48, h].rearrange("p o k q -> p o (k q)")).then_inc(s_out[h], 16)

                load_yin(0, 0)
                load_yin(0, 1)
                sp.wait_ge(pe_t, l * UNITS + 4)
                load_yin(1, 0)
                store_s(0, 0, 4 + CREDIT)
                sp.wait_ge(pe_t, l * UNITS + 8)
                load_yin(1, 1)
                with sp.Fori(1, NC_ - 1) as c:
                    store_s(c - 1, 1, c * OG + CREDIT)
                    sp.wait_ge(pe_t, l * UNITS + c * OG + 4)
                    load_yin(c + 1, 0)
                    store_s(c, 0, c * OG + 4 + CREDIT)
                    sp.wait_ge(pe_t, l * UNITS + c * OG + 8)
                    load_yin(c + 1, 1)
                c = NC_ - 1
                store_s(c - 1, 1, c * OG + CREDIT)
                store_s(c, 0, c * OG + 4 + CREDIT)
                store_s(c, 1, c * OG + 8 + CREDIT)
            for h in range(2):
                sp.wait_ge(s_out[h], L * NC_ * 32 + CREDIT)

        @block.gpsimd
        def _(pool):
            nc.gpsimd.memset(Sp[:], 0.0).then_inc(zero, 1)
            pool.wait_ge(p_ev, 24)
            with pool.Fori(0, L) as l:
                pool.wait_ge(pe_mix, l * 2 * M + CREDIT)
                for x in range(M):
                    pool.dma_start(Wm[:, x].rearrange("p k o -> p (k o)"),
                                   d["w_modes"][bass.ds(l * 128, 128), x * 768:(x + 1) * 768]).then_inc(wm_l, 16)
                wait_apart(pool, wm_l, l * 16 * M + 16 * M, stood)
                for x in range(M):
                    w = Wm[:, x, :, 0:32]
                    nc.gpsimd.tensor_scalar(w, w, sign[:, 0:1], None, ALU.mult).then_inc(wm_s, 1)

        @block.tensor
        def _(pe):
            mm = nc.tensor.matmul
            for s in (pe_w2, pe_mix, pe_w1, pe_s, pe_u, pe_g, pe_q):
                pe.sem_inc(s, CREDIT)
            pe.wait_ge(ld, LOADED)
            for t in range(32):
                last = mm(bank[t // 16][:, (t % 16) * 24:(t % 16) * 24 + 24], xT[:, t * 128:(t + 1) * 128], first_y, start=True, stop=True)
            last.then_inc(p_pe, 1)
            pe.wait_ge(p_ev, 2)
            for k in range(2):
                last = mm(bank[2][0:96, 0:384], fwd_x[:, k], g0[:, :, k, :], start=(k == 0), stop=(k == 1))
            last.then_inc(p_pe, 1)
            mm(bank[3][0:64, 0:128], pexp, q1a[:], start=True, stop=True).then_inc(p_pe, 1)
            pe.wait_ge(p_ev, 4)
            mm(bank[4][0:3, 0:128], p12, q1a[:], start=True, stop=True).then_inc(p_pe, 1)
            pe.wait_ge(p_ev, 6)
            for h in range(2):
                last = mm(bank[5][:, 64 * h:64 * h + 64], gl[:, 128 * h:128 * h + 128], grid_r, start=True, stop=True)
            last.then_inc(p_pe, 1)
            for i in range(2 * NC_):
                c, h = i // 2, i % 2
                pe.wait_ge(p_ev, 7 + i - 1 if i >= 2 else 7)
                mm(bank[(6, 2)[i % 2]][:], kb[:, 128 * h:128 * h + 128], xT[:, c * COLS:(c + 1) * COLS], start=True, stop=True).then_inc(p_pe, 1)

            with pe.Fori(0, L) as l:
                U = l * UNITS
                pe.wait_ge(w2l, l * 16 + 16)
                pe.wait_ge(p_ev, 23)
                pe.wait_ge(ev_q, l * NC_ + CREDIT)
                pe.wait_ge(ev_g, U + CREDIT)
                for og in range(OG):
                    mm(bank[4 + og // 4][:, (og % 4) * 128:(og % 4) * 128 + 128], w2e[:, og, :], q1a[0:32, :],
                       start=True, stop=True).then_inc(pe_qb, 1)
                pe.wait_ge(wl, l * 32 + 32)

                def mix_in(x, h):
                    if x == 0 and h == 0:
                        pe.wait_ge(ev_s, U + CREDIT)
                    if h == 0:
                        pe.wait_ge(sd_l[x % 3], l * 4 * 64 + (x // 3 + 1) * 64)
                    pe.wait_ge(ev_w2, l * 2 * M + 2 * x + h + CREDIT)
                    mm(bank[6][:, 0:HALF], w_in[:], sd[:, x % 3, h * HALF:(h + 1) * HALF], start=True, stop=True).then_inc(pe_w2, 1)

                def mix_modes(x, h):
                    if x == 0 and h == 0:
                        pe.wait_ge(wm_s, l * M + M)
                    pe.wait_ge(ev_w2, l * 2 * M + 2 * x + 2 + CREDIT)
                    pe.wait_ge(ev_a, l * 2 * M + 2 * x + h - 1 + CREDIT)
                    wait_apart(pe, ev_b, l * 2 * M + 2 * x + h - 1 + CREDIT, stood)
                    for k in range(M // 2):
                        for g in range(2):
                            ky = h * (M // 2) + k
                            last = mm(bank[2 * g + h][64 * g:64 * g + 64, 64 * k:64 * k + 64], Wm[64 * g:64 * g + 64, x, ky, :],
                                      Sp[64 * g:64 * g + 64, x, :, ky, :], start=True, stop=True)
                    last.then_inc(pe_mix, 1)

                def mix_out(x, h):
                    pe.wait_ge(ev_a, l * 2 * M + 2 * x + h + 1 + CREDIT)
                    pe.wait_ge(ev_b, l * 2 * M + 2 * x + h + 1 + CREDIT)
                    if x == 0:
                        pe.wait_ge(ev_qt, l * 2 + 2)
                    else:
                        pe.wait_ge(ev_w1, l * 2 * M + 2 * x + h - 1)
                    mm(bank[4 + h][:, 0:HALF], w_1[:], ym[:, h].rearrange("p k b -> p (k b)"), start=True, stop=True).then_inc(pe_w1, 1)

                for x in range(M + 1):
                    for h in range(2):
                        if x < M:
                            mix_in(x, h)
                        if x >= 1:
                            mix_modes(x - 1, h)
                            if h == 1:
                                mix_out(x - 1, 0)
                        if h == 0 and x >= 2:
                            mix_out(x - 2, 1)
                mix_out(M - 1, 1)

                def t1_product(u, og, c):
                    hh = og // 4
                    if og % 4 == 0:
                        pe.wait_ge(yin_l[hh], l * NC_ * 32 + c * 32 + 32)
                    pe.wait_ge(ev_th, u + CREDIT)
                    pe.wait_ge(ev_tl, u + CREDIT)
                    for bq in range(BQ):
                        for k in range(2):
                            last = mm(bank[7][64 * k:64 * k + 48, bq * 128:bq * 128 + 128],
                                      yin[:, hh, (og % 4) * 4:(og % 4) * 4 + 4, :, bq].rearrange("p o k -> p (o k)"), inv_x[:, k, :], start=True, stop=True)
                    last.then_inc(pe_t, 1)

                def u_product(u, og):
                    pe.wait_ge(ev_tl, u + 1 + CREDIT)
                    for h in range(2):
                        pe.wait_ge(ev_rl, 2 * u + h - 1 + CREDIT)
                        for i, (a, b) in enumerate(((0, 0), (1, 0), (0, 1))):
                            last = mm(bank[1 + h][:], inv_y[b][0:112, h], t1[a][0:112, og % 2], start=(i == 0), stop=(i == 2))
                        last.then_inc(pe_u, 1)

                def q_product(u, og, c):
                    pe.wait_ge(ev_rl, 2 * u + 2 + CREDIT)
                    if og == 0:
                        pe.wait_ge(ev_q, l * NC_ + c + CREDIT)
                    for h in range(2):
                        for i, (a, b) in enumerate(((0, 0), (1, 0), (0, 1))):
                            last = mm(bank[3 + h][:], q_st[b][:, og], r[a][:, og % 2, h], start=(og == 0 and i == 0), stop=(og == OG - 1 and i == 2))
                    if og == OG - 1:
                        last.then_inc(pe_q, 1)

                def g_product(u, og):
                    pe.wait_ge(ev_g, u + CREDIT)
                    for bq in range(BQ):
                        n = 0
                        for h in range(2):
                            for a, b in ((0, 0), (0, 1), (1, 0)):
                                last = mm(bank[5][:, bq * 96:bq * 96 + 96], r[a][:, og % 2, h, bq * 128:bq * 128 + 128], fwd_y[b][:, h], start=(n == 0), stop=(n == 5))
                                n += 1
                    last.then_inc(pe_g, 1)

                def s_product(u, og):
                    pe.wait_ge(ev_g, u + 1 + CREDIT)
                    pe.wait_ge(ev_s, u + CREDIT)
                    for k in range(2):
                        last = mm(bank[6][0:96, 0:192], fwd_x[:, k], gs[:, og % 2, :, k, :], start=(k == 0), stop=(k == 1))
                    last.then_inc(pe_s, 1)

                def slot(c, s, first):
                    u = U + c * OG + s
                    t1_product(u, s, c)
                    if not first or s >= 1:
                        u_product(u - 1, (s - 1) % OG)
                    if not first or s >= 2:
                        q_product(u - 2, (s - 2) % OG, c if s >= 2 else c - 1)
                        g_product(u - 2, (s - 2) % OG)
                    if not first or s >= 3:
                        s_product(u - 3, (s - 3) % OG)

                pe.wait_ge(ev_ql, l * 2 + 2)
                pe.wait_ge(ev_w1, l * 2 * M + 2 * M)
                for s in range(OG):
                    slot(0, s, True)
                with pe.Fori(1, NC_) as c:
                    for s in range(OG):
                        slot(c, s, False)
                e = U + UNITS
                u_product(e - 1, 7)
                q_product(e - 2, 6, NC_ - 1)
                g_product(e - 2, 6)
                s_product(e - 3, 5)
                q_product(e - 1, 7, NC_ - 1)
                g_product(e - 1, 7)
                s_product(e - 2, 6)
                s_product(e - 1, 7)
            pe.wait_ge(relu_d, NC_)
            pe.wait_ge(q2_d, 1)
            for t in range(32):
                c, bq = t // 4, t % 4
                for h in range(2):
                    last = mm(bank[t // 8][:, (t % 8) * 64 + 32 * h:(t % 8) * 64 + 32 * h + 32],
                              acc[:, c, h, bq * 128:bq * 128 + 128], q2c[:], start=True, stop=True)
                if t % 8 == 7:
                    last.then_inc(pe_f, 1)

        @block.scalar
        def _(act):
            cp = ACT.Copy
            for s in (ev_a, ev_th, ev_rh, ev_g):
                act.sem_inc(s, CREDIT)
            act.wait_ge(p_pe, 1)
            for i in range(2):
                nc.scalar.activation(g0.rearrange("p t r k -> p (t r k)")[:, i * 384:(i + 1) * 384], bank[i][:, 0:384], cp).then_inc(p_ev, 1)
            with act.Fori(0, L) as l:
                U = l * UNITS
                for i in range(2):
                    act.wait_ge(ev_qt, l * 2 + i + 1)
                    nc.scalar.activation(q_st[0][:, 4 * i:4 * i + 4].rearrange("p a b -> p (a b)"), q_tmp[:].rearrange("p a b -> p (a b)"), cp).then_inc(ev_qh, 1)
                for x in range(M):
                    for h in range(2):
                        act.wait_ge(pe_mix, l * 2 * M + 2 * x + h + 1 + CREDIT)
                        act.wait_ge(pe_w1, l * 2 * M + 2 * x + h - 1 + CREDIT)
                        nc.scalar.activation(ym[0:64, h].rearrange("p k b -> p (k b)"), bank[h][0:64, 0:HALF], cp).then_inc(ev_a, 1)

                def t1_high(u, og):
                    act.wait_ge(pe_t, u + 1)
                    act.wait_ge(pe_u, 2 * u - 2 + CREDIT)
                    nc.scalar.activation(t1[0][0:112, og % 2], bank[7][0:112, :], cp).then_inc(ev_th, 1)

                def r_high(u, og):
                    for h in range(2):
                        act.wait_ge(pe_u, 2 * u + h + 1 + CREDIT)
                        if h == 0:
                            act.wait_ge(pe_g, u - 1 + CREDIT)
                        nc.scalar.activation(r[0][:, og % 2, h], bank[1 + h][:], ACT.Relu).then_inc(ev_rh, 1)

                def g_copy(u, og):
                    act.wait_ge(pe_g, u + 1 + CREDIT)
                    act.wait_ge(pe_s, u - 1 + CREDIT)
                    nc.scalar.activation(gs[:, og % 2].rearrange("p a b c -> p (a b c)"), bank[5][:, 0:384], cp).then_inc(ev_g, 1)

                def slot(c, s, first):
                    u = U + c * OG + s
                    t1_high(u, s)
                    if not first or s >= 1:
                        r_high(u - 1, (s - 1) % OG)
                    if not first or s >= 2:
                        g_copy(u - 2, (s - 2) % OG)

                for s in range(OG):
                    slot(0, s, True)
                with act.Fori(1, NC_) as c:
                    for s in range(OG):
                        slot(c, s, False)
                e = U + UNITS
                r_high(e - 1, 7)
                g_copy(e - 2, 6)
                g_copy(e - 1, 7)
            for c in range(NC_):
                act.wait_ge(ev_q, (L - 1) * NC_ + c + 1 + CREDIT)
                v = acc[:, c].rearrange("p h n -> p (h n)")
                nc.scalar.activation(v, v, ACT.Relu).then_inc(relu_d, 1)

        @block.vector
        def _(dve):
            V = nc.vector
            for s in (ev_w2, ev_b, ev_tl, ev_rl, ev_q, ev_s):
                dve.sem_inc(s, CREDIT)
            V.memset(bank[7][:], 0.0)
            dve.wait_ge(p_pe, 2)
            V.tensor_copy(ss[:].rearrange("p a o k q -> p (a o) q k")[:, 0:NC_],
                          bank[2][0:96, 0:384].rearrange("p (c q k) -> p c q k", c=NC_, q=BQ)).then_inc(p_ev, 1)
            dve.wait_ge(ld, LOADED)
            V.tensor_scalar(bias_s64[:], bias_s[:, 0:4], float(S), None, ALU.mult)
            V.tensor_scalar(bias_1_64[:], bias_1[:], float(S), None, ALU.mult)
            V.tensor_scalar(q2c[:], eye[:, 0:Y32], q2s[:, 0:1], 1.0 / (H_SCALE * Q_SCALE), ALU.mult, ALU.mult).then_inc(q2_d, 1)
            V.tensor_reduce(p12[0:32, 2:3], bias_s[:, 0:5], mybir.AxisListType.X, ALU.add).then_inc(p_ev, 1)
            dve.wait_ge(p_pe, 3)
            V.tensor_tensor(kb.rearrange("p (h n) -> p h n", h=2), pick.rearrange("p (h n) -> p h n", h=2),
                            bank[3][0:64, None, 0:128].broadcast_to((64, 2, 128)), ALU.mult).then_inc(p_ev, 1)
            dve.wait_ge(p_pe, 4)
            V.tensor_tensor(gl.rearrange("p (h n) -> p h n", h=2), grid_l.rearrange("p (h n) -> p h n", h=2),
                            bank[4][0:3, None, 0:128].broadcast_to((3, 2, 128)), ALU.mult).then_inc(p_ev, 1)
            dve.wait_ge(p_pe, 5)
            V.tensor_copy(g2, bank[5][:, 0:128]).then_inc(p_ev, 1)
            dve.wait_ge(p_ev, 7)
            for i in range(2 * NC_):
                c, h = i // 2, i % 2
                dve.wait_ge(p_pe, 6 + i)
                V.tensor_tensor(acc[:, c, h].rearrange("p (b x) -> p b x", x=S), bank[(6, 2)[i % 2]][:].rearrange("p (b x) -> p b x", x=S),
                                g2[:, None, 64 * h:64 * h + 64].broadcast_to((128, 8, 64)), ALU.add).then_inc(p_ev, 1)
            dve.wait_ge(p_ev, 23)
            dve.sem_inc(p_ev, 1)
            dve.wait_ge(zero, 1)
            dve.wait_ge(pre, 16 * 6)

            with dve.Fori(0, L) as l:
                U = l * UNITS
                for i in range(2):
                    dve.wait_ge(pe_qb, l * 8 + 4 * i + 4)
                    if i == 1:
                        dve.wait_ge(ev_ql, l * 2 + 1)
                    else:
                        dve.wait_ge(ev_q, l * NC_ + CREDIT)
                    V.tensor_tensor(q_tmp[:], bank[4 + i][:].rearrange("p (a b) -> p a b", a=4), eye[:, None, :].broadcast_to((128, 4, 128)), ALU.mult).then_inc(ev_qt, 1)
                    dve.wait_ge(ev_qh, l * 2 + i + 1)
                    V.tensor_tensor(q_st[1][:, 4 * i:4 * i + 4], q_tmp[:], q_st[0][:, 4 * i:4 * i + 4], ALU.subtract).then_inc(ev_ql, 1)
                s0 = Sp[0:32, 0, :, 0, :]
                V.tensor_scalar(s0, s0, bias_s64[:, bass.ds(l, 1)], None, ALU.add).then_inc(bs_done, 1)
                dve.wait_ge(bs_done, l + 1)

                def s_update(x, h):
                    dve.wait_ge(pe_w2, l * 2 * M + 2 * x + h + 1 + CREDIT)
                    v = Sp[:, x, 8 * h:8 * h + 8].rearrange("p b k q -> p (b k q)")
                    V.tensor_tensor(v, v, bank[6][:, 0:HALF], ALU.add).then_inc(ev_w2, 1)

                def mixed(x, h):
                    dve.wait_ge(pe_mix, l * 2 * M + 2 * x + h + 1 + CREDIT)
                    dve.wait_ge(pe_w1, l * 2 * M + 2 * x + h - 1 + CREDIT)
                    V.tensor_copy(ym[64:128, h].rearrange("p k b -> p (k b)"), bank[2 + h][64:128, 0:HALF]).then_inc(ev_b, 1)

                def y1_copy(x, h):
                    dve.wait_ge(pe_w1, l * 2 * M + 2 * x + h + 1 + CREDIT)
                    if x >= 2:
                        dve.wait_ge(y_st[x % 2], l * 6 * 64 + (x // 2) * 64)
                    V.tensor_copy(y1[:, x % 2, :, 6 * h:6 * h + 6, :].rearrange("p b k q -> p k b q"),
                                  bank[4 + h][:, 0:HALF].rearrange("p (k b q) -> p k b q", b=NB, q=BQ)).then_inc(ev_w1, 1)
                    if x == 0 and h == 0:
                        dve.wait_ge(ev_w1, l * 2 * M + 1)
                        y0 = y1[0:32, 0, :, 0, :]
                        V.tensor_scalar(y0, y0, bias_1_64[:, bass.ds(l, 1)], None, ALU.add).then_inc(ev_db, 1)

                for x in range(M + 1):
                    for h in range(2):
                        if x < M:
                            s_update(x, h)
                        if x >= 1:
                            mixed(x - 1, h)
                            if h == 1:
                                y1_copy(x - 1, 0)
                        if h == 0 and x >= 2:
                            y1_copy(x - 2, 1)
                y1_copy(M - 1, 1)

                def t1_low(u, og):
                    dve.wait_ge(ev_th, u + 1 + CREDIT)
                    V.tensor_tensor(t1[1][0:112, og % 2], bank[7][0:112, :], t1[0][0:112, og % 2], ALU.subtract).then_inc(ev_tl, 1)

                def r_low(u, og):
                    for h in range(2):
                        dve.wait_ge(ev_rh, 2 * u + h + 1 + CREDIT)
                        V.scalar_tensor_tensor(r[1][:, og % 2, h], bank[1 + h][:], 0.0, r[0][:, og % 2, h], ALU.max, ALU.subtract).then_inc(ev_rl, 1)

                def s_copy(u, og, c_last):
                    dve.wait_ge(pe_s, u + 1 + CREDIT)
                    if og % 4 == 0:
                        dve.wait_ge(s_out[og // 4], l * NC_ * 32 + c_last * 32 + CREDIT)
                    V.tensor_copy(ss[:, og // 4, (og % 4) * 4:(og % 4) * 4 + 4].rearrange("p o k q -> p q (o k)"),
                                  bank[6][0:96, 0:192].rearrange("p (q n) -> p q n", q=BQ)).then_inc(ev_s, 1)

                def q_add(c):
                    dve.wait_ge(pe_q, l * NC_ + c + 1 + CREDIT)
                    for h in range(2):
                        v = acc[:, bass.ds(c, 1), h].rearrange("p c n -> p (c n)") if not isinstance(c, int) else acc[:, c, h]
                        last = V.tensor_tensor(v, v, bank[3 + h][:], ALU.add)
                    last.then_inc(ev_q, 1)

                def slot(c, s, first):
                    u = U + c * OG + s
                    t1_low(u, s)
                    if not first or s >= 1:
                        r_low(u - 1, (s - 1) % OG)
                    if not first and s == 1:
                        q_add(c - 1)
                    if not first or s >= 3:
                        s_copy(u - 3, (s - 3) % OG, c if s >= 3 else c - 1)

                for s in range(OG):
                    slot(0, s, True)
                with dve.Fori(1, NC_) as c:
                    for s in range(OG):
                        slot(c, s, False)
                e = U + UNITS
                r_low(e - 1, 7)
                s_copy(e - 3, 5, NC_ - 1)
                q_add(NC_ - 1)
                s_copy(e - 2, 6, NC_ - 1)
                s_copy(e - 1, 7, NC_ - 1)
            for i in range(4):
                dve.wait_ge(pe_f, i + 1)
                V.tensor_scalar(tok[:, 8 * i:8 * i + 8].rearrange("p a b -> p (a b)"), bank[i][:], q2b[:, 0:1], None, ALU.add).then_inc(ev_f, 1)

        all_images.__exit__(None, None, None)
        tokens(nc, d, tok, Sp[:].rearrange("p x b k q -> p (x b k q)"), Wm[:].rearrange("p x k o -> p (x k o)"), bank, sb, sem, out)


D, E, G_TILES, STEPS = 64, 8, 4, 4
GT = G_TILES * 128
GAMMA, THETA, EPS, MIN_SUM = 0.96875, 10000.0, 1e-5, 1e-12


def token_constants():
    n = np.arange(S)
    inv_freq = (1.0 / np.float32(THETA) ** (np.arange(0, D, 2, dtype=np.float32) / np.float32(D))).astype(np.float32)
    ang = (n.astype(np.float32)[:, None] * inv_freq[None, :]).astype(np.float64)
    cos = np.repeat(np.cos(ang).T, 2, axis=0)
    sin = np.repeat(np.sin(ang).T, 2, axis=0)
    sin[0::2] *= -1.0
    diff = n[None, :] - n[:, None]
    decay = np.where(diff >= 0, np.exp(np.maximum(diff, 0) * np.log(GAMMA)), 0.0)
    causal = np.where(diff >= 0, 1.0 / np.maximum(n, 1)[None, :], 0.0)
    two = lambda m: np.kron(np.eye(2), m)
    f = lambda a: np.ascontiguousarray(a, dtype=np.float32)
    return {"rope_cos": f(np.tile(cos, (2, 1))), "rope_sin": f(np.tile(sin, (2, 1))),
            "mask0": f(two(decay)), "mask1": f(two(causal)), "ident": f(np.eye(128)), "ones": f(np.ones((1, 128)))}


def tokens(nc, d, tok, area_a, area_b, bank, sb, sem, out):
    f32 = mybir.dt.float32
    ALU, ACT, X_AXIS = mybir.AluOpType, mybir.ActivationFunctionType, mybir.AxisListType.X
    used = [0]

    def view(area, n, p=128):
        a = area[0:p, used[0]:used[0] + n]
        used[0] += n
        return a

    x = view(area_a, 512).rearrange("p (j t d) -> p j t d", j=2, t=G_TILES)
    xt = view(area_a, 1024, 64).rearrange("p (j n) -> p j n", j=2)
    v = view(area_a, 1024).rearrange("p (j n) -> p j n", j=2)
    rope_a = view(area_a, 1024).rearrange("p (j n) -> p j n", j=2)
    rope_b = view(area_a, 1024).rearrange("p (j n) -> p j n", j=2)
    q_t = view(area_a, 1024, 64).rearrange("p (j n) -> p j n", j=2)
    k_t = view(area_a, 1024, 64).rearrange("p (j n) -> p j n", j=2)
    att = view(area_a, 1024).rearrange("p (j n) -> p j n", j=2)
    used[0] = 0
    xt_all = view(area_b, 4096, 64)
    hid = view(area_b, 1024).rearrange("p (j n) -> p j n", j=2)
    prod = view(area_b, 2048).rearrange("p (t n) -> p t n", t=G_TILES)
    stats = view(area_b, 48).rearrange("p (t n) -> p t n", t=8)
    mv = view(area_b, 16).rearrange("p (t n) -> p t n", t=8)
    rstd, var_eps = view(area_b, 8), view(area_b, 8)
    minus_half = sb("minus_half", [128, 8])
    gate = view(area_b, 256).rearrange("p (t e) -> p t e", e=E)
    prob = view(area_b, 256).rearrange("p (t e) -> p t e", e=E)
    top = view(area_b, 256).rearrange("p (t e) -> p t e", e=E)
    wgt = view(area_b, 256).rearrange("p (t e) -> p t e", e=E)
    row_max, row_sum = view(area_b, 32), view(area_b, 32)
    mixed = view(area_b, 256)
    names = {"rope_cos": [128, D], "rope_sin": [128, D], "mask0": [128, 128], "mask1": [128, 128], "ident": [128, 128], "ones": [1, 128],
             "wqk0": [64, 128], "wqks0": [64, 128], "wqk1": [64, 128], "wv0": [64, 128], "wv1_l": [64, 64], "wo1": [64, 128],
             "gate_w0": [64, E], "gate_w1": [64, E], "gate_b": [128, E],
             "w1_0": [64, E * 128], "b1_0": [128, E], "w2_0": [128, E * D], "b2_0": [1, E * D],
             "w1_1": [64, E * D], "b1_1": [128, E // 2], "w2_1": [128, E // 2 * 128], "b2_1": [1, E * D]}
    c = {n: sb("c_" + n, s) for n, s in names.items()}
    wvo = sb("wvo", [64, 128])
    loaded, wvo_p, wvo_d = sem("token_constants_loaded"), sem("wvo_product"), sem("wvo_ready")
    LOADED = 16 * len(names)
    s = {}
    for kind, n in (("attn", 2), ("gatein", 2), ("moe", 2)):
        for i in range(n):
            s[kind + str(i)] = {m: sem(f"{kind}{i}_{m}") for m in {
                "attn": ("bn", "var", "rstd", "x", "tr", "xt", "qk", "rope_t", "q", "k", "v", "vc", "sc", "att", "ctx", "h"),
                "gatein": ("bn", "var", "rstd", "x", "tr", "xt", "lg", "lgc", "all", "res"),
                "moe": ("hid", "gelu", "y", "free", "mix", "h", "hs")}[kind]}
    gate_s, shifted, exp_s = sem("gate_step"), sem("logits_shifted"), sem("logits_exponentiated")
    done, stood = sem("stored"), sem("token_wait_stood_apart")
    gate_count = [0]

    def group(a, i, j):
        return a[:, bass.ds(i * 8 + 4 * j, 4)]

    block = nc.Block()
    with block as block:
        @block.sync
        def _(sp):
            for n in names:
                sp.dma_start(c[n][:], d[n]).then_inc(loaded, 16)
            with sp.Fori(0, STEPS) as i:
                for j in range(2):
                    sp.wait_ge(s["moe1"]["h"], i * 2 + j + 1)
                    for bh in range(BH):
                        sp.dma_start(out[bass.ds(i * 4 + 2 * j + bh, 1)].rearrange("a q x y -> x (a q) y"),
                                     tok[64 * bh:64 * bh + 64, bass.ds(i * 8 + 4 * j, 4)]).then_inc(done, 16)
            sp.wait_ge(done, 16 * 4 * STEPS)

        @block.tensor
        def _(pe):
            mm = nc.tensor.matmul
            pe.wait_ge(loaded, LOADED)
            mm(bank[0][0:64, 0:128], c["wv1_l"][:], c["wo1"][:], start=True, stop=True).then_inc(wvo_p, 1)
            pe.wait_ge(wvo_d, 1)

            def transposes(m, i, j):
                wait_apart(pe, m["x"], i * 2 + j + 1, stood)
                for t in range(G_TILES):
                    last = nc.tensor.transpose(bank[j][0:64, t * 128:(t + 1) * 128], x[:, j, t], c["ident"][:])
                last.then_inc(m["tr"], 1)

            def attention(n):
                m = s[f"attn{n}"]
                with pe.Fori(0, STEPS) as i:
                    for j in range(2):
                        transposes(m, i, j)
                    for j in range(2):
                        pe.wait_ge(m["xt"], i * 2 + j + 1)
                        last = mm(bank[2 + j][:], c[f"wqk{n}"][:], xt[:, j], start=True, stop=True)
                        if n == 0:
                            last = mm(bank[4 + j][:], c["wqks0"][:], xt[:, j], start=True, stop=True)
                        last.then_inc(m["qk"], 1)
                        for t in range(G_TILES):
                            last = mm(bank[6 + j][:, t * 128:(t + 1) * 128], xt[:, j, t * 128:(t + 1) * 128], (c["wv0"] if n == 0 else wvo)[:], start=True, stop=True)
                        last.then_inc(m["v"], 1)
                    for j in range(2):
                        pe.wait_ge(m["q"], i * 2 + j + 1)
                        pe.wait_ge(m["k"], i * 2 + j + 1)
                        for t in range(G_TILES):
                            k = slice(t * 128, (t + 1) * 128)
                            last = mm(bank[j][:, k], k_t[:, j, k], q_t[:, j, k], start=True, stop=True)
                        last.then_inc(m["sc"], 1)
                    for j in range(2):
                        pe.wait_ge(m["att"], i * 2 + j + 1)
                        pe.wait_ge(m["vc"], i * 2 + j + 1)
                        for t in range(G_TILES):
                            k = slice(t * 128, (t + 1) * 128)
                            last = mm(bank[2 + j][:, k], att[:, j, k], v[:, j, k], start=True, stop=True)
                        last.then_inc(m["ctx"], 1)
                    pe.wait_ge(m["h"], i * 2 + 2)

            def gate_inputs(n):
                m = s[f"gatein{n}"]
                with pe.Fori(0, STEPS) as i:
                    for j in range(2):
                        transposes(m, i, j)
                    for j in range(2):
                        pe.wait_ge(m["xt"], i * 2 + j + 1)
                        for t in range(G_TILES):
                            last = mm(bank[2 + j][:, t * E:(t + 1) * E], xt[:, j, t * 128:(t + 1) * 128], c[f"gate_w{n}"][:], start=True, stop=True)
                        last.then_inc(m["lg"], 1)
                    pe.wait_ge(m["lgc"], i * 2 + 2)

            def experts(n):
                m = s[f"moe{n}"]
                H = E if n == 0 else E // 2
                W = D if n == 0 else 128

                def hidden(i, j, e):
                    k = j * H + e
                    wait_apart(pe, m["gelu"], i * 2 * H + k - 1 + CREDIT, stood)
                    mm(bank[k % 2][:], c[f"w1_{n}"][:, e * 128:(e + 1) * 128], xt_all[:, bass.ds(i * 1024 + 512 * j, 512)], start=True, stop=True).then_inc(m["hid"], 1)

                def outputs(i, j, e):
                    k = j * H + e
                    for t in range(G_TILES):
                        if e == 0:
                            pe.wait_ge(m["free"], i * 8 + j * 4 + t + 1 - 4 + CREDIT)
                            mm(bank[2 + t][:], c["ones"][:], c[f"b2_{n}"][:], start=True, stop=False)
                    pe.wait_ge(m["gelu"], i * 2 * H + k + 1 + CREDIT)
                    for t in range(G_TILES):
                        last = mm(bank[2 + t][:, e * W:(e + 1) * W], hid[:, k % 2, t * 128:(t + 1) * 128], c[f"w2_{n}"][:, e * W:(e + 1) * W], start=False, stop=(e == H - 1))
                    last.then_inc(m["y"], 1)

                pe.sem_inc(m["y"], CREDIT)
                pe.wait_ge(s[f"gatein{n}"]["all"], 2 * STEPS + CREDIT)
                with pe.Fori(0, STEPS) as i:
                    for j in range(2):
                        hidden(i, j, 0)
                        for e in range(H):
                            if e + 1 < H:
                                hidden(i, j, e + 1)
                            outputs(i, j, e)

            attention(0)
            gate_inputs(0)
            experts(0)
            attention(1)
            gate_inputs(1)
            experts(1)

        @block.scalar
        def _(act):
            cp = ACT.Copy

            def attention(n):
                m = s[f"attn{n}"]
                with act.Fori(0, STEPS) as i:
                    for j in range(2):
                        act.wait_ge(m["tr"], i * 2 + j + 1 + CREDIT)
                        nc.scalar.activation(xt[:, j], bank[j][0:64, :], cp).then_inc(m["xt"], 1)
                    for j in range(2):
                        act.wait_ge(m["v"], i * 2 + j + 1)
                        nc.scalar.activation(v[:, j], bank[6 + j][:], cp).then_inc(m["vc"], 1)

            def gate_inputs(n):
                m = s[f"gatein{n}"]
                with act.Fori(0, STEPS) as i:
                    for j in range(2):
                        act.wait_ge(m["tr"], i * 2 + j + 1 + CREDIT)
                        act.wait_ge(m["all"], i * 2 + j - 1 + CREDIT)
                        nc.scalar.activation(xt[:, j], bank[j][0:64, :], cp).then_inc(m["xt"], 1)

            def experts(n):
                m = s[f"moe{n}"]
                H = E if n == 0 else E // 2
                act.sem_inc(m["gelu"], CREDIT)
                act.wait_ge(shifted, n + 1)
                p2 = prob.rearrange("p t e -> p (t e)")
                nc.scalar.activation(p2, p2, ACT.Exp).then_inc(exp_s, 1)
                with act.Fori(0, STEPS) as i:
                    for j in range(2):
                        for e in range(H):
                            k = j * H + e
                            act.wait_ge(m["hid"], i * 2 * H + k + 1)
                            act.wait_ge(m["y"], i * 2 * H + k - 1 + CREDIT)
                            nc.scalar.activation(hid[:, k % 2], bank[k % 2][:], ACT.Gelu, bias=c[f"b1_{n}"][:, e:e + 1]).then_inc(m["gelu"], 1)

            act.wait_ge(loaded, LOADED)
            attention(0)
            gate_inputs(0)
            experts(0)
            attention(1)
            gate_inputs(1)
            experts(1)

        @block.gpsimd
        def _(pool):
            def deviations(m, i):
                pool.wait_ge(m["var"], i + 1)
                nc.gpsimd.tensor_tensor(rstd, var_eps, minus_half[:], ALU.pow).then_inc(m["rstd"], 1)

            def rope(n):
                m = s[f"attn{n}"]
                with pool.Fori(0, STEPS) as i:
                    deviations(m, i)
                    for j in range(2 if n == 0 else 0):
                        pool.wait_ge(m["rope_t"], i * 2 + j + 1)
                        nc.gpsimd.tensor_tensor(q_t[:, j], rope_a[0:64, j], rope_b[0:64, j], ALU.add).then_inc(m["q"], 1)

            def keep_xt(n):
                m = s[f"gatein{n}"]
                pool.sem_inc(m["all"], CREDIT)
                with pool.Fori(0, STEPS) as i:
                    deviations(m, i)
                    for j in range(2):
                        pool.wait_ge(m["xt"], i * 2 + j + 1)
                        nc.gpsimd.tensor_copy(xt_all[:, bass.ds(i * 1024 + 512 * j, 512)], xt[:, j]).then_inc(m["all"], 1)

            rope(0)
            keep_xt(0)
            rope(1)
            keep_xt(1)

        @block.vector
        def _(dve):
            V = nc.vector

            def layernorm(m, i):
                for t in range(2 * G_TILES):
                    V.bn_stats(stats[:, t], tok[:, bass.ds(i * 8 + t, 1)].rearrange("p a d -> p (a d)")).then_inc(m["bn"], 1)
                wait_apart(dve, m["bn"], i * 16 + 8, stood)
                for t in range(2 * G_TILES):
                    V.bn_aggr(mv[:, t], stats[:, t]).then_inc(m["bn"], 1)
                dve.wait_ge(m["bn"], i * 16 + 16)
                V.tensor_scalar(var_eps, mv[:, :, 1], EPS, None, ALU.add).then_inc(m["var"], 1)
                dve.wait_ge(m["rstd"], i + 1)
                for j in range(2):
                    dve.wait_ge(m["tr"], i * 2 + j - 1 + CREDIT)
                    for t in range(G_TILES):
                        k = j * G_TILES + t
                        last = V.tensor_scalar(x[:, j, t], tok[:, bass.ds(i * 8 + k, 1)].rearrange("p a d -> p (a d)"),
                                               mv[:, k, 0:1], rstd[:, k:k + 1], ALU.subtract, ALU.mult)
                    last.then_inc(m["x"], 1)

            def attention(n):
                m = s[f"attn{n}"]
                dve.sem_inc(m["tr"], CREDIT)
                with dve.Fori(0, STEPS) as i:
                    layernorm(m, i)
                    for j in range(2):
                        dve.wait_ge(m["qk"], i * 2 + j + 1)
                        if n == 0:
                            for dst, b, table in ((rope_a, 2, "rope_cos"), (rope_b, 4, "rope_sin")):
                                last = V.tensor_tensor(dst[:, j].rearrange("p (b x) -> p b x", x=S), bank[b + j][:].rearrange("p (b x) -> p b x", x=S),
                                                       c[table][:, None, :].broadcast_to((128, 8, S)), ALU.mult)
                            last.then_inc(m["rope_t"], 1)
                            dve.wait_ge(m["rope_t"], i * 2 + j + 1)
                            V.tensor_tensor(k_t[:, j], rope_a[64:128, j], rope_b[64:128, j], ALU.add).then_inc(m["k"], 1)
                        else:
                            V.tensor_copy(q_t[:, j], bank[2 + j][0:64, :]).then_inc(m["q"], 1)
                            V.tensor_copy(k_t[:, j], bank[2 + j][64:128, :]).then_inc(m["k"], 1)
                    for j in range(2):
                        dve.wait_ge(m["sc"], i * 2 + j + 1)
                        sc = bank[j][:].rearrange("p (t n) -> p t n", t=G_TILES)
                        mask = c[f"mask{n}"][:, None, :].broadcast_to((128, G_TILES, 128))
                        o = att[:, j].rearrange("p (t n) -> p t n", t=G_TILES)
                        if n == 0:
                            V.tensor_tensor(o, sc, mask, ALU.mult).then_inc(m["att"], 1)
                        else:
                            V.scalar_tensor_tensor(o, sc, 0.0, mask, ALU.max, ALU.mult).then_inc(m["att"], 1)
                    for j in range(2):
                        dve.wait_ge(m["ctx"], i * 2 + j + 1)
                        h = group(tok, i, j)
                        V.tensor_tensor(h, h, bank[2 + j][:].rearrange("p (t n) -> p t n", t=G_TILES)[:, :, 0:D], ALU.add).then_inc(m["h"], 1)

            def gate_inputs(n):
                m = s[f"gatein{n}"]
                dve.sem_inc(m["tr"], CREDIT)
                with dve.Fori(0, STEPS) as i:
                    layernorm(m, i)
                    for j in range(2):
                        if n == 1:
                            h = group(tok, i, j)
                            dve.wait_ge(m["x"], i * 2 + j + 1)
                            V.tensor_tensor(h, h, x[:, j], ALU.add).then_inc(m["res"], 1)
                    for j in range(2):
                        dve.wait_ge(m["lg"], i * 2 + j + 1)
                        lg = bank[2 + j][:, 0:32].rearrange("p (t e) -> p t e", e=E)
                        if n == 0:
                            V.tensor_tensor(group(gate, i, j), lg, c["gate_b"][:, None, :].broadcast_to((128, G_TILES, E)), ALU.add).then_inc(m["lgc"], 1)
                        else:
                            V.tensor_copy(group(gate, i, j), lg).then_inc(m["lgc"], 1)

            def top_two(n):
                wide = lambda a: a[:, :, None].broadcast_to((128, 32, E))

                def step(ins):
                    gate_count[0] += 1
                    ins.then_inc(gate_s, 1)
                    dve.wait_ge(gate_s, gate_count[0])

                step(V.tensor_reduce(row_max, gate, X_AXIS, ALU.max))
                V.tensor_tensor(prob, gate, wide(row_max), ALU.subtract).then_inc(shifted, 1)
                dve.wait_ge(exp_s, n + 1)
                step(V.tensor_reduce(row_sum, prob, X_AXIS, ALU.add))
                step(V.reciprocal(row_sum, row_sum))
                step(V.tensor_tensor(prob, prob, wide(row_sum), ALU.mult))
                for t in range(32):
                    last = V.max(top[:, t], prob[:, t])
                step(last)
                step(V.tensor_tensor(wgt, prob, top[:, :, 1:2].broadcast_to((128, 32, E)), ALU.is_ge))
                step(V.tensor_tensor(wgt, wgt, prob, ALU.mult))
                if n == 1:
                    step(V.tensor_tensor(row_sum, top[:, :, 0], top[:, :, 1], ALU.add))
                    step(V.tensor_scalar(row_sum, row_sum, MIN_SUM, None, ALU.max))
                    step(V.reciprocal(row_sum, row_sum))
                    step(V.tensor_tensor(wgt, wgt, wide(row_sum), ALU.mult))

            def experts(n):
                m = s[f"moe{n}"]
                H = E if n == 0 else E // 2
                dve.sem_inc(m["free"], CREDIT)
                with dve.Fori(0, STEPS) as i:
                    for j in range(2):
                        dve.wait_ge(m["y"], i * 2 * H + (j + 1) * H + CREDIT)
                        for t in range(G_TILES):
                            w = wgt[:, bass.ds(i * 8 + 4 * j + t, 1)].rearrange("p a e -> p (a e)")
                            V.tensor_tensor(prod[:, t].rearrange("p (e d) -> p e d", e=E), bank[2 + t][:].rearrange("p (e d) -> p e d", e=E),
                                            w[:, :, None].broadcast_to((128, E, D)), ALU.mult).then_inc(m["free"], 1)
                        dve.wait_ge(m["free"], i * 8 + 4 * j + 4 + CREDIT)
                        V.tensor_reduce(mixed.rearrange("p (t d) -> p t d", t=G_TILES), prod.rearrange("p t (e d) -> p t d e", e=E), X_AXIS, ALU.add).then_inc(m["mix"], 1)
                        dve.wait_ge(m["mix"], i * 2 + j + 1)
                        h = group(tok, i, j)
                        V.tensor_tensor(h, h, mixed.rearrange("p (t d) -> p t d", t=G_TILES), ALU.add).then_inc(m["h"], 1)

            V.memset(minus_half[:], -0.5)
            dve.wait_ge(loaded, LOADED)
            dve.wait_ge(wvo_p, 1)
            V.tensor_copy(wvo[:], bank[0][0:64, 0:128]).then_inc(wvo_d, 1)
            attention(0)
            dve.wait_ge(s["attn0"]["h"], 2 * STEPS)
            gate_inputs(0)
            dve.wait_ge(s["gatein0"]["lgc"], 2 * STEPS)
            top_two(0)
            experts(0)
            dve.wait_ge(s["moe0"]["h"], 2 * STEPS)
            attention(1)
            dve.wait_ge(s["attn1"]["h"], 2 * STEPS)
            gate_inputs(1)
            dve.wait_ge(s["gatein1"]["lgc"], 2 * STEPS)
            dve.wait_ge(s["gatein1"]["res"], 2 * STEPS)
            top_two(1)
            experts(1)


def token_layout(inp):
    f = lambda a: np.ascontiguousarray(a, dtype=np.float32)
    g = lambda n: inp[n]
    swap = np.arange(D).reshape(-1, 2)[:, ::-1].ravel()
    o = {}
    o["wqk0"] = f(np.concatenate([g("L0_attn_W_Q"), g("L0_attn_W_K")], 1))
    o["wqks0"] = f(np.concatenate([g("L0_attn_W_Q")[:, swap], g("L0_attn_W_K")[:, swap]], 1))
    o["wqk1"] = f(np.concatenate([g("L1_attn_Wq").T, g("L1_attn_Wk").T], 1))
    o["wv0"] = f(np.tile(g("L0_attn_W_V"), (1, 2)))
    o["wv1_l"] = f(g("L1_attn_Wv"))
    o["wo1"] = f(np.tile(g("L1_attn_Wo").T, (1, 2)))
    o["gate_w0"], o["gate_w1"] = f(g("L0_ffn_gate_w")), f(g("L1_ffn_router_w").T)
    o["gate_b"] = f(np.broadcast_to(g("L0_ffn_gate_b")[None], (128, E)))
    o["w1_0"] = f(g("L0_ffn_W1").transpose(1, 0, 2).reshape(D, E * 128))
    o["b1_0"] = f(g("L0_ffn_b1").T)
    o["w2_0"] = f(g("L0_ffn_W2").transpose(1, 0, 2).reshape(128, E * D))
    o["b2_0"] = f(g("L0_ffn_b2").reshape(1, E * D))
    o["w1_1"] = f(g("L1_ffn_w1").transpose(1, 0, 2).reshape(D, E * D))
    o["b1_1"] = f(g("L1_ffn_b1").reshape(E // 2, 128).T)
    w2 = np.zeros((E // 2, 2, D, 2, D), np.float32)
    for k in range(2):
        w2[:, k, :, k] = g("L1_ffn_w2").reshape(E // 2, 2, D, D)[:, k]
    o["w2_1"] = f(w2.transpose(1, 2, 0, 3, 4).reshape(128, E // 2 * 128))
    o["b2_1"] = f(g("L1_ffn_b2").reshape(1, E * D))
    return o | token_constants()


def host_layout(x, inp):
    f = lambda a: np.ascontiguousarray(a)
    p_w, p_b, fw = inp["L0_tok_p_w"], inp["L0_tok_p_b"], inp["L0_tok_fw"]
    w1, b1, w2, b2 = inp["L0_tok_w1_w"], inp["L0_tok_w1_b"], inp["L0_tok_w2_w"], inp["L0_tok_w2_b"]
    q1, q1b, q2, q2b = inp["L0_tok_q1_w"], inp["L0_tok_q1_b"], inp["L0_tok_q2_w"], inp["L0_tok_q2_b"]
    o = {}
    o["xT"] = f(x[..., 0].reshape(NC_, BH, BQ, S, S).transpose(4, 0, 2, 1, 3).reshape(S, NC_ * COLS))
    w_in, w_1 = np.zeros((L, 4, C, 4, C), np.float32), np.zeros((L, 4, C, 4, C), np.float32)
    for q in range(4):
        w_in[0, q, :3, q] = p_w.T
        w_in[1:, q, :, q] = w2[:L - 1].transpose(0, 2, 1)
        w_1[:, q, :, q] = w1.transpose(0, 2, 1)
    o["w_in"], o["w_1"] = w_in.reshape(L * 128, 128), w_1.reshape(L * 128, 128)
    o["bias_s"] = f(np.concatenate([p_b[None], b2]).T)
    o["bias_1"] = f(b1.T)
    w = fw.transpose(0, 1, 2, 4, 5, 6, 3)
    o["w_modes"] = f(np.stack([w, w[..., ::-1, :]], 2).reshape(L * 128, M * M * 64))
    o["w2e"] = f(np.repeat(w2.reshape(L * C, C), Y32, axis=1))
    q1a = np.concatenate([q1.T, q1b[None]])
    o["q1a"] = f(np.repeat(q1a, Y32, axis=1))
    pexp = np.zeros((33, 64), np.float32)
    pexp[:32] = p_w[:, 0:1]
    p12 = np.zeros((33, 3), np.float32)
    p12[:32, :2] = p_w[:, 1:3]
    p12[32, 2] = 1.0
    o["pexp"], o["p12"] = pexp, p12
    o["q2s"] = f(np.repeat(q2[0], Y32)[:, None])
    o["q2b"] = f(np.broadcast_to(q2b.reshape(1, 1), (128, 1)))
    return o | dft_constants() | token_layout(inp)


def kernel(**inputs):
    import concourse.bacc as bacc
    from concourse.bass_utils import run_bass_kernel_spmd as run
    inp = {k: np.asarray(v) for k, v in inputs.items()}
    arrays = host_layout(inp["x"], inp)
    nc = bacc.Bacc("TRN2", target_bir_lowering=False, num_devices=1)
    d = {n: nc.dram_tensor("in_" + n, a.shape, mybir.dt.from_np(a.dtype), kind="ExternalInput").ap() for n, a in arrays.items()}
    out = nc.dram_tensor("out", (B // BQ, BQ, S, S), mybir.dt.float32, kind="ExternalOutput").ap()
    fno(nc, d, out)
    r = run(nc, [{"in_" + n: a for n, a in arrays.items()}], core_ids=[0])
    return np.asarray(r.results[0]["out"]).reshape(B, S, S)
```

```python
import concourse.bass as bass
from concourse import mybir
from contextlib import ExitStack
import numpy as np

B, S, C, L, M, MID = 64, 64, 32, 4, 12, 4
KX = 2 * M
NC_, BH, BQ = 8, 2, 4
CH = BH * BQ
NB = B // BQ
OG = 8
O4, Y32 = 4, 32
COLS = BQ * BH * S
SPEC = B * M
HALF = SPEC // 2
UNITS = NC_ * OG


def dft_constants():
    n = np.arange(S)
    kx = np.concatenate([np.arange(M), np.arange(S - M, S)])
    ky = np.arange(M)
    rt = np.sqrt(S)
    wx = 2 * np.pi * np.outer(kx, n) / S
    wy = 2 * np.pi * np.outer(ky, n) / S
    cx, sx, cy, sy = np.cos(wx) / rt, np.sin(wx) / rt, np.cos(wy) / rt, np.sin(wy) / rt
    twice = np.where(ky == 0, 1.0, 2.0)[:, None]
    inv_x = np.zeros((BH, 2, 2, M, 2, BH, S))
    fwd_x = np.zeros((BH, S, 2, BH, 2, 2, M))
    for b in range(BH):
        for g in range(2):
            c, s = cx[g * M:(g + 1) * M], sx[g * M:(g + 1) * M]
            inv_x[b, g, 0, :, 0, b], inv_x[b, g, 1, :, 0, b] = c, -s
            inv_x[b, g, 0, :, 1, b], inv_x[b, g, 1, :, 1, b] = s, c
            fwd_x[b, :, 0, b, g, 0], fwd_x[b, :, 1, b, g, 0] = c.T, s.T
            fwd_x[b, :, 0, b, g, 1], fwd_x[b, :, 1, b, g, 1] = -s.T, c.T
    inv_y = np.zeros((128, 2, O4, Y32))
    fwd_y = np.zeros((O4, Y32, 2, 2, O4, M))
    for o in range(O4):
        for h in range(2):
            y = slice(h * Y32, (h + 1) * Y32)
            inv_y[o * M:(o + 1) * M, h, o] = (twice * cy)[:, y]
            inv_y[64 + o * M:64 + (o + 1) * M, h, o] = -(twice * sy)[:, y]
            fwd_y[o, :, h, 0, o] = cy[:, y].T
            fwd_y[o, :, h, 1, o] = -sy[:, y].T
    first_y = np.concatenate([cy.T, -sy.T], 1)
    line = np.linspace(0.0, 1.0, S)
    grids = []
    for image in (np.broadcast_to(line[:, None], (S, S)), np.broadcast_to(line[None, :], (S, S))):
        f = (cx - 1j * sx) @ image @ (cy - 1j * sy).T
        f = f.reshape(2, M, M)
        grids.append(np.stack([f.real, f.imag], 1).reshape(4 * M, M))
    grid_spec = np.broadcast_to(np.stack(grids, 1)[:, :, None, :, None], (4 * M, 2, NB, M, BQ)).reshape(4 * M, 2, SPEC)
    gl = np.ones((3, 2, MID, Y32))
    gl[1] = line.reshape(2, 1, Y32)
    gr = np.ones((3, S))
    gr[0] = line
    eye = np.zeros((O4, Y32, MID, Y32))
    eye[:, np.arange(Y32), :, np.arange(Y32)] = 1.0
    pick = np.zeros((S, 2, MID, Y32))
    for h in range(2):
        for y in range(Y32):
            pick[h * Y32 + y, h, :, y] = 1.0
    sign = np.ones((128, 1))
    for g in range(2):
        sign[64 * g + 32:64 * g + 64] = -1.0
    f = lambda a, *s: np.ascontiguousarray(a.reshape(*s), dtype=np.float32)
    out = {
        "inv_x": f(T_SCALE * inv_x, 96, 2 * BH * S), "fwd_x": f(fwd_x / G_SCALE, 128, 2 * 96), "first_y": f(G_SCALE * np.kron(np.eye(2), first_y), 2 * S, 2 * 2 * M),
        "grid_spec": f(grid_spec, 48, 2 * SPEC), "grid_l": f(H_SCALE * gl, 3, 256), "grid_r": f(gr, 3, S),
        "eye": f(Q_SCALE * eye, 128, 128), "pick": f(H_SCALE * np.kron(np.eye(2), pick.reshape(S, 256)), 2 * S, 2 * 256), "sign": f(sign, 128, 1),
    }
    for name, a, shape in (("inv_y", U_SCALE * inv_y, (128, 256)), ("fwd_y", F_SCALE * fwd_y, (128, 192))):
        hi = a.reshape(shape).astype(np.float16)
        lo = (a.reshape(shape) - hi.astype(np.float64)).astype(np.float16)
        out[name + "_h"], out[name + "_l"] = hi, lo
    return out

T_SCALE, U_SCALE, F_SCALE, Q_SCALE = 4.0, 8.0, 8.0, 16.0
R_SCALE = T_SCALE * U_SCALE
G_SCALE = R_SCALE * F_SCALE
H_SCALE = R_SCALE * Q_SCALE
CREDIT = 8


def wait_apart(eng, sem, value, stood):
    eng.wait_ge(sem, value)
    eng.sem_inc(stood, 1)


def fno(nc, d, out):
    f32, f16 = mybir.dt.float32, mybir.dt.float16
    ALU, ACT = mybir.AluOpType, mybir.ActivationFunctionType
    ctx = ExitStack()
    with ctx:
        sb = lambda n, s, t=f32: ctx.enter_context(nc.sbuf_tensor(n, s, t))
        sem = lambda n: ctx.enter_context(nc.semaphore(n))
        bank = [ctx.enter_context(nc.psum_tensor(f"bank{i}", [128, 512], f32)) for i in range(8)]
        Yd = nc.dram_tensor("y_spectrum", (4, M, C, NB, M * BQ), f32, kind="Internal").ap()
        Sd = nc.dram_tensor("r_spectrum", (4, M, C, NB, M * BQ), f32, kind="Internal").ap()
        Yd48 = Yd.rearrange("q x o b n -> (q x) o b n")
        Sd48 = Sd.rearrange("q x o b n -> (q x) o b n")

        inv_x, fwd_x = sb("inv_x_sb", [96, 2, 128]), sb("fwd_x_sb", [128, 2, 96])
        inv_y = [sb(f"inv_y{i}", [128, 2, 128], f16) for i in "hl"]
        fwd_y = [sb(f"fwd_y{i}", [128, 2, 96], f16) for i in "hl"]
        eye, sign = sb("eye_sb", [128, 128]), sb("sign_sb", [128, 1])
        q1a, bias_s, bias_1 = sb("q1a_sb", [33, 128]), sb("bias_s_sb", [32, 5]), sb("bias_1_sb", [32, 4])
        bias_s64, bias_1_64 = sb("bias_s64", [32, 4]), sb("bias_1_64", [32, 4])
        Sp = sb("S_spec", [128, M, NB, M, BQ])
        Wm = sb("W_modes", [128, M, M, 64])
        acc = sb("head_acc", [128, NC_, 2, COLS])
        w_in, w_1 = sb("w_in", [128, 128]), sb("w_1", [128, 128])
        w2e = sb("w2_exp", [32, OG, 128])
        q_tmp = sb("q_tmp", [128, 4, 128])
        q_st = [sb(f"q_st{i}", [128, OG, 128], f16) for i in "hl"]
        sd = sb("sd_ring", [128, 3, SPEC])
        ym = sb("ym_ring", [128, 2, M // 2, B])
        y1 = sb("y1_ring", [128, 2, NB, M, BQ])
        yin = sb("yin", [96, 2, 16, M, BQ])
        t1 = [sb(f"t1{i}", [128, 2, COLS], f16) for i in "hl"]
        r = [sb(f"r{i}", [128, 2, 2, COLS], f16) for i in "hl"]
        gs = sb("gs", [128, 2, BQ, 2, 48])
        ss = sb("ss", [96, 2, 16, M, BQ])
        tok = sb("tok", [128, 32, 64])
        q2s, q2b, q2c = sb("q2s_sb", [128, 1]), sb("q2b_sb", [128, 1]), sb("q2c", [128, Y32])
        ident = sb("ident", [128, 128])
        head = sd[:].rearrange("p a n -> p (a n)")[:, 0:NC_ // 2 * COLS].rearrange("p (i n) -> p i n", n=COLS)
        xT = tok[:].rearrange("p a b -> p (a b)")
        g0 = ym[:].rearrange("p h k b -> p (h k b)").rearrange("p (t r k) -> p t r k", t=32, r=2)
        y1_flat, yin_flat, gs_flat = (t[:].rearrange(f"p {n} -> p ({n})") for t, n in ((y1, "a b k q"), (yin, "a o k q"), (gs, "a q r k")))
        pick, kb = y1_flat[:, 0:512], y1_flat[:, 512:1024]
        grid_l, gl = yin_flat[0:3, 0:256], yin_flat[0:3, 256:512]
        pexp, p12, first_y = gs_flat[0:33, 0:128], gs_flat[0:33, 128:131], gs_flat[:, 136:184]
        grid_r, g2 = gs_flat[0:3, 192:256], gs_flat[:, 256:384]

        b = token_buffers(sb, Sp[:].rearrange("p x b k q -> p (x b k q)"), Wm[:].rearrange("p x k o -> p (x k o)"),
                          acc[:].rearrange("p c h n -> p (c h n)"))
        b_l, b_split = sem("token_constants_loaded"), sem("token_weights_split")
        wvo_p, wvo_h = sem("wvo_product"), sem("wvo_high")
        ld, ld_x = sem("constants_loaded"), sem("image_loaded")
        zero = sem("zeroed")
        pre = sem("first_spectrum_stored")
        p_pe, p_ev = sem("prologue_product"), sem("prologue_evacuated")
        wl, w2l = sem("layer_weights_loaded"), sem("w2_expanded_loaded")
        wm_l, wm_s = [sem(f"mode_weights_loaded{i}") for i in range(M)], sem("mode_weights_signed")
        sd_l = [sem(f"slab_loaded{i}") for i in range(3)]
        pe_w2, ev_w2 = sem("w2_mixed"), sem("S_updated")
        pe_mix, ev_a, ev_b = sem("modes_mixed"), sem("mixed_evac_g0"), sem("mixed_evac_g1")
        pe_w1, ev_w1, ev_db = sem("w1_mixed"), sem("y1_evacuated"), sem("y1_biased")
        bs_done = sem("S_biased")
        y_st = [sem(f"y_stored{i}") for i in range(2)]
        pe_qb, ev_qt, ev_qh, ev_ql = sem("q_built"), sem("q_masked"), sem("q_high"), sem("q_low")
        yin_l = [sem(f"yin_loaded{i}") for i in range(2)]
        pe_t, ev_th, ev_tl = sem("t1_product"), sem("t1_high"), sem("t1_low")
        pe_u, ev_rh, ev_rl = sem("u_product"), sem("r_high"), sem("r_low")
        pe_q, ev_q = sem("q_product"), sem("q_added")
        pe_g, ev_g = sem("g_product"), sem("g_evacuated")
        pe_s, ev_s = sem("s_product"), sem("s_evacuated")
        s_out = [sem(f"s_stored{i}") for i in range(2)]
        relu_d, pe_f, ev_f, q2_d = sem("head_relu"), sem("head_product"), sem("tok_ready"), sem("q2_ready")
        stood = sem("wait_stood_apart")
        LOADS_X = ["xT", "first_y", "fwd_x"]
        LOADS = ["inv_x", "inv_y_h", "inv_y_l", "fwd_y_h", "fwd_y_l", "eye", "sign", "q1a", "bias_s", "bias_1",
                 "pick", "grid_l", "grid_r", "pexp", "p12", "q2s", "q2b", "ident"]
        dst = {"inv_x": inv_x[:].rearrange("p a b -> p (a b)"), "fwd_x": fwd_x[:].rearrange("p a b -> p (a b)"),
               "inv_y_h": inv_y[0][:].rearrange("p a b -> p (a b)"), "inv_y_l": inv_y[1][:].rearrange("p a b -> p (a b)"),
               "fwd_y_h": fwd_y[0][:].rearrange("p a b -> p (a b)"), "fwd_y_l": fwd_y[1][:].rearrange("p a b -> p (a b)"),
               "eye": eye[:], "sign": sign[:], "q1a": q1a[:], "bias_s": bias_s[:], "bias_1": bias_1[:], "xT": xT,
               "pick": pick, "grid_l": grid_l, "grid_r": grid_r, "pexp": pexp, "p12": p12, "first_y": first_y,
               "q2s": q2s[:], "q2b": q2b[:], "ident": ident[:]}
        LOADED = 16 * len(LOADS)
        all_images = nc.Block()
        block = all_images.__enter__()

        @block.sync
        def _(sp):
            for n in LOADS_X:
                sp.dma_start(dst[n], d[n]).then_inc(ld_x, 16)
            sp.dma_start(Sd48[:, 1:3].rearrange("p o b n -> p o (b n)"), d["grid_spec"].rearrange("p (o n) -> p o n", o=2)).then_inc(pre, 16)
            for n in LOADS:
                sp.dma_start(dst[n], d[n]).then_inc(ld, 16)

            def load_weights(l):
                sp.dma_start(w_in[:], d["w_in"][bass.ds(l * 128, 128), :]).then_inc(wl, 16)
                sp.dma_start(w_1[:], d["w_1"][bass.ds(l * 128, 128), :]).then_inc(wl, 16)
                sp.dma_start(w2e[:].rearrange("p a b -> p (a b)"), d["w2e"][bass.ds(l * 32, 32), :]).then_inc(w2l, 16)

            load_weights(0)
            sp.sem_inc(s_out[0], CREDIT)
            sp.sem_inc(s_out[1], CREDIT)
            sp.wait_ge(p_ev, 3)
            for bh in range(BH):
                sp.dma_start(Sd48[:, 0].rearrange("p (c h) n -> p c h n", h=BH)[:, :, bh],
                             ss[48 * bh:48 * bh + 48].rearrange("p a o k q -> p (a o) (k q)")[:, 0:NC_]).then_inc(pre, 16)
            sp.wait_ge(pre, 16 * 3)
            sp.wait_ge(zero, 1)

            def layer(l, channels):
                if not isinstance(l, int):
                    sp.wait_ge(s_out[0], l * NC_ * 32 + CREDIT)
                    sp.wait_ge(s_out[1], l * NC_ * 32 + CREDIT)

                def store_y(x):
                    wait_apart(sp, ev_w1, l * 2 * M + 2 * x + 2, stood)
                    if x == 0:
                        sp.wait_ge(ev_db, l + 1)
                    for q in range(4):
                        sp.dma_start(Yd[q, x].rearrange("o b n -> o (b n)"),
                                     y1[32 * q:32 * q + 32, x % 2].rearrange("p b k q -> p (b k q)")).then_inc(y_st[x % 2], 16)

                for x in range(M):
                    if not isinstance(l, int) or x >= 3:
                        sp.wait_ge(pe_w2, l * 2 * M + 2 * (x - 3) + 2 + CREDIT)
                    for q in range(4):
                        sp.dma_start(sd[32 * q:32 * q + channels, x % 3], Sd[q, x, 0:channels].rearrange("o b n -> o (b n)")).then_inc(sd_l[x % 3], 16)
                    if x >= 4:
                        store_y(x - 4)
                for x in range(M - 4, M):
                    store_y(x)
                sp.wait_ge(y_st[0], (l + 1) * 6 * 64)
                sp.wait_ge(y_st[1], (l + 1) * 6 * 64)

                def load_yin(c, h):
                    for bh in range(BH):
                        sp.dma_start(yin[48 * bh:48 * bh + 48, h].rearrange("p o k q -> p o (k q)"),
                                     Yd48[:, 16 * h:16 * h + 16, bass.ds(c * BH + bh, 1), :].rearrange("p o b n -> p o (b n)")).then_inc(yin_l[h], 16)

                def store_s(c, h, k):
                    sp.wait_ge(ev_s, l * UNITS + k)
                    for bh in range(BH):
                        sp.dma_start(Sd48[:, 16 * h:16 * h + 16, bass.ds(c * BH + bh, 1), :].rearrange("p o b n -> p o (b n)"),
                                     ss[48 * bh:48 * bh + 48, h].rearrange("p o k q -> p o (k q)")).then_inc(s_out[h], 16)

                load_yin(0, 0)
                load_yin(0, 1)
                load_weights(l + 1)
                sp.wait_ge(pe_t, l * UNITS + 4)
                load_yin(1, 0)
                store_s(0, 0, 4 + CREDIT)
                sp.wait_ge(pe_t, l * UNITS + 8)
                load_yin(1, 1)
                with sp.Fori(1, NC_ - 1) as c:
                    store_s(c - 1, 1, c * OG + CREDIT)
                    sp.wait_ge(pe_t, l * UNITS + c * OG + 4)
                    load_yin(c + 1, 0)
                    store_s(c, 0, c * OG + 4 + CREDIT)
                    sp.wait_ge(pe_t, l * UNITS + c * OG + 8)
                    load_yin(c + 1, 1)
                c = NC_ - 1
                store_s(c - 1, 1, c * OG + CREDIT)
                store_s(c, 0, c * OG + 4 + CREDIT)
                store_s(c, 1, c * OG + 8 + CREDIT)

            layer(0, 3)
            with sp.Fori(1, L) as l:
                layer(l, C)
            for h in range(2):
                sp.wait_ge(s_out[h], L * NC_ * 32 + CREDIT)

        @block.gpsimd
        def _(pool):
            def load_modes(l):
                for x in range(M):
                    pool.dma_start(Wm[:, x].rearrange("p k o -> p (k o)"),
                                   d["w_modes"][bass.ds(l * 128, 128), x * 768:(x + 1) * 768]).then_inc(wm_l[x], 16)

            def sign_modes(l):
                for x in range(M):
                    wait_apart(pool, wm_l[x], l * 16 + 16, stood)
                    w = Wm[:, x, :, 0:32]
                    nc.gpsimd.tensor_scalar(w, w, sign[:, 0:1], None, ALU.mult).then_inc(wm_s, 1)

            nc.gpsimd.memset(sd[:], 0.0).then_inc(zero, 1)
            nc.gpsimd.memset(Sp[:], 0.0).then_inc(zero, 1)
            load_modes(0)
            pool.wait_ge(ld, LOADED)
            with pool.Fori(0, L - 1) as l:
                sign_modes(l)
                pool.wait_ge(pe_mix, (l + 1) * 2 * M + CREDIT)
                pool.wait_ge(pe_t, l * UNITS + OG)
                load_modes(l + 1)
            sign_modes(L - 1)
            pool.wait_ge(pe_mix, L * 2 * M + CREDIT)
            for tile, n in b.loads:
                pool.dma_start(tile, d[n]).then_inc(b_l, 16)
            P = nc.gpsimd
            count = [0]

            def step(ins):
                count[0] += 1
                ins.then_inc(b_split, 1)
                pool.wait_ge(b_split, count[0])

            step(P.memset(b.minus_half[:], -0.5))
            step(P.memset(b.ones[:], 1.0))
            step(P.memset(b.w64_l[64:128], 0.0))
            step(P.memset(b.wvo_l[64:128], 0.0))
            step(P.memset(b.b2hl[:].rearrange("p a n -> p (a n)"), 0.0))
            pool.wait_ge(b_l, 16 * len(b.loads))
            step(P.tensor_copy(b.w64_h[:], b.w64))
            step(P.tensor_tensor(b.w64_l[0:64], b.w64[0:64], b.w64_h[0:64], ALU.subtract))
            b2_h, b2_l = (b.b2hl[k:k + 1].rearrange("p a n -> p (a n)") for k in (0, 32))
            for high, low, whole in ((b.w2_h[0][:], b.w2_l[0][:], b.w2f[0]), (b.w2_h[1][:], b.w2_l[1][:], b.w2f[1]), (b2_h, b2_l, b.b2f)):
                step(P.tensor_copy(high, whole))
                step(P.tensor_tensor(low, whole, high, ALU.subtract))

        @block.tensor
        def _(pe):
            mm = nc.tensor.matmul
            for s in (pe_w2, pe_mix, pe_w1, pe_s, pe_u, pe_g, pe_q):
                pe.sem_inc(s, CREDIT)
            pe.wait_ge(ld_x, 16 * len(LOADS_X))
            for t in range(32):
                c, bq = t // 4, t % 4
                last = mm(bank[t // 16][:, (t % 16) * 24:(t % 16) * 24 + 24], xT[:, (c // 2) * COLS + bq * 128:(c // 2) * COLS + (bq + 1) * 128],
                          first_y[:, (c % 2) * 24:(c % 2) * 24 + 24], start=True, stop=True)
            last.then_inc(p_pe, 1)
            pe.wait_ge(p_ev, 2)
            for k in range(2):
                last = mm(bank[2][0:96, 0:384], fwd_x[:, k], g0[:, :, k, :], start=(k == 0), stop=(k == 1))
            last.then_inc(p_pe, 1)
            pe.wait_ge(ld, LOADED)
            mm(bank[3][:, 0:128], pexp, q1a[:], start=True, stop=True).then_inc(p_pe, 1)
            pe.wait_ge(p_ev, 4)
            mm(bank[4][0:3, 0:128], p12, q1a[:], start=True, stop=True).then_inc(p_pe, 1)
            pe.wait_ge(p_ev, 6)
            for h in range(2):
                last = mm(bank[5][:, 64 * h:64 * h + 64], gl[:, 128 * h:128 * h + 128], grid_r, start=True, stop=True)
            last.then_inc(p_pe, 1)
            for i in range(2 * NC_):
                c, h = i // 2, i % 2
                pe.wait_ge(p_ev, 7 + i - 1 if i >= 2 else 7)
                mm(bank[(6, 2)[i % 2]][:], kb[:, 256 * (c % 2) + 128 * h:256 * (c % 2) + 128 * h + 128], xT[:, (c // 2) * COLS:(c // 2 + 1) * COLS], start=True, stop=True).then_inc(p_pe, 1)

            with pe.Fori(0, L) as l:
                U = l * UNITS
                pe.wait_ge(w2l, l * 16 + 16)
                pe.wait_ge(p_ev, 23)
                pe.wait_ge(ev_q, l * NC_ + CREDIT)
                pe.wait_ge(ev_g, U + CREDIT)
                for og in range(OG):
                    mm(bank[4 + og // 4][:, (og % 4) * 128:(og % 4) * 128 + 128], w2e[:, og, :], q1a[0:32, :],
                       start=True, stop=True).then_inc(pe_qb, 1)
                pe.wait_ge(wl, l * 32 + 32)

                def mix_in(x, h):
                    if x == 0 and h == 0:
                        pe.wait_ge(ev_s, U + CREDIT)
                    if h == 0:
                        pe.wait_ge(sd_l[x % 3], l * 4 * 64 + (x // 3 + 1) * 64)
                    pe.wait_ge(ev_w2, l * 2 * M + 2 * x + h + CREDIT)
                    mm(bank[6][:, 0:HALF], w_in[:], sd[:, x % 3, h * HALF:(h + 1) * HALF], start=True, stop=True).then_inc(pe_w2, 1)

                def mix_modes(x, h):
                    if h == 0:
                        pe.wait_ge(wm_s, l * M + x + 1)
                    pe.wait_ge(ev_w2, l * 2 * M + 2 * x + 2 + CREDIT)
                    pe.wait_ge(ev_a, l * 2 * M + 2 * x + h - 1 + CREDIT)
                    wait_apart(pe, ev_b, l * 2 * M + 2 * x + h - 1 + CREDIT, stood)
                    for k in range(M // 2):
                        for g in range(2):
                            ky = h * (M // 2) + k
                            last = mm(bank[2 * g + h][64 * g:64 * g + 64, 64 * k:64 * k + 64], Wm[64 * g:64 * g + 64, x, ky, :],
                                      Sp[64 * g:64 * g + 64, x, :, ky, :], start=True, stop=True)
                    last.then_inc(pe_mix, 1)

                def mix_out(x, h):
                    pe.wait_ge(ev_a, l * 2 * M + 2 * x + h + 1 + CREDIT)
                    pe.wait_ge(ev_b, l * 2 * M + 2 * x + h + 1 + CREDIT)
                    if x == 0:
                        pe.wait_ge(ev_qt, l * 2 + 2)
                    else:
                        pe.wait_ge(ev_w1, l * 2 * M + 2 * x + h - 1)
                    mm(bank[4 + h][:, 0:HALF], w_1[:], ym[:, h].rearrange("p k b -> p (k b)"), start=True, stop=True).then_inc(pe_w1, 1)

                for x in range(M + 1):
                    for h in range(2):
                        if x < M:
                            mix_in(x, h)
                        if x >= 1:
                            mix_modes(x - 1, h)
                            if h == 1:
                                mix_out(x - 1, 0)
                        if h == 0 and x >= 2:
                            mix_out(x - 2, 1)
                mix_out(M - 1, 1)

                def t1_product(u, og, c):
                    hh = og // 4
                    if og % 4 == 0:
                        pe.wait_ge(yin_l[hh], l * NC_ * 32 + c * 32 + 32)
                    pe.wait_ge(ev_th, u + CREDIT)
                    pe.wait_ge(ev_tl, u + CREDIT)
                    for bq in range(BQ):
                        for k in range(2):
                            last = mm(bank[7][64 * k:64 * k + 48, bq * 128:bq * 128 + 128],
                                      yin[:, hh, (og % 4) * 4:(og % 4) * 4 + 4, :, bq].rearrange("p o k -> p (o k)"), inv_x[:, k, :], start=True, stop=True)
                    last.then_inc(pe_t, 1)

                def u_product(u, og):
                    pe.wait_ge(ev_tl, u + 1 + CREDIT)
                    for h in range(2):
                        pe.wait_ge(ev_rl, 2 * u + h - 1 + CREDIT)
                        for i, (a, b) in enumerate(((0, 0), (1, 0), (0, 1))):
                            last = mm(bank[1 + h][:], inv_y[b][0:112, h], t1[a][0:112, og % 2], start=(i == 0), stop=(i == 2))
                        last.then_inc(pe_u, 1)

                def q_product(u, og, c):
                    pe.wait_ge(ev_rl, 2 * u + 2 + CREDIT)
                    if og == 0:
                        pe.wait_ge(ev_q, l * NC_ + c + CREDIT)
                    for h in range(2):
                        for i, (a, b) in enumerate(((0, 0), (1, 0), (0, 1))):
                            last = mm(bank[3 + h][:], q_st[b][:, og], r[a][:, og % 2, h], start=(og == 0 and i == 0), stop=(og == OG - 1 and i == 2))
                    if og == OG - 1:
                        last.then_inc(pe_q, 1)

                def g_product(u, og):
                    pe.wait_ge(ev_g, u + CREDIT)
                    for bq in range(BQ):
                        n = 0
                        for h in range(2):
                            for a, b in ((0, 0), (0, 1), (1, 0)):
                                last = mm(bank[5][:, bq * 96:bq * 96 + 96], r[a][:, og % 2, h, bq * 128:bq * 128 + 128], fwd_y[b][:, h], start=(n == 0), stop=(n == 5))
                                n += 1
                    last.then_inc(pe_g, 1)

                def s_product(u, og):
                    pe.wait_ge(ev_g, u + 1 + CREDIT)
                    pe.wait_ge(ev_s, u + CREDIT)
                    for k in range(2):
                        last = mm(bank[6][0:96, 0:192], fwd_x[:, k], gs[:, og % 2, :, k, :], start=(k == 0), stop=(k == 1))
                    last.then_inc(pe_s, 1)

                def slot(c, s, first):
                    u = U + c * OG + s
                    t1_product(u, s, c)
                    if not first or s >= 1:
                        u_product(u - 1, (s - 1) % OG)
                    if not first or s >= 2:
                        q_product(u - 2, (s - 2) % OG, c if s >= 2 else c - 1)
                        g_product(u - 2, (s - 2) % OG)
                    if not first or s >= 3:
                        s_product(u - 3, (s - 3) % OG)

                pe.wait_ge(ev_ql, l * 2 + 2)
                pe.wait_ge(ev_w1, l * 2 * M + 2 * M)
                for s in range(OG):
                    slot(0, s, True)
                with pe.Fori(1, NC_) as c:
                    for s in range(OG):
                        slot(c, s, False)
                e = U + UNITS
                u_product(e - 1, 7)
                q_product(e - 2, 6, NC_ - 1)
                g_product(e - 2, 6)
                s_product(e - 3, 5)
                q_product(e - 1, 7, NC_ - 1)
                g_product(e - 1, 7)
                s_product(e - 2, 6)
                s_product(e - 1, 7)
            pe.wait_ge(b_l, 16 * len(b.loads))
            mm(bank[7][:, 0:D], b.c["wv1_l"][:], b.c["wo1"][:], start=True, stop=True).then_inc(wvo_p, 1)
            pe.wait_ge(q2_d, 1)
            for i in range(NC_ // 2):
                pe.wait_ge(relu_d, 2 * i + 2)
                for j in range(4):
                    last = mm(bank[i][32 * j:32 * j + 32, :], q2c[:], acc[:, 2 * i + j // 2, j % 2, :], start=True, stop=True)
                last.then_inc(pe_f, 1)
            for i in range(NC_ // 2):
                pe.wait_ge(ev_f, i + 1)
                if i == NC_ // 2 - 1:
                    pe.wait_ge(wvo_h, 2)
                for bq in range(BQ):
                    last = nc.tensor.transpose(bank[4 + i][:, 128 * bq:128 * bq + 128], head[:, i, 128 * bq:128 * bq + 128], ident[:])
                last.then_inc(pe_f, 1)

        @block.scalar
        def _(act):
            cp = ACT.Copy
            for s in (ev_a, ev_th, ev_rh, ev_g):
                act.sem_inc(s, CREDIT)
            act.wait_ge(p_pe, 1)
            for i in range(2):
                nc.scalar.activation(g0.rearrange("p t r k -> p (t r k)")[:, i * 384:(i + 1) * 384], bank[i][:, 0:384], cp).then_inc(p_ev, 1)
            with act.Fori(0, L) as l:
                U = l * UNITS
                for i in range(2):
                    act.wait_ge(ev_qt, l * 2 + i + 1)
                    nc.scalar.activation(q_st[0][:, 4 * i:4 * i + 4].rearrange("p a b -> p (a b)"), q_tmp[:].rearrange("p a b -> p (a b)"), cp).then_inc(ev_qh, 1)
                for x in range(M):
                    for h in range(2):
                        act.wait_ge(pe_mix, l * 2 * M + 2 * x + h + 1 + CREDIT)
                        act.wait_ge(pe_w1, l * 2 * M + 2 * x + h - 1 + CREDIT)
                        nc.scalar.activation(ym[0:64, h].rearrange("p k b -> p (k b)"), bank[h][0:64, 0:HALF], cp).then_inc(ev_a, 1)

                def t1_high(u, og):
                    act.wait_ge(pe_t, u + 1)
                    act.wait_ge(pe_u, 2 * u - 2 + CREDIT)
                    nc.scalar.activation(t1[0][0:112, og % 2], bank[7][0:112, :], cp).then_inc(ev_th, 1)

                def r_high(u, og):
                    for h in range(2):
                        act.wait_ge(pe_u, 2 * u + h + 1 + CREDIT)
                        if h == 0:
                            act.wait_ge(pe_g, u - 1 + CREDIT)
                        nc.scalar.activation(r[0][:, og % 2, h], bank[1 + h][:], ACT.Relu).then_inc(ev_rh, 1)

                def g_copy(u, og):
                    act.wait_ge(pe_g, u + 1 + CREDIT)
                    act.wait_ge(pe_s, u - 1 + CREDIT)
                    nc.scalar.activation(gs[:, og % 2].rearrange("p a b c -> p (a b c)"), bank[5][:, 0:384], cp).then_inc(ev_g, 1)

                def slot(c, s, first):
                    u = U + c * OG + s
                    t1_high(u, s)
                    if not first or s >= 1:
                        r_high(u - 1, (s - 1) % OG)
                    if not first or s >= 2:
                        g_copy(u - 2, (s - 2) % OG)

                for s in range(OG):
                    slot(0, s, True)
                with act.Fori(1, NC_) as c:
                    for s in range(OG):
                        slot(c, s, False)
                e = U + UNITS
                r_high(e - 1, 7)
                g_copy(e - 2, 6)
                g_copy(e - 1, 7)
            for c in range(NC_):
                act.wait_ge(ev_q, (L - 1) * NC_ + c + 1 + CREDIT)
                v = acc[:, c].rearrange("p h n -> p (h n)")
                nc.scalar.activation(v, v, ACT.Relu).then_inc(relu_d, 1)

        @block.vector
        def _(dve):
            V = nc.vector
            for s in (ev_w2, ev_b, ev_tl, ev_rl, ev_q, ev_s):
                dve.sem_inc(s, CREDIT)
            V.memset(bank[7][:], 0.0)
            dve.wait_ge(p_pe, 2)
            V.tensor_copy(ss[:].rearrange("p a o k q -> p (a o) q k")[:, 0:NC_],
                          bank[2][0:96, 0:384].rearrange("p (c q k) -> p c q k", c=NC_, q=BQ)).then_inc(p_ev, 1)
            dve.wait_ge(ld, LOADED)
            V.tensor_scalar(bias_s64[:], bias_s[:, 0:4], float(S), None, ALU.mult)
            V.tensor_scalar(bias_1_64[:], bias_1[:], float(S), None, ALU.mult)
            V.tensor_scalar(q2c[:], eye[:, 0:Y32], q2s[:, 0:1], 1.0 / (H_SCALE * Q_SCALE), ALU.mult, ALU.mult).then_inc(q2_d, 1)
            V.tensor_reduce(p12[0:32, 2:3], bias_s[:, 0:5], mybir.AxisListType.X, ALU.add).then_inc(p_ev, 1)
            dve.wait_ge(p_pe, 3)
            V.tensor_tensor(kb.rearrange("p (h n) -> p h n", h=4), pick.rearrange("p (h n) -> p h n", h=4),
                            bank[3][:, None, 0:128].broadcast_to((128, 4, 128)), ALU.mult).then_inc(p_ev, 1)
            dve.wait_ge(p_pe, 4)
            V.tensor_tensor(gl.rearrange("p (h n) -> p h n", h=2), grid_l.rearrange("p (h n) -> p h n", h=2),
                            bank[4][0:3, None, 0:128].broadcast_to((3, 2, 128)), ALU.mult).then_inc(p_ev, 1)
            dve.wait_ge(p_pe, 5)
            V.tensor_copy(g2, bank[5][:, 0:128]).then_inc(p_ev, 1)
            dve.wait_ge(p_ev, 7)
            for i in range(2 * NC_):
                c, h = i // 2, i % 2
                dve.wait_ge(p_pe, 6 + i)
                V.tensor_tensor(acc[:, c, h].rearrange("p (b x) -> p b x", x=S), bank[(6, 2)[i % 2]][:].rearrange("p (b x) -> p b x", x=S),
                                g2[:, None, 64 * h:64 * h + 64].broadcast_to((128, 8, 64)), ALU.add).then_inc(p_ev, 1)
            dve.wait_ge(p_ev, 23)
            dve.sem_inc(p_ev, 1)
            dve.wait_ge(zero, 2)

            with dve.Fori(0, L) as l:
                U = l * UNITS
                for i in range(2):
                    dve.wait_ge(pe_qb, l * 8 + 4 * i + 4)
                    if i == 1:
                        dve.wait_ge(ev_ql, l * 2 + 1)
                    else:
                        dve.wait_ge(ev_q, l * NC_ + CREDIT)
                    V.tensor_tensor(q_tmp[:], bank[4 + i][:].rearrange("p (a b) -> p a b", a=4), eye[:, None, :].broadcast_to((128, 4, 128)), ALU.mult).then_inc(ev_qt, 1)
                    dve.wait_ge(ev_qh, l * 2 + i + 1)
                    V.tensor_tensor(q_st[1][:, 4 * i:4 * i + 4], q_tmp[:], q_st[0][:, 4 * i:4 * i + 4], ALU.subtract).then_inc(ev_ql, 1)
                s0 = Sp[0:32, 0, :, 0, :]
                V.tensor_scalar(s0, s0, bias_s64[:, bass.ds(l, 1)], None, ALU.add).then_inc(bs_done, 1)
                dve.wait_ge(bs_done, l + 1)

                def s_update(x, h):
                    dve.wait_ge(pe_w2, l * 2 * M + 2 * x + h + 1 + CREDIT)
                    v = Sp[:, x, 8 * h:8 * h + 8].rearrange("p b k q -> p (b k q)")
                    V.tensor_tensor(v, v, bank[6][:, 0:HALF], ALU.add).then_inc(ev_w2, 1)

                def mixed(x, h):
                    dve.wait_ge(pe_mix, l * 2 * M + 2 * x + h + 1 + CREDIT)
                    dve.wait_ge(pe_w1, l * 2 * M + 2 * x + h - 1 + CREDIT)
                    V.tensor_copy(ym[64:128, h].rearrange("p k b -> p (k b)"), bank[2 + h][64:128, 0:HALF]).then_inc(ev_b, 1)

                def y1_copy(x, h):
                    dve.wait_ge(pe_w1, l * 2 * M + 2 * x + h + 1 + CREDIT)
                    if x >= 2:
                        dve.wait_ge(y_st[x % 2], l * 6 * 64 + (x // 2) * 64)
                    V.tensor_copy(y1[:, x % 2, :, 6 * h:6 * h + 6, :].rearrange("p b k q -> p k b q"),
                                  bank[4 + h][:, 0:HALF].rearrange("p (k b q) -> p k b q", b=NB, q=BQ)).then_inc(ev_w1, 1)
                    if x == 0 and h == 0:
                        dve.wait_ge(ev_w1, l * 2 * M + 1)
                        y0 = y1[0:32, 0, :, 0, :]
                        V.tensor_scalar(y0, y0, bias_1_64[:, bass.ds(l, 1)], None, ALU.add).then_inc(ev_db, 1)

                for x in range(M + 1):
                    for h in range(2):
                        if x < M:
                            s_update(x, h)
                        if x >= 1:
                            mixed(x - 1, h)
                            if h == 1:
                                y1_copy(x - 1, 0)
                        if h == 0 and x >= 2:
                            y1_copy(x - 2, 1)
                y1_copy(M - 1, 1)

                def t1_low(u, og):
                    dve.wait_ge(ev_th, u + 1 + CREDIT)
                    V.tensor_tensor(t1[1][0:112, og % 2], bank[7][0:112, :], t1[0][0:112, og % 2], ALU.subtract).then_inc(ev_tl, 1)

                def r_low(u, og):
                    for h in range(2):
                        dve.wait_ge(ev_rh, 2 * u + h + 1 + CREDIT)
                        V.scalar_tensor_tensor(r[1][:, og % 2, h], bank[1 + h][:], 0.0, r[0][:, og % 2, h], ALU.max, ALU.subtract).then_inc(ev_rl, 1)

                def s_copy(u, og, c_last):
                    dve.wait_ge(pe_s, u + 1 + CREDIT)
                    if og % 4 == 0:
                        dve.wait_ge(s_out[og // 4], l * NC_ * 32 + c_last * 32 + CREDIT)
                    V.tensor_copy(ss[:, og // 4, (og % 4) * 4:(og % 4) * 4 + 4].rearrange("p o k q -> p q (o k)"),
                                  bank[6][0:96, 0:192].rearrange("p (q n) -> p q n", q=BQ)).then_inc(ev_s, 1)

                def q_add(c):
                    dve.wait_ge(pe_q, l * NC_ + c + 1 + CREDIT)
                    for h in range(2):
                        v = acc[:, bass.ds(c, 1), h].rearrange("p c n -> p (c n)") if not isinstance(c, int) else acc[:, c, h]
                        last = V.tensor_tensor(v, v, bank[3 + h][:], ALU.add)
                    last.then_inc(ev_q, 1)

                def slot(c, s, first):
                    u = U + c * OG + s
                    t1_low(u, s)
                    if not first or s >= 1:
                        r_low(u - 1, (s - 1) % OG)
                    if not first and s == 1:
                        q_add(c - 1)
                    if not first or s >= 3:
                        s_copy(u - 3, (s - 3) % OG, c if s >= 3 else c - 1)

                for s in range(OG):
                    slot(0, s, True)
                with dve.Fori(1, NC_) as c:
                    for s in range(OG):
                        slot(c, s, False)
                e = U + UNITS
                r_low(e - 1, 7)
                s_copy(e - 3, 5, NC_ - 1)
                q_add(NC_ - 1)
                s_copy(e - 2, 6, NC_ - 1)
                s_copy(e - 1, 7, NC_ - 1)
            dve.wait_ge(wvo_p, 1)
            V.tensor_copy(b.wvo_h[:], bank[7][:, 0:D]).then_inc(wvo_h, 1)
            dve.wait_ge(wvo_h, 1)
            V.tensor_tensor(b.wvo_l[0:64], bank[7][0:64, 0:D], b.wvo_h[0:64], ALU.subtract).then_inc(wvo_h, 1)
            for i in range(NC_ // 2):
                dve.wait_ge(pe_f, i + 1)
                V.tensor_scalar(head[:, i], bank[i][:], q2b[:, 0:1], None, ALU.add).then_inc(ev_f, 1)
            for i in range(NC_ // 2):
                dve.wait_ge(pe_f, NC_ // 2 + i + 1)
                V.tensor_copy(tok[:, 8 * i:8 * i + 8].rearrange("p (c q) y -> p q c y", c=2),
                              bank[4 + i][:].rearrange("p (q c y) -> p q c y", q=BQ, c=2)).then_inc(ev_f, 1)

        all_images.__exit__(None, None, None)
        tokens(nc, d, tok, b, ident, bank, sem, out)


D, E, G_TILES, STEPS = 64, 8, 4, 4
GT = G_TILES * 128
T_BANKS, LG_BANKS = (0, 1, 4, 5), (2, 3, 6, 7)
HID = 4
GAMMA, THETA, EPS, MIN_SUM = 0.96875, 10000.0, 1e-5, 1e-12


def token_constants():
    n = np.arange(S)
    inv_freq = (1.0 / np.float32(THETA) ** (np.arange(0, D, 2, dtype=np.float32) / np.float32(D))).astype(np.float32)
    ang = (n.astype(np.float32)[:, None] * inv_freq[None, :]).astype(np.float64)
    cos = np.repeat(np.cos(ang).T, 2, axis=0)
    sin = np.repeat(np.sin(ang).T, 2, axis=0)
    sin[0::2] *= -1.0
    diff = n[None, :] - n[:, None]
    decay = np.where(diff >= 0, np.exp(np.maximum(diff, 0) * np.log(GAMMA)), 0.0)
    causal = np.where(diff >= 0, 1.0 / np.maximum(n, 1)[None, :], 0.0)
    side = lambda m: np.kron(np.eye(2), m)
    f = lambda a: np.ascontiguousarray(a, dtype=np.float32)
    return {"rope_cos": f(np.tile(cos, (2, 1))), "rope_sin": f(np.tile(sin, (2, 1))),
            "mask0": f(side(decay)), "mask1": f(side(causal)), "ident": f(np.eye(128))}


W64 = {"wqk0": 128, "wqks0": 128, "wv0": 64, "gate_w0": E, "w1_0": E * 128, "wqk1": 128, "gate_w1": E, "w1_1": E * D}
W64_AT = {n: sum(list(W64.values())[:k]) for k, n in enumerate(W64)}
W64_N = sum(W64.values())


class Buffers:
    pass


def token_buffers(sb, area_a, area_b, area_c):
    f32, f16 = mybir.dt.float32, mybir.dt.float16
    used = [0]

    def view(area, n, p=128):
        a = area[0:p, used[0]:used[0] + n]
        used[0] += n
        return a

    two = lambda a: a.rearrange("p (j n) -> p j n", j=2)
    b = Buffers()
    b.x = view(area_a, 1024).rearrange("p (j t d) -> p j t d", j=4, t=G_TILES)
    b.v = two(view(area_a, 1024))
    b.rope_a, b.rope_b = two(view(area_a, 1024)), two(view(area_a, 1024))
    b.q_t, b.k_t = two(view(area_a, 1024, 64)), two(view(area_a, 1024, 64))
    b.att = two(view(area_a, 1024))
    b.w64 = view(area_a, W64_N)
    used[0] = 0
    b.prod = view(area_b, 2048).rearrange("p (t n) -> p t n", t=G_TILES)
    b.stats = view(area_b, 48).rearrange("p (t n) -> p t n", t=8)
    b.mv = view(area_b, 16).rearrange("p (t n) -> p t n", t=8)
    b.mean, b.rstd, b.var_eps = view(area_b, 32), view(area_b, 32), view(area_b, 32)
    b.gate, b.prob, b.top, b.wgt = (view(area_b, 256).rearrange("p (t e) -> p t e", e=E) for _ in range(4))
    b.row_max, b.row_sum = view(area_b, 32), view(area_b, 32)
    b.xs = view(area_b, 2048).bitcast(f16)
    b.b2f = view(area_b, 1024, 1)
    b.w2f = [view(area_b, 512), view(area_b, 512)]
    used[0] = 0
    b.hid = view(area_c, HID * GT).rearrange("p (j n) -> p j n", j=HID)
    b.hid_h, b.hid_l = (view(area_c, HID * GT // 2).bitcast(f16).rearrange("p (j n) -> p j n", j=HID) for _ in "hl")
    b.minus_half = sb("minus_half", [128, 32])
    b.w64_h, b.w64_l = sb("w64_h", [128, W64_N], f16), sb("w64_l", [128, W64_N], f16)
    b.w2_h = [sb(f"w2_h{n}", [128, 512], f16) for n in range(2)]
    b.w2_l = [sb(f"w2_l{n}", [128, 512], f16) for n in range(2)]
    b.wvo_h, b.wvo_l = sb("wvo_h", [128, D], f16), sb("wvo_l", [128, D], f16)
    b.b2hl = sb("b2hl", [33, 2, E * D], f16)
    b.ones = sb("ones33", [33, 128], f16)
    names = {"rope_cos": [128, D], "rope_sin": [128, D], "mask0": [128, 128], "mask1": [128, 128],
             "wv1_l": [64, 128], "wo1": [64, D], "gate_b": [128, E], "b1_0": [128, E], "b1_1": [128, E // 2]}
    b.c = {n: sb("c_" + n, shape) for n, shape in names.items()}
    b.loads = [(b.c[n][:], n) for n in names] + [(b.w64, "w64"), (b.w2f[0], "w2_0"), (b.w2f[1], "w2_1"), (b.b2f, "b2")]
    return b


def tokens(nc, d, tok, b, ident, bank, sem, out):
    ALU, ACT, X_AXIS = mybir.AluOpType, mybir.ActivationFunctionType, mybir.AxisListType.X
    x, v, rope_a, rope_b, q_t, k_t, att = b.x, b.v, b.rope_a, b.rope_b, b.q_t, b.k_t, b.att
    prod, stats, mv, mean, rstd, var_eps = b.prod, b.stats, b.mv, b.mean, b.rstd, b.var_eps
    gate, prob, top, wgt, row_max, row_sum = b.gate, b.prob, b.top, b.wgt, b.row_max, b.row_sum
    xs, hid, hid_h, hid_l, minus_half, c = b.xs, b.hid, b.hid_h, b.hid_l, b.minus_half, b.c
    w64_h, w64_l, w2_h, w2_l, wvo_h, wvo_l, b2hl, ones = b.w64_h, b.w64_l, b.w2_h, b.w2_l, b.wvo_h, b.wvo_l, b.b2hl, b.ones
    hid_bank = [bank[k] for k in (0, 1, 6, 7)]
    s = {}
    for kind, n in (("attn", 2), ("gatein", 2), ("moe", 2)):
        for i in range(n):
            s[kind + str(i)] = {m: sem(f"{kind}{i}_{m}") for m in {
                "attn": ("bn", "dev", "var", "rstd", "x", "tr", "xh", "xl", "qk", "rope_t", "q", "k", "v", "vc", "sc", "att", "ctx", "h"),
                "gatein": ("bn", "dev", "var", "rstd", "x", "tr", "xh", "xl", "lg", "lgc", "res"),
                "moe": ("hid", "high", "low", "y", "free", "sum", "h")}[kind]}
    gate_s, shifted, exp_s = sem("gate_step"), sem("logits_shifted"), sem("logits_exponentiated")
    done, stood = sem("stored"), sem("token_wait_stood_apart")
    gate_count = [0]

    def group(a, i, j):
        return a[:, bass.ds(i * 8 + 4 * j, 4)]

    def w(n, half, a=0, b=None):
        at = W64_AT[n]
        return (w64_h, w64_l)[half][:, at + a:at + (W64[n] if b is None else b)]

    def steps(eng, first, body):
        first()
        with eng.Fori(0, STEPS - 1) as i:
            body(i, False)
        body(STEPS - 1, True)

    with nc.Block() as block:
        @block.sync
        def _(sp):
            with sp.Fori(0, STEPS) as i:
                for j in range(2):
                    wait_apart(sp, s["moe1"]["h"], i * 2 + j + 1 + CREDIT, stood)
                    for bh in range(BH):
                        sp.dma_start(out[bass.ds(i * 4 + 2 * j + bh, 1)].rearrange("a q x y -> x (a q) y"),
                                     tok[64 * bh:64 * bh + 64, bass.ds(i * 8 + 4 * j, 4)]).then_inc(done, 16)
            sp.wait_ge(done, 16 * 4 * STEPS)

        @block.tensor
        def _(pe):
            mm = nc.tensor.matmul

            def transposes(m, i):
                wait_apart(pe, m["x"], i + 1, stood)
                for j in range(2):
                    if not isinstance(i, int) or i > 0:
                        wait_apart(pe, m["xl"], i * 2 + j - 1, stood)
                    for t in range(G_TILES):
                        last = nc.tensor.transpose(bank[j][0:64, t * 128:(t + 1) * 128], x[:, j, t], ident[:])
                    last.then_inc(m["tr"], 1)

            def with_tokens(o, w_h, w_l, cols):
                mm(o, w_h, cols, start=True, stop=False)
                return mm(o, w_l, cols, start=False, stop=True)

            def attention(n):
                m = s[f"attn{n}"]

                def body(i, last_step):
                    for j in range(2):
                        cols = xs[:, bass.ds(i * 1024 + 512 * j, 512)]
                        pe.wait_ge(m["xl"], i * 2 + j + 1)
                        last = with_tokens(bank[2 + j][:], w(f"wqk{n}", 0), w(f"wqk{n}", 1), cols)
                        if n == 0:
                            last = with_tokens(bank[4 + j][:], w("wqks0", 0), w("wqks0", 1), cols)
                        last.then_inc(m["qk"], 1)
                        for t in range(G_TILES):
                            tile = xs[:, bass.ds(i * 1024 + 512 * j + 128 * t, 128)]
                            o = bank[6 + j][:, t * D:(t + 1) * D]
                            mm(o, tile, w("wv0", 0) if n == 0 else wvo_h[:], start=True, stop=False)
                            last = mm(o, tile, w("wv0", 1) if n == 0 else wvo_l[:], start=False, stop=True)
                        last.then_inc(m["v"], 1)
                    for j in range(2):
                        pe.wait_ge(m["q"], i * 2 + j + 1)
                        pe.wait_ge(m["k"], i * 2 + j + 1)
                        for t in range(G_TILES):
                            k = slice(t * 128, (t + 1) * 128)
                            last = mm(bank[4 + j][:, k], k_t[:, j, k], q_t[:, j, k], start=True, stop=True)
                        last.then_inc(m["sc"], 1)
                    if not last_step:
                        transposes(m, i + 1)
                    for j in range(2):
                        pe.wait_ge(m["att"], i * 2 + j + 1)
                        pe.wait_ge(m["vc"], i * 2 + j + 1)
                        for t in range(G_TILES):
                            k = slice(t * 128, (t + 1) * 128)
                            last = mm(bank[2 + j][:, k], att[:, j, k], v[:, j, k], start=True, stop=True)
                        last.then_inc(m["ctx"], 1)
                    pe.wait_ge(m["h"], i * 2 + 2)

                steps(pe, lambda: transposes(m, 0), body)

            def gate_inputs(n):
                m = s[f"gatein{n}"]
                with pe.Fori(0, STEPS // 2) as half:
                    for k in range(4):
                        if k % 2 == 0:
                            wait_apart(pe, m["x"], half * 2 + k // 2 + 1, stood)
                        for t in range(G_TILES):
                            last = nc.tensor.transpose(bank[T_BANKS[k]][0:64, t * 128:(t + 1) * 128], x[:, k, t], ident[:])
                        last.then_inc(m["tr"], 1)
                    for k in range(4):
                        pe.wait_ge(m["xl"], half * 4 + k + 1)
                        for t in range(G_TILES):
                            tile = xs[:, bass.ds(half * 4 * GT + GT * k + 128 * t, 128)]
                            o = bank[LG_BANKS[k]][:, t * E:(t + 1) * E]
                            mm(o, tile, w(f"gate_w{n}", 0), start=True, stop=False)
                            last = mm(o, tile, w(f"gate_w{n}", 1), start=False, stop=True)
                        last.then_inc(m["lg"], 1)
                    pe.wait_ge(m["lgc"], half * 4 + 4)

            def experts(n):
                m = s[f"moe{n}"]
                H = E if n == 0 else E // 2
                W = D if n == 0 else 128
                pe.sem_inc(m["y"], CREDIT)

                def hidden(i, k):
                    pe.wait_ge(m["high"], i * 2 * H + k - HID + 1 + CREDIT)
                    e = k % H
                    w_h, w_l = (w(f"w1_{n}", half, e * 128, (e + 1) * 128) for half in range(2))
                    with_tokens(hid_bank[k % HID][:], w_h, w_l, xs[:, bass.ds(i * 1024 + GT * (k // H), GT)]).then_inc(m["hid"], 1)

                def first():
                    for k in range(HID - 1):
                        hidden(0, k)

                def body(i, last_step):
                    for k in range(2 * H):
                        j, e = k // H, k % H
                        if k + HID - 1 < 2 * H:
                            hidden(i, k + HID - 1)
                        elif not last_step:
                            hidden(i + 1, k + HID - 1 - 2 * H)
                        pe.wait_ge(m["low"], i * 2 * H + k + 1)
                        for t in range(G_TILES):
                            if e == 0:
                                pe.wait_ge(m["free"], i * 8 + j * 4 + t + 1 - 4 + CREDIT)
                                mm(bank[2 + t][:], ones[:], b2hl[:, n], start=True, stop=False)
                            o = bank[2 + t][:, e * W:(e + 1) * W]
                            for a, b in ((hid_h, w2_h), (hid_h, w2_l), (hid_l, w2_h)):
                                last = mm(o, a[:, k % HID, t * 128:(t + 1) * 128], b[n][:, e * W:(e + 1) * W], start=False, stop=(e == H - 1 and a is hid_l))
                        last.then_inc(m["y"], 1)

                steps(pe, first, body)

            attention(0)
            gate_inputs(0)
            experts(0)
            attention(1)
            gate_inputs(1)
            experts(1)

        @block.scalar
        def _(act):
            cp = ACT.Copy

            def high(m, i, banks=(0, 1)):
                for j in range(2):
                    act.wait_ge(m["tr"], i * 2 + j + 1)
                    nc.scalar.activation(xs[0:64, bass.ds(i * 1024 + 512 * j, 512)], bank[banks[j]][0:64, :], cp).then_inc(m["xh"], 1)

            def attention(n):
                m = s[f"attn{n}"]

                def body(i, last_step):
                    for j in range(2):
                        act.wait_ge(m["v"], i * 2 + j + 1)
                        nc.scalar.activation(v[:, j].rearrange("p (t a d) -> p t a d", t=G_TILES, a=2),
                                             bank[6 + j][:, 0:256].rearrange("p (t d) -> p t d", t=G_TILES)[:, :, None, :].broadcast_to((128, G_TILES, 2, D)), cp).then_inc(m["vc"], 1)
                    if not last_step:
                        high(m, i + 1)

                steps(act, lambda: high(m, 0), body)

            def gate_inputs(n):
                m = s[f"gatein{n}"]
                with act.Fori(0, STEPS // 2) as half:
                    for k in range(2):
                        high(m, half * 2 + k, T_BANKS[2 * k:2 * k + 2])

            def experts(n):
                m = s[f"moe{n}"]
                H = E if n == 0 else E // 2
                act.sem_inc(m["high"], CREDIT)
                act.wait_ge(shifted, n + 1)
                p2 = prob.rearrange("p t e -> p (t e)")
                nc.scalar.activation(p2, p2, ACT.Exp).then_inc(exp_s, 1)
                with act.Fori(0, STEPS) as i:
                    for k in range(2 * H):
                        act.wait_ge(m["hid"], i * 2 * H + k + 1)
                        act.wait_ge(m["y"], i * 2 * H + k - HID + 1 + CREDIT)
                        bias = c[f"b1_{n}"][:, k % H:k % H + 1]
                        nc.scalar.activation(hid[:, k % HID], hid_bank[k % HID][:], ACT.Gelu, bias=bias)
                        nc.scalar.activation(hid_h[:, k % HID], hid_bank[k % HID][:], ACT.Gelu, bias=bias).then_inc(m["high"], 1)

            attention(0)
            gate_inputs(0)
            experts(0)
            attention(1)
            gate_inputs(1)
            experts(1)

        @block.gpsimd
        def _(pool):
            def deviations(m, i):
                pool.wait_ge(m["var"], i + 1)
                k = bass.ds(i * 8, 8)
                nc.gpsimd.tensor_tensor(rstd[:, k], var_eps[:, k], minus_half[:, 0:8], ALU.pow).then_inc(m["rstd"], 1)

            m = s["attn0"]
            for i in range(STEPS):
                deviations(m, i)
            with pool.Fori(0, STEPS) as i:
                for j in range(2):
                    pool.wait_ge(m["rope_t"], i * 2 + j + 1)
                    nc.gpsimd.tensor_tensor(q_t[:, j], rope_a[0:64, j], rope_b[0:64, j], ALU.add).then_inc(m["q"], 1)
                deviations(s["gatein0"], i)

            def combine(m, i, j):
                pool.wait_ge(m["free"], i * 8 + 4 * j + 4 + CREDIT)
                for k in range(3):
                    n = E * D >> (k + 1)
                    if k:
                        wait_apart(pool, m["sum"], i * 6 + 3 * j + k, stood)
                    half = prod[:, :, 0:n]
                    nc.gpsimd.tensor_tensor(half, half, prod[:, :, n:2 * n], ALU.add).then_inc(m["sum"], 1)
                wait_apart(pool, m["sum"], i * 6 + 3 * j + 3, stood)
                h = group(tok, i, j)
                nc.gpsimd.tensor_tensor(h, h, prod[:, :, 0:D], ALU.add).then_inc(m["h"], 1)

            with pool.Fori(0, STEPS) as i:
                for j in range(2):
                    combine(s["moe0"], i, j)
                deviations(s["attn1"], i)
            with pool.Fori(0, STEPS) as i:
                deviations(s["gatein1"], i)
            with pool.Fori(0, STEPS) as i:
                for j in range(2):
                    combine(s["moe1"], i, j)

        @block.vector
        def _(dve):
            V = nc.vector

            def statistics(m, i):
                for t in range(2 * G_TILES):
                    V.bn_stats(stats[:, t], tok[:, bass.ds(i * 8 + t, 1)].rearrange("p a n -> p (a n)")).then_inc(m["bn"], 1)
                wait_apart(dve, m["bn"], i * 16 + 8, stood)
                for t in range(2 * G_TILES):
                    V.bn_aggr(mv[:, t], stats[:, t]).then_inc(m["bn"], 1)
                dve.wait_ge(m["bn"], i * 16 + 16)
                k = bass.ds(i * 8, 8)
                V.tensor_copy(mean[:, k], mv[:, :, 0])
                V.tensor_scalar(var_eps[:, k], mv[:, :, 1], EPS, None, ALU.add).then_inc(m["var"], 1)
                wait_apart(dve, m["var"], i + 1, stood)

            def layernorm(m, i, slots=slice(0, 2)):
                k = bass.ds(i * 8, 8)
                wide = lambda a: a.broadcast_to((128, 8, D))
                xi = x[:, slots].rearrange("p j t d -> p (j t) d")
                V.tensor_tensor(xi, tok[:, k], wide(mean[:, k, None]), ALU.subtract).then_inc(m["dev"], 1)
                dve.wait_ge(m["dev"], i + 1)
                dve.wait_ge(m["rstd"], i + 1)
                V.tensor_tensor(xi, xi, wide(rstd[:, k, None]), ALU.mult).then_inc(m["x"], 1)

            def low(m, i, banks=(0, 1)):
                for j in range(2):
                    dve.wait_ge(m["xh"], i * 2 + j + 1)
                    cols = bass.ds(i * 1024 + 512 * j, 512)
                    V.tensor_tensor(xs[64:128, cols], bank[banks[j]][0:64, :], xs[0:64, cols], ALU.subtract).then_inc(m["xl"], 1)

            def attention(n):
                m = s[f"attn{n}"]

                def first():
                    layernorm(m, 0)
                    low(m, 0)

                def body(i, last_step):
                    for j in range(2):
                        dve.wait_ge(m["qk"], i * 2 + j + 1)
                        if n == 0:
                            for dst, b, table in ((rope_a, 2, "rope_cos"), (rope_b, 4, "rope_sin")):
                                last = V.tensor_tensor(dst[:, j].rearrange("p (b x) -> p b x", x=S), bank[b + j][:].rearrange("p (b x) -> p b x", x=S),
                                                       c[table][:, None, :].broadcast_to((128, 8, S)), ALU.mult)
                            last.then_inc(m["rope_t"], 1)
                            dve.wait_ge(m["rope_t"], i * 2 + j + 1)
                            V.tensor_tensor(k_t[:, j], rope_a[64:128, j], rope_b[64:128, j], ALU.add).then_inc(m["k"], 1)
                        else:
                            V.tensor_copy(q_t[:, j], bank[2 + j][0:64, :]).then_inc(m["q"], 1)
                            V.tensor_copy(k_t[:, j], bank[2 + j][64:128, :]).then_inc(m["k"], 1)
                    if not last_step:
                        dve.wait_ge(m["tr"], i * 2 + 2)
                        layernorm(m, i + 1)
                    for j in range(2):
                        dve.wait_ge(m["sc"], i * 2 + j + 1)
                        sc = bank[4 + j][:].rearrange("p (t n) -> p t n", t=G_TILES)
                        mask = c[f"mask{n}"][:, None, :].broadcast_to((128, G_TILES, 128))
                        o = att[:, j].rearrange("p (t n) -> p t n", t=G_TILES)
                        if n == 0:
                            V.tensor_tensor(o, sc, mask, ALU.mult).then_inc(m["att"], 1)
                        else:
                            V.scalar_tensor_tensor(o, sc, 0.0, mask, ALU.max, ALU.mult).then_inc(m["att"], 1)
                    if not last_step:
                        low(m, i + 1)
                    for j in range(2):
                        dve.wait_ge(m["ctx"], i * 2 + j + 1)
                        h = group(tok, i, j)
                        V.tensor_tensor(h, h, bank[2 + j][:].rearrange("p (t n) -> p t n", t=G_TILES)[:, :, 0:D], ALU.add).then_inc(m["h"], 1)
                    wait_apart(dve, m["h"], i * 2 + 2, stood)
                    statistics(s[f"gatein{n}"], i)

                steps(dve, first, body)

            def gate_inputs(n):
                m = s[f"gatein{n}"]
                with dve.Fori(0, STEPS // 2) as half:
                    for k in range(2):
                        layernorm(m, half * 2 + k, slice(2 * k, 2 * k + 2))
                    for k in range(2):
                        i = half * 2 + k
                        if n == 1:
                            dve.wait_ge(m["x"], i + 1)
                            h = tok[:, bass.ds(i * 8, 8)]
                            V.tensor_tensor(h, h, x[:, 2 * k:2 * k + 2].rearrange("p j t d -> p (j t) d"), ALU.add).then_inc(m["res"], 1)
                        low(m, i, T_BANKS[2 * k:2 * k + 2])
                    if n == 1:
                        dve.wait_ge(m["res"], half * 2 + 2)
                    for k in range(4):
                        dve.wait_ge(m["lg"], half * 4 + k + 1)
                        lg = bank[LG_BANKS[k]][:, 0:32].rearrange("p (t e) -> p t e", e=E)
                        g = gate[:, bass.ds(half * 16 + 4 * k, 4)]
                        if n == 0:
                            V.tensor_tensor(g, lg, c["gate_b"][:, None, :].broadcast_to((128, G_TILES, E)), ALU.add).then_inc(m["lgc"], 1)
                        else:
                            V.tensor_copy(g, lg).then_inc(m["lgc"], 1)

            def top_two(n):
                wide = lambda a: a[:, :, None].broadcast_to((128, 32, E))

                def step(ins):
                    gate_count[0] += 1
                    ins.then_inc(gate_s, 1)
                    dve.wait_ge(gate_s, gate_count[0])

                step(V.tensor_reduce(row_max, gate, X_AXIS, ALU.max))
                V.tensor_tensor(prob, gate, wide(row_max), ALU.subtract).then_inc(shifted, 1)
                dve.wait_ge(exp_s, n + 1)
                step(V.tensor_reduce(row_sum, prob, X_AXIS, ALU.add))
                step(V.reciprocal(row_sum, row_sum))
                step(V.tensor_tensor(prob, prob, wide(row_sum), ALU.mult))
                for t in range(32):
                    last = V.max(top[:, t], prob[:, t])
                step(last)
                step(V.tensor_tensor(wgt, prob, top[:, :, 1:2].broadcast_to((128, 32, E)), ALU.is_ge))
                step(V.tensor_tensor(wgt, wgt, prob, ALU.mult))
                if n == 1:
                    step(V.tensor_tensor(row_sum, top[:, :, 0], top[:, :, 1], ALU.add))
                    step(V.tensor_scalar(row_sum, row_sum, MIN_SUM, None, ALU.max))
                    step(V.reciprocal(row_sum, row_sum))
                    step(V.tensor_tensor(wgt, wgt, wide(row_sum), ALU.mult))

            def experts(n):
                m = s[f"moe{n}"]
                H = E if n == 0 else E // 2
                dve.sem_inc(m["free"], CREDIT)
                dve.sem_inc(m["h"], CREDIT)

                def statistics_of(i):
                    if n == 0:
                        wait_apart(dve, m["h"], i * 2 + 2 + CREDIT, stood)
                        statistics(s["attn1"], i)

                def body(i, first):
                    for k in range(2 * H):
                        dve.wait_ge(m["high"], i * 2 * H + k + 1 + CREDIT)
                        V.tensor_tensor(hid_l[:, k % HID], hid[:, k % HID], hid_h[:, k % HID], ALU.subtract).then_inc(m["low"], 1)
                        if k == H:
                            combine(n, i, 0)
                        if k == 0 and not first:
                            combine(n, i - 1, 1)
                        if k == H - 1 and not first:
                            statistics_of(i - 1)

                body(0, True)
                with dve.Fori(1, STEPS) as i:
                    body(i, False)
                combine(n, STEPS - 1, 1)
                statistics_of(STEPS - 1)

            def combine(n, i, j):
                m = s[f"moe{n}"]
                H = E if n == 0 else E // 2
                dve.wait_ge(m["y"], i * 2 * H + (j + 1) * H + CREDIT)
                dve.wait_ge(m["h"], i * 2 + j + CREDIT)
                for t in range(G_TILES):
                    wt = wgt[:, bass.ds(i * 8 + 4 * j + t, 1)].rearrange("p a e -> p (a e)")
                    V.tensor_tensor(prod[:, t].rearrange("p (e d) -> p e d", e=E), bank[2 + t][:].rearrange("p (e d) -> p e d", e=E),
                                    wt[:, :, None].broadcast_to((128, E, D)), ALU.mult).then_inc(m["free"], 1)

            for i in range(STEPS):
                statistics(s["attn0"], i)
            attention(0)
            dve.wait_ge(s["attn0"]["h"], 2 * STEPS)
            gate_inputs(0)
            dve.wait_ge(s["gatein0"]["lgc"], 2 * STEPS)
            top_two(0)
            experts(0)
            dve.wait_ge(s["moe0"]["h"], 2 * STEPS + CREDIT)
            attention(1)
            dve.wait_ge(s["attn1"]["h"], 2 * STEPS)
            gate_inputs(1)
            dve.wait_ge(s["gatein1"]["lgc"], 2 * STEPS)
            dve.wait_ge(s["gatein1"]["res"], STEPS)
            top_two(1)
            experts(1)


def token_layout(inp):
    f = lambda a: np.ascontiguousarray(a, dtype=np.float32)
    g = lambda n: inp[n]
    swap = np.arange(D).reshape(-1, 2)[:, ::-1].ravel()
    o = {}
    parts = {
        "wqk0": np.concatenate([g("L0_attn_W_Q"), g("L0_attn_W_K")], 1),
        "wqks0": np.concatenate([g("L0_attn_W_Q")[:, swap], g("L0_attn_W_K")[:, swap]], 1),
        "wv0": g("L0_attn_W_V"), "gate_w0": g("L0_ffn_gate_w"),
        "w1_0": g("L0_ffn_W1").transpose(1, 0, 2).reshape(D, E * 128),
        "wqk1": np.concatenate([g("L1_attn_Wq").T, g("L1_attn_Wk").T], 1),
        "gate_w1": g("L1_ffn_router_w").T, "w1_1": g("L1_ffn_w1").transpose(1, 0, 2).reshape(D, E * D)}
    o["w64"] = f(np.tile(np.concatenate([parts[n] for n in W64], 1), (2, 1)))
    o["wv1_l"] = f(np.tile(g("L1_attn_Wv"), (1, 2)))
    o["wo1"] = f(g("L1_attn_Wo").T)
    o["gate_b"] = f(np.broadcast_to(g("L0_ffn_gate_b")[None], (128, E)))
    o["b1_0"] = f(g("L0_ffn_b1").T)
    o["b1_1"] = f(g("L1_ffn_b1").reshape(E // 2, 128).T)
    o["w2_0"] = f(g("L0_ffn_W2").transpose(1, 0, 2).reshape(128, E * D))
    w2 = np.zeros((E // 2, 2, D, 2, D), np.float32)
    for k in range(2):
        w2[:, k, :, k] = g("L1_ffn_w2").reshape(E // 2, 2, D, D)[:, k]
    o["w2_1"] = f(w2.transpose(1, 2, 0, 3, 4).reshape(128, E // 2 * 128))
    o["b2"] = f(np.concatenate([g("L0_ffn_b2").reshape(1, -1), g("L1_ffn_b2").reshape(1, -1)], 1))
    return o | token_constants()


def host_layout(x, inp):
    f = lambda a: np.ascontiguousarray(a)
    p_w, p_b, fw = inp["L0_tok_p_w"], inp["L0_tok_p_b"], inp["L0_tok_fw"]
    w1, b1, w2, b2 = inp["L0_tok_w1_w"], inp["L0_tok_w1_b"], inp["L0_tok_w2_w"], inp["L0_tok_w2_b"]
    q1, q1b, q2, q2b = inp["L0_tok_q1_w"], inp["L0_tok_q1_b"], inp["L0_tok_q2_w"], inp["L0_tok_q2_b"]
    o = {}
    o["xT"] = f(x[..., 0].reshape(NC_ // 2, 2, BH, BQ, S, S).transpose(1, 5, 0, 3, 2, 4).reshape(2 * S, NC_ // 2 * COLS))
    w_in, w_1 = np.zeros((L + 1, 4, C, 4, C), np.float32), np.zeros((L + 1, 4, C, 4, C), np.float32)
    for q in range(4):
        w_in[0, q, :3, q] = p_w.T
        w_in[1:L, q, :, q] = w2[:L - 1].transpose(0, 2, 1)
        w_1[:L, q, :, q] = w1.transpose(0, 2, 1)
    o["w_in"], o["w_1"] = w_in.reshape(-1, 128), w_1.reshape(-1, 128)
    o["bias_s"] = f(np.concatenate([p_b[None], b2]).T)
    o["bias_1"] = f(b1.T)
    w = fw.transpose(0, 1, 2, 4, 5, 6, 3)
    o["w_modes"] = f(np.stack([w, w[..., ::-1, :]], 2).reshape(L * 128, M * M * 64))
    o["w2e"] = np.zeros(((L + 1) * C, C * Y32), np.float32)
    o["w2e"][:L * C] = np.repeat(w2.reshape(L * C, C), Y32, axis=1)
    q1a = np.concatenate([q1.T, q1b[None]])
    o["q1a"] = f(np.repeat(q1a, Y32, axis=1))
    pexp = np.zeros((33, 128), np.float32)
    pexp[:32] = p_w[:, 0:1]
    p12 = np.zeros((33, 3), np.float32)
    p12[:32, :2] = p_w[:, 1:3]
    p12[32, 2] = 1.0
    o["pexp"], o["p12"] = pexp, p12
    o["q2s"] = f(np.repeat(q2[0], Y32)[:, None])
    o["q2b"] = f(np.broadcast_to(q2b.reshape(1, 1), (128, 1)))
    return o | dft_constants() | token_layout(inp)


def kernel(**inputs):
    import concourse.bacc as bacc
    from concourse.bass_utils import run_bass_kernel_spmd as run
    inp = {k: np.asarray(v) for k, v in inputs.items()}
    arrays = host_layout(inp["x"], inp)
    nc = bacc.Bacc("TRN2", target_bir_lowering=False, num_devices=1)
    d = {n: nc.dram_tensor("in_" + n, a.shape, mybir.dt.from_np(a.dtype), kind="ExternalInput").ap() for n, a in arrays.items()}
    out = nc.dram_tensor("out", (B // BQ, BQ, S, S), mybir.dt.float32, kind="ExternalOutput").ap()
    fno(nc, d, out)
    r = run(nc, [{"in_" + n: a for n, a in arrays.items()}], core_ids=[0])
    return np.asarray(r.results[0]["out"]).reshape(B, S, S)
```

```python
import concourse.bass as bass
from concourse import mybir
from contextlib import ExitStack
import numpy as np

B, S, C, L, M, MID = 64, 64, 32, 4, 12, 4
NC_, BH, BQ = 8, 2, 4
NB = B // BQ
OG = 8
O4, Y32 = 4, 32
COLS = BQ * BH * S
SPEC = B * M
HALF = SPEC // 2
UNITS = NC_ * OG


def dft_constants():
    n = np.arange(S)
    kx = np.concatenate([np.arange(M), np.arange(S - M, S)])
    ky = np.arange(M)
    rt = np.sqrt(S)
    wx = 2 * np.pi * np.outer(kx, n) / S
    wy = 2 * np.pi * np.outer(ky, n) / S
    cx, sx, cy, sy = np.cos(wx) / rt, np.sin(wx) / rt, np.cos(wy) / rt, np.sin(wy) / rt
    twice = np.where(ky == 0, 1.0, 2.0)[:, None]
    inv_x = np.zeros((BH, 2, 2, M, 2, BH, S))
    fwd_x = np.zeros((BH, S, 2, BH, 2, 2, M))
    for b in range(BH):
        for g in range(2):
            c, s = cx[g * M:(g + 1) * M], sx[g * M:(g + 1) * M]
            inv_x[b, g, 0, :, 0, b], inv_x[b, g, 1, :, 0, b] = c, -s
            inv_x[b, g, 0, :, 1, b], inv_x[b, g, 1, :, 1, b] = s, c
            fwd_x[b, :, 0, b, g, 0], fwd_x[b, :, 1, b, g, 0] = c.T, s.T
            fwd_x[b, :, 0, b, g, 1], fwd_x[b, :, 1, b, g, 1] = -s.T, c.T
    inv_x, fwd_x = inv_x.transpose(0, 3, 1, 2, 4, 5, 6), fwd_x.transpose(0, 1, 2, 3, 6, 4, 5)
    inv_y = np.zeros((128, 2, O4, Y32))
    fwd_y = np.zeros((O4, Y32, 2, 2, O4, M))
    for o in range(O4):
        for h in range(2):
            y = slice(h * Y32, (h + 1) * Y32)
            inv_y[o * M:(o + 1) * M, h, o] = (twice * cy)[:, y]
            inv_y[64 + o * M:64 + (o + 1) * M, h, o] = -(twice * sy)[:, y]
            fwd_y[o, :, h, 0, o] = cy[:, y].T
            fwd_y[o, :, h, 1, o] = -sy[:, y].T
    first_y = np.concatenate([cy.T, -sy.T], 1)
    line = np.linspace(0.0, 1.0, S)
    grids = []
    for image in (np.broadcast_to(line[:, None], (S, S)), np.broadcast_to(line[None, :], (S, S))):
        f = (cx - 1j * sx) @ image @ (cy - 1j * sy).T
        f = f.reshape(2, M, M)
        grids.append(np.stack([f.real, f.imag], 1).transpose(2, 0, 1, 3).reshape(4 * M, M))
    grid_spec = np.broadcast_to(np.stack(grids, 1)[:, :, None, :, None], (4 * M, 2, NB, M, BQ)).reshape(4 * M, 2, SPEC)
    gl = np.ones((3, 2, MID, Y32))
    gl[1] = line.reshape(2, 1, Y32)
    gr = np.ones((3, S))
    gr[0] = line
    eye = np.zeros((O4, Y32, MID, Y32))
    eye[:, np.arange(Y32), :, np.arange(Y32)] = 1.0
    sign = np.ones((128, 1))
    for g in range(2):
        sign[64 * g + 32:64 * g + 64] = -1.0
    f = lambda a, *s: np.ascontiguousarray(a.reshape(*s), dtype=np.float32)
    out = {
        "fwd_x": f(fwd_x / G_SCALE, 128, 2 * 96), "first_y": f(G_SCALE * np.kron(np.eye(2), first_y), 2 * S, 2 * 2 * M),
        "grid_spec": f(grid_spec, 48, 2 * SPEC), "grid_l": f(H_SCALE * gl, 3, 256), "grid_r": f(gr, 3, S),
        "eye": f(Q_SCALE * eye, 128, 128), "sign": f(sign, 128, 1),
    }
    for name, a, shape in (("inv_x", T_SCALE * inv_x, (96, 256)), ("fwd_x", X_SCALE * fwd_x, (128, 192)), ("inv_y", U_SCALE * inv_y, (128, 256)), ("fwd_y", F_SCALE * fwd_y, (128, 192))):
        hi = a.reshape(shape).astype(np.float16)
        lo = (a.reshape(shape) - hi.astype(np.float64)).astype(np.float16)
        out[name + "_h"], out[name + "_l"] = hi, lo
    return out

T_SCALE, U_SCALE, F_SCALE, Q_SCALE = 4.0, 8.0, 8.0, 16.0
R_SCALE = T_SCALE * U_SCALE
G_SCALE = R_SCALE * F_SCALE
GS_SCALE, X_SCALE = 4.0, 8.0
H_SCALE = R_SCALE * Q_SCALE
CREDIT = 8


def wait_apart(eng, sem, value, stood):
    eng.wait_ge(sem, value)
    eng.sem_inc(stood, 1)


def build_program(nc, d, out):
    f32, f16 = mybir.dt.float32, mybir.dt.float16
    ALU, ACT = mybir.AluOpType, mybir.ActivationFunctionType
    with ExitStack() as ctx:
        sb = lambda n, s, t=f32: ctx.enter_context(nc.sbuf_tensor(n, s, t))
        sem = lambda n: ctx.enter_context(nc.semaphore(n))
        bank = [ctx.enter_context(nc.psum_tensor(f"bank{i}", [128, 512], f32)) for i in range(8)]
        Yd = nc.dram_tensor("y_spectrum", (M, 4, C, NB, M * BQ), f32, kind="Internal").ap()
        Sd = nc.dram_tensor("r_spectrum", (M, 4, C, NB, M * BQ), f32, kind="Internal").ap()
        Yd48 = Yd.rearrange("x q o b n -> (x q) o b n")
        Sd48 = Sd.rearrange("x q o b n -> (x q) o b n")

        fwd_x_f = sb("fwd_x_f", [128, 2, 96])
        inv_x = [sb(f"inv_x{i}", [96, 2, 128], f16) for i in "hl"]
        fwd_x = [sb(f"fwd_x{i}", [128, 2, 96], f16) for i in "hl"]
        inv_y = [sb(f"inv_y{i}", [128, 2, 128], f16) for i in "hl"]
        fwd_y = [sb(f"fwd_y{i}", [128, 2, 96], f16) for i in "hl"]
        eye, sign = sb("eye_sb", [128, 128]), sb("sign_sb", [128, 1])
        q1a, bias_s, bias_1 = sb("q1a_sb", [33, 128]), sb("bias_s_sb", [32, 5]), sb("bias_1_sb", [32, 4])
        bias_s64, bias_1_64 = sb("bias_s64", [32, 4]), sb("bias_1_64", [32, 4])
        Sp = sb("S_spec", [128, M, NB, M, BQ])
        Wm = sb("W_modes", [128, M, M, 64])
        acc = sb("head_acc", [128, NC_, 2, COLS])
        w_in, w_1 = sb("w_in", [128, 128]), sb("w_1", [128, 128])
        w2e = sb("w2_exp", [32, OG, 128])
        q_tmp = sb("q_tmp", [128, 4, 128])
        q_st = [sb(f"q_st{i}", [128, OG, 128], f16) for i in "hl"]
        sd = sb("sd_ring", [128, 3, SPEC])
        ym = sb("ym_ring", [128, 2, M // 2, B])
        y1 = sb("y1_ring", [128, 2, NB, M, BQ])
        yin = sb("yin", [96, 2, 16, M, BQ])
        ys = [sb(f"yin_{i}", [96, 2, 16, M, BQ], f16) for i in "hl"]
        t1 = [sb(f"t1{i}", [128, 2, COLS], f16) for i in "hl"]
        r = [sb(f"r{i}", [128, 2, 2, COLS], f16) for i in "hl"]
        gs = [sb(f"gs{i}", [128, 2, BQ, 2, 48], f16) for i in "hl"]
        ss = sb("ss", [96, 2, 16, M, BQ])
        tok = sb("tok", [128, 32, 64])
        q2s, q2b, q2c = sb("q2s_sb", [128, 1]), sb("q2b_sb", [128, 1]), sb("q2c", [128, Y32])
        ident = sb("ident", [128, 128])
        head = sd[:].rearrange("p a n -> p (a n)")[:, 0:NC_ // 2 * COLS].rearrange("p (i n) -> p i n", n=COLS)
        xT = tok[:].rearrange("p a b -> p (a b)")
        g0 = ym[:].rearrange("p h k b -> p (h k b)").rearrange("p (t r k) -> p t r k", t=32, r=2)
        yin_flat, q_flat = yin[:].rearrange("p a o k q -> p (a o k q)"), q_tmp[:].rearrange("p a b -> p (a b)")
        grid_l, gl = yin_flat[0:3, 0:256], yin_flat[0:3, 256:512]
        p0, p12, first_y = q_flat[0:33, 0:1], q_flat[0:33, 128:131], q_flat[:, 136:184]
        grid_r = q_flat[0:3, 192:256]
        w_img, g2 = sb("w_image", [128, 1]), sb("grid_part", [128, 128])

        b = token_buffers(sb, Sp[:].rearrange("p x b k q -> p (x b k q)"), Wm[:].rearrange("p x k o -> p (x k o)"),
                          acc[:].rearrange("p c h n -> p (c h n)"))
        b_l, b_split = sem("token_constants_loaded"), sem("token_weights_split")
        wvo_p, wvo_h = sem("wvo_product"), sem("wvo_high")
        ld, ld_x = sem("constants_loaded"), sem("image_loaded")
        zero = sem("zeroed")
        pre = sem("first_spectrum_stored")
        x_l, acc_img, acc_ready = sem("head_images_loaded"), sem("head_images_weighted"), sem("head_sum_ready")
        p_pe, p_ev = sem("prologue_product"), sem("prologue_evacuated")
        wl, w2l = sem("layer_weights_loaded"), sem("w2_expanded_loaded")
        wm_l, wm_s = [sem(f"mode_weights_loaded{i}") for i in range(M)], sem("mode_weights_signed")
        sd_l, sd_l0 = [sem(f"slab_loaded{i}") for i in range(3)], [sem(f"first_slab_loaded{i}") for i in range(3)]
        pe_w2, ev_w2 = sem("w2_mixed"), sem("S_updated")
        pe_mix, ev_a, ev_b = sem("modes_mixed"), sem("mixed_evac_g0"), sem("mixed_evac_g1")
        pe_w1, ev_w1, ev_db = sem("w1_mixed"), sem("y1_evacuated"), sem("y1_biased")
        bs_done = sem("S_biased")
        y_st = [sem(f"y_stored{i}") for i in range(2)]
        pe_qb, ev_qt, ev_qh, ev_ql = sem("q_built"), sem("q_masked"), sem("q_high"), sem("q_low")
        yin_l = [sem(f"yin_loaded{i}") for i in range(2)]
        pe_t, ev_th, ev_tl = sem("t1_product"), sem("t1_high"), sem("t1_low")
        pe_u, ev_rh, ev_rl = sem("u_product"), sem("r_high"), sem("r_low")
        pe_q, ev_q = sem("q_product"), sem("q_added")
        y_high, y_split = sem("yin_high"), sem("yin_split")
        pe_g, ev_g, ev_gl = sem("g_product"), sem("g_high"), sem("g_low")
        pe_s, ev_s = sem("s_product"), sem("s_evacuated")
        s_out = [sem(f"s_stored{i}") for i in range(2)]
        relu_d, pe_f, ev_f, q2_d = sem("head_relu"), sem("head_product"), sem("tok_ready"), sem("q2_ready")
        stood = sem("wait_stood_apart")
        LOADS_X = ["xT", "first_y", "fwd_x"]
        LOADS = ["inv_x_h", "inv_x_l", "fwd_x_h", "fwd_x_l", "inv_y_h", "inv_y_l", "fwd_y_h", "fwd_y_l", "eye", "sign", "q1a", "bias_s", "bias_1",
                 "grid_l", "grid_r", "p0", "p12", "q2s", "q2b", "ident"]
        dst = {"inv_x_h": inv_x[0][:].rearrange("p a b -> p (a b)"), "inv_x_l": inv_x[1][:].rearrange("p a b -> p (a b)"),
               "fwd_x_h": fwd_x[0][:].rearrange("p a b -> p (a b)"), "fwd_x_l": fwd_x[1][:].rearrange("p a b -> p (a b)"),
               "fwd_x": fwd_x_f[:].rearrange("p a b -> p (a b)"),
               "inv_y_h": inv_y[0][:].rearrange("p a b -> p (a b)"), "inv_y_l": inv_y[1][:].rearrange("p a b -> p (a b)"),
               "fwd_y_h": fwd_y[0][:].rearrange("p a b -> p (a b)"), "fwd_y_l": fwd_y[1][:].rearrange("p a b -> p (a b)"),
               "eye": eye[:], "sign": sign[:], "q1a": q1a[:], "bias_s": bias_s[:], "bias_1": bias_1[:], "xT": xT,
               "grid_l": grid_l, "grid_r": grid_r, "p0": p0, "p12": p12, "first_y": first_y,
               "q2s": q2s[:], "q2b": q2b[:], "ident": ident[:]}
        LOADED = 16 * len(LOADS)
        with nc.Block() as block:
            @block.sync
            def _(sp):
                for n in LOADS_X:
                    sp.dma_start(dst[n], d[n]).then_inc(ld_x, 16)
                sp.dma_start(Sd48[:, 1:3].rearrange("p o b n -> p o (b n)"), d["grid_spec"].rearrange("p (o n) -> p o n", o=2)).then_inc(pre, 16)
                for n in LOADS:
                    sp.dma_start(dst[n], d[n]).then_inc(ld, 16)

                def load_weights(l):
                    sp.dma_start(w_in[:], d["w_in"][bass.ds(l * 128, 128), :]).then_inc(wl, 16)
                    sp.dma_start(w_1[:], d["w_1"][bass.ds(l * 128, 128), :]).then_inc(wl, 16)
                    sp.dma_start(w2e[:].rearrange("p a b -> p (a b)"), d["w2e"][bass.ds(l * 32, 32), :]).then_inc(w2l, 16)

                load_weights(0)
                sp.sem_inc(s_out[0], CREDIT)
                sp.sem_inc(s_out[1], CREDIT)
                sp.wait_ge(p_ev, 3)
                for bh in range(BH):
                    sp.dma_start(Sd48[:, 0].rearrange("p (c h) n -> p c h n", h=BH)[:, :, bh],
                                 ss[48 * bh:48 * bh + 48].rearrange("p a o k q -> p (a o) (k q)")[:, 0:NC_]).then_inc(pre, 16)
                sp.wait_ge(pre, 16 * 3)
                sp.wait_ge(zero, 1)

                def layer(l, first, last_layer):
                    if not first:
                        sp.wait_ge(s_out[0], l * NC_ * 32 + CREDIT)
                        sp.wait_ge(s_out[1], l * NC_ * 32 + CREDIT)

                    def store_y(x):
                        wait_apart(sp, ev_w1, l * 2 * M + 2 * x + 2, stood)
                        if x == 0:
                            sp.wait_ge(ev_db, l + 1)
                        sp.dma_start(Yd[x].rearrange("q o b n -> (q o) (b n)"),
                                     y1[:, x % 2].rearrange("p b k q -> p (b k q)")).then_inc(y_st[x % 2], 16)

                    for x in range(M):
                        if not first or x >= 3:
                            sp.wait_ge(pe_w2, l * 2 * M + 2 * (x - 3) + 2 + CREDIT)
                        if first:
                            for q in range(4):
                                sp.dma_start(sd[32 * q:32 * q + 3, x % 3], Sd[x, q, 0:3].rearrange("o b n -> o (b n)")).then_inc((sd_l if q == 0 else sd_l0)[x % 3], 16)
                        else:
                            sp.dma_start(sd[:, x % 3], Sd[x].rearrange("q o b n -> (q o) (b n)")).then_inc(sd_l[x % 3], 16)
                        if first and 1 <= x <= 8:
                            m, half = divmod(x - 1, 2)
                            sp.dma_start(acc[32 * m:32 * m + 32, 4 * half:4 * half + 4].rearrange("p c h n -> p (c h n)"),
                                         d["x_head"][:, half * 4096:(half + 1) * 4096]).then_inc(x_l, 16)
                        if x >= 4:
                            store_y(x - 4)
                    for x in range(M - 4, M):
                        store_y(x)
                    sp.wait_ge(y_st[0], (l + 1) * 6 * 16)
                    sp.wait_ge(y_st[1], (l + 1) * 6 * 16)

                    def load_yin(c, h):
                        for bh in range(BH):
                            sp.dma_start(yin[48 * bh:48 * bh + 48, h].rearrange("p o k q -> p o (k q)"),
                                         Yd48[:, 16 * h:16 * h + 16, bass.ds(c * BH + bh, 1), :].rearrange("p o b n -> p o (b n)")).then_inc(yin_l[h], 16)

                    def store_s(c, h, k):
                        if last_layer:
                            return
                        sp.wait_ge(ev_s, l * UNITS + k)
                        for bh in range(BH):
                            sp.dma_start(Sd48[:, 16 * h:16 * h + 16, bass.ds(c * BH + bh, 1), :].rearrange("p o b n -> p o (b n)"),
                                         ss[48 * bh:48 * bh + 48, h].rearrange("p o k q -> p o (k q)")).then_inc(s_out[h], 16)

                    load_yin(0, 0)
                    load_yin(0, 1)
                    load_weights(l + 1)
                    sp.wait_ge(y_split, l * 2 * NC_ + 1)
                    load_yin(1, 0)
                    sp.wait_ge(y_split, l * 2 * NC_ + 2)
                    load_yin(1, 1)
                    store_s(0, 0, 4 + CREDIT)
                    with sp.Fori(1, NC_ - 1) as c:
                        store_s(c - 1, 1, c * OG + CREDIT)
                        sp.wait_ge(y_split, l * 2 * NC_ + c * 2 + 1)
                        load_yin(c + 1, 0)
                        sp.wait_ge(y_split, l * 2 * NC_ + c * 2 + 2)
                        load_yin(c + 1, 1)
                        store_s(c, 0, c * OG + 4 + CREDIT)
                    c = NC_ - 1
                    store_s(c - 1, 1, c * OG + CREDIT)
                    store_s(c, 0, c * OG + 4 + CREDIT)
                    store_s(c, 1, c * OG + 8 + CREDIT)

                layer(0, True, False)
                with sp.Fori(1, L - 1) as l:
                    layer(l, False, False)
                layer(L - 1, False, True)
                for h in range(2):
                    sp.wait_ge(s_out[h], (L - 1) * NC_ * 32 + CREDIT)

            @block.gpsimd
            def _(pool):
                def load_modes(l):
                    for x in range(M):
                        pool.dma_start(Wm[:, x].rearrange("p k o -> p (k o)"),
                                       d["w_modes"][bass.ds(l * 128, 128), x * 768:(x + 1) * 768]).then_inc(wm_l[x], 16)

                def sign_modes(l):
                    for x in range(M):
                        wait_apart(pool, wm_l[x], l * 16 + 16, stood)
                        w = Wm[:, x, :, 0:32]
                        nc.gpsimd.tensor_scalar(w, w, sign[:, 0:1], None, ALU.mult).then_inc(wm_s, 1)

                nc.gpsimd.memset(sd[:], 0.0).then_inc(zero, 1)
                nc.gpsimd.memset(Sp[:], 0.0).then_inc(zero, 1)
                load_modes(0)
                pool.wait_ge(ld, LOADED)

                def split_y(l, c):
                    for h in range(2):
                        wait_apart(pool, yin_l[h], l * NC_ * 32 + c * 32 + 32, stood)
                        wait_apart(pool, pe_t, l * UNITS + (c - 1) * OG + 4 * h + 4, stood)
                        flat = lambda t: t[:, h].rearrange("p o k q -> p (o k q)")
                        nc.gpsimd.tensor_copy(flat(ys[0]), flat(yin)).then_inc(y_high, 1)
                        wait_apart(pool, y_high, l * 2 * NC_ + c * 2 + h + 1, stood)
                        nc.gpsimd.tensor_tensor(flat(ys[1]), flat(yin), flat(ys[0]), ALU.subtract).then_inc(y_split, 1)

                def split_chunks(l):
                    with pool.Fori(1, NC_) as c:
                        split_y(l, c)

                sign_modes(0)
                pool.wait_ge(p_ev, 7)
                pool.wait_ge(x_l, 16 * 8)
                for c in range(NC_):
                    for h in range(2):
                        v = acc[:, c, h].rearrange("p (b x) -> p b x", x=S)
                        nc.gpsimd.tensor_tensor(acc[:, c, h], acc[:, c, h], w_img[:, 0:1].broadcast_to((128, COLS)), ALU.mult).then_inc(acc_img, 1)
                        pool.wait_ge(acc_img, 2 * c + h + 1)
                        nc.gpsimd.tensor_tensor(v, v, g2[:, None, 64 * h:64 * h + 64].broadcast_to((128, 8, 64)), ALU.add).then_inc(acc_ready, 1)
                with pool.Fori(0, L - 1) as l:
                    pool.wait_ge(y_split, l * 2 * NC_ + 2)
                    pool.wait_ge(pe_mix, (l + 1) * 2 * M + CREDIT)
                    load_modes(l + 1)
                    split_chunks(l)
                    sign_modes(l + 1)
                pool.wait_ge(pe_mix, L * 2 * M + CREDIT)
                for tile, n in b.loads:
                    pool.dma_start(tile, d[n]).then_inc(b_l, 16)
                split_chunks(L - 1)
                P = nc.gpsimd
                count = [0]

                def step(ins):
                    count[0] += 1
                    ins.then_inc(b_split, 1)
                    pool.wait_ge(b_split, count[0])

                step(P.memset(b.minus_half[:], -0.5))
                step(P.memset(b.ones[:], 1.0))
                step(P.memset(b.w64_l[64:128], 0.0))
                step(P.memset(b.wvo_l[64:128], 0.0))
                step(P.memset(b.b2hl[:].rearrange("p a n -> p (a n)"), 0.0))
                pool.wait_ge(b_l, 16 * len(b.loads))
                step(P.tensor_copy(b.w64_h[:], b.w64))
                step(P.tensor_tensor(b.w64_l[0:64], b.w64[0:64], b.w64_h[0:64], ALU.subtract))
                b2_h, b2_l = (b.b2hl[k:k + 1].rearrange("p a n -> p (a n)") for k in (0, 32))
                for high, low, whole in ((b.w2_h[0][:], b.w2_l[0][:], b.w2f[0]), (b.w2_h[1][:], b.w2_l[1][:], b.w2f[1]), (b2_h, b2_l, b.b2f)):
                    step(P.tensor_copy(high, whole))
                    step(P.tensor_tensor(low, whole, high, ALU.subtract))

            @block.tensor
            def _(pe):
                mm = nc.tensor.matmul
                for s in (pe_w2, pe_mix, pe_w1, pe_s, pe_u, pe_g, pe_q):
                    pe.sem_inc(s, CREDIT)
                pe.wait_ge(ld_x, 16 * len(LOADS_X))
                for t in range(16):
                    last = mm(bank[t // 8][:, (t % 8) * 48:(t % 8) * 48 + 48], xT[:, t * 128:(t + 1) * 128], first_y, start=True, stop=True)
                last.then_inc(p_pe, 1)
                pe.wait_ge(p_ev, 2)
                for k in range(2):
                    last = mm(bank[2][0:96, 0:384], fwd_x_f[:, k], g0[:, :, k, :], start=(k == 0), stop=(k == 1))
                last.then_inc(p_pe, 1)
                pe.wait_ge(ld, LOADED)
                mm(bank[3][:, 0:1], q1a[:], p0, start=True, stop=True)
                pe.wait_ge(p_ev, 4)
                mm(bank[4][0:3, 0:128], p12, q1a[:], start=True, stop=True).then_inc(p_pe, 1)
                pe.wait_ge(p_ev, 6)
                for h in range(2):
                    last = mm(bank[5][:, 64 * h:64 * h + 64], gl[:, 128 * h:128 * h + 128], grid_r, start=True, stop=True)
                last.then_inc(p_pe, 1)

                def layer(l, last_layer):
                    U = l * UNITS
                    pe.wait_ge(w2l, l * 16 + 16)
                    pe.wait_ge(p_ev, 7)
                    for og in range(OG):
                        mm(bank[og // 4][:, (og % 4) * 128:(og % 4) * 128 + 128], w2e[:, og, :], q1a[0:32, :],
                           start=True, stop=True).then_inc(pe_qb, 1)
                    pe.wait_ge(wl, l * 32 + 32)

                    def mix_in(x, h):
                        if x == 0 and h == 0:
                            pe.wait_ge(ev_s, U + CREDIT)
                        if h == 0:
                            pe.wait_ge(sd_l0[x % 3], (x // 3 + 1) * 48)
                            pe.wait_ge(sd_l[x % 3], l * 4 * 16 + (x // 3 + 1) * 16)
                        pe.wait_ge(ev_w2, l * 2 * M + 2 * x + h + CREDIT)
                        mm(bank[6][:, 0:HALF], w_in[:], sd[:, x % 3, h * HALF:(h + 1) * HALF], start=True, stop=True).then_inc(pe_w2, 1)

                    def mix_modes(x, h):
                        if h == 0:
                            pe.wait_ge(wm_s, l * M + x + 1)
                        pe.wait_ge(ev_w2, l * 2 * M + 2 * x + 2 + CREDIT)
                        if x == 0 and h == 0:
                            pe.wait_ge(ev_qt, l * 2 + 2)
                        pe.wait_ge(ev_a, l * 2 * M + 2 * x + h - 1 + CREDIT)
                        wait_apart(pe, ev_b, l * 2 * M + 2 * x + h - 1 + CREDIT, stood)
                        for k in range(M // 2):
                            for g in range(2):
                                ky = h * (M // 2) + k
                                last = mm(bank[2 * g + h][64 * g:64 * g + 64, 64 * k:64 * k + 64], Wm[64 * g:64 * g + 64, x, ky, :],
                                          Sp[64 * g:64 * g + 64, x, :, ky, :], start=True, stop=True)
                        last.then_inc(pe_mix, 1)

                    def mix_out(x, h):
                        pe.wait_ge(ev_a, l * 2 * M + 2 * x + h + 1 + CREDIT)
                        pe.wait_ge(ev_b, l * 2 * M + 2 * x + h + 1 + CREDIT)
                        if x == 0:
                            pe.wait_ge(ev_q, l * NC_ + CREDIT)
                            pe.wait_ge(ev_gl, U + CREDIT)
                        else:
                            pe.wait_ge(ev_w1, l * 2 * M + 2 * x + h - 1)
                        mm(bank[4 + h][:, 0:HALF], w_1[:], ym[:, h].rearrange("p k b -> p (k b)"), start=True, stop=True).then_inc(pe_w1, 1)

                    for x in range(M + 1):
                        for h in range(2):
                            if x < M:
                                mix_in(x, h)
                            if x >= 1:
                                mix_modes(x - 1, h)
                                if h == 1:
                                    mix_out(x - 1, 0)
                            if h == 0 and x >= 2:
                                mix_out(x - 2, 1)
                    mix_out(M - 1, 1)

                    def t1_product(u, og, c):
                        hh = og // 4
                        if og % 4 == 0:
                            wait_apart(pe, y_split, l * 2 * NC_ + c * 2 + hh + 1, stood)
                        pe.wait_ge(ev_th, u + CREDIT)
                        pe.wait_ge(ev_tl, u + CREDIT)
                        for bq in range(BQ):
                            for k in range(2):
                                for i, (a, b) in enumerate(((0, 0), (1, 0), (0, 1))):
                                    last = mm(bank[7][64 * k:64 * k + 48, bq * 128:bq * 128 + 128],
                                              ys[a][:, hh, (og % 4) * 4:(og % 4) * 4 + 4, :, bq].rearrange("p o k -> p (o k)"), inv_x[b][:, k, :], start=(i == 0), stop=(i == 2))
                        last.then_inc(pe_t, 1)

                    def u_product(u, og):
                        pe.wait_ge(ev_tl, u + 1 + CREDIT)
                        for h in range(2):
                            pe.wait_ge(ev_rl, 2 * u + h - 1 + CREDIT)
                            for i, (a, b) in enumerate(((0, 0), (1, 0), (0, 1))):
                                last = mm(bank[1 + h][:], inv_y[b][0:112, h], t1[a][0:112, og % 2], start=(i == 0), stop=(i == 2))
                            last.then_inc(pe_u, 1)

                    def q_product(u, og, c):
                        pe.wait_ge(ev_rl, 2 * u + 2 + CREDIT)
                        if og == 0:
                            pe.wait_ge(ev_q, l * NC_ + c + CREDIT)
                        for h in range(2):
                            for i, (a, b) in enumerate(((0, 0), (1, 0), (0, 1))):
                                last = mm(bank[3 + h][:], q_st[b][:, og], r[a][:, og % 2, h], start=(og == 0 and i == 0), stop=(og == OG - 1 and i == 2))
                        if og == OG - 1:
                            last.then_inc(pe_q, 1)

                    def g_product(u, og):
                        pe.wait_ge(ev_rl, 2 * u + 2 + CREDIT)
                        pe.wait_ge(ev_gl, u + CREDIT)
                        for bq in range(BQ):
                            n = 0
                            for h in range(2):
                                for a, b in ((0, 0), (0, 1), (1, 0)):
                                    last = mm(bank[5][:, bq * 96:bq * 96 + 96], r[a][:, og % 2, h, bq * 128:bq * 128 + 128], fwd_y[b][:, h], start=(n == 0), stop=(n == 5))
                                    n += 1
                        last.then_inc(pe_g, 1)

                    def s_product(u, og):
                        pe.wait_ge(ev_gl, u + 1 + CREDIT)
                        pe.wait_ge(ev_s, u + CREDIT)
                        n = 0
                        for k in range(2):
                            for a, b in ((0, 0), (1, 0), (0, 1)):
                                last = mm(bank[6][0:96, 0:192], fwd_x[b][:, k], gs[a][:, og % 2, :, k, :], start=(n == 0), stop=(n == 5))
                                n += 1
                        last.then_inc(pe_s, 1)

                    def slot(c, s, first):
                        u = U + c * OG + s
                        t1_product(u, s, c)
                        if not first or s >= 1:
                            u_product(u - 1, (s - 1) % OG)
                        if not first or s >= 2:
                            q_product(u - 2, (s - 2) % OG, c if s >= 2 else c - 1)
                        if not last_layer and (not first or s >= 2):
                            g_product(u - 2, (s - 2) % OG)
                        if not last_layer and (not first or s >= 3):
                            s_product(u - 3, (s - 3) % OG)

                    pe.wait_ge(ev_ql, l * 2 + 2)
                    pe.wait_ge(ev_w1, l * 2 * M + 2 * M)
                    for s in range(OG):
                        slot(0, s, True)
                    with pe.Fori(1, NC_) as c:
                        for s in range(OG):
                            slot(c, s, False)
                    e = U + UNITS
                    u_product(e - 1, 7)
                    if not last_layer:
                        g_product(e - 2, 6)
                        s_product(e - 3, 5)
                        g_product(e - 1, 7)
                        s_product(e - 2, 6)
                        s_product(e - 1, 7)
                    q_product(e - 2, 6, NC_ - 1)
                    q_product(e - 1, 7, NC_ - 1)
                with pe.Fori(0, L - 1) as l:
                    layer(l, False)
                layer(L - 1, True)
                pe.wait_ge(b_l, 16 * len(b.loads))
                mm(bank[7][:, 0:D], b.c["wv1_l"][:], b.c["wo1"][:], start=True, stop=True).then_inc(wvo_p, 1)
                pe.wait_ge(q2_d, 1)
                for i in range(NC_ // 2):
                    pe.wait_ge(relu_d, 2 * i + 2)
                    for j in range(4):
                        last = mm(bank[i][32 * j:32 * j + 32, :], q2c[:], acc[:, 2 * i + j // 2, j % 2, :], start=True, stop=True)
                    last.then_inc(pe_f, 1)
                for i in range(NC_ // 2):
                    pe.wait_ge(ev_f, i + 1)
                    if i == NC_ // 2 - 1:
                        pe.wait_ge(wvo_h, 2)
                    for bq in range(BQ):
                        last = nc.tensor.transpose(bank[4 + i][:, 128 * bq:128 * bq + 128], head[:, i, 128 * bq:128 * bq + 128], ident[:])
                    last.then_inc(pe_f, 1)

            @block.scalar
            def _(act):
                cp = ACT.Copy
                for s in (ev_a, ev_th, ev_rh, ev_g):
                    act.sem_inc(s, CREDIT)
                act.wait_ge(p_pe, 1)
                for i in range(2):
                    nc.scalar.activation(g0.rearrange("p t r k -> p (t r k)")[:, i * 384:(i + 1) * 384], bank[i][:, 0:384], cp).then_inc(p_ev, 1)
                def layer(l, last_layer):
                    U = l * UNITS
                    for i in range(2):
                        act.wait_ge(ev_qt, l * 2 + i + 1)
                        nc.scalar.activation(q_st[0][:, 4 * i:4 * i + 4].rearrange("p a b -> p (a b)"), q_tmp[:].rearrange("p a b -> p (a b)"), cp).then_inc(ev_qh, 1)
                    for x in range(M):
                        for h in range(2):
                            act.wait_ge(pe_mix, l * 2 * M + 2 * x + h + 1 + CREDIT)
                            act.wait_ge(pe_w1, l * 2 * M + 2 * x + h - 1 + CREDIT)
                            nc.scalar.activation(ym[0:64, h].rearrange("p k b -> p (k b)"), bank[h][0:64, 0:HALF], cp).then_inc(ev_a, 1)

                    for h in range(2):
                        act.wait_ge(yin_l[h], l * NC_ * 32 + 32)
                        nc.scalar.activation(ys[0][:, h].rearrange("p o k q -> p (o k q)"), yin[:, h].rearrange("p o k q -> p (o k q)"), cp).then_inc(y_high, 1)

                    def t1_high(u, og):
                        act.wait_ge(pe_t, u + 1)
                        act.wait_ge(pe_u, 2 * u - 2 + CREDIT)
                        nc.scalar.activation(t1[0][0:112, og % 2], bank[7][0:112, :], cp).then_inc(ev_th, 1)

                    def r_high(u, og):
                        for h in range(2):
                            act.wait_ge(pe_u, 2 * u + h + 1 + CREDIT)
                            if h == 0 and not last_layer:
                                act.wait_ge(pe_g, u - 1 + CREDIT)
                            nc.scalar.activation(r[0][:, og % 2, h], bank[1 + h][:], ACT.Relu).then_inc(ev_rh, 1)

                    def g_copy(u, og):
                        act.wait_ge(pe_g, u + 1 + CREDIT)
                        act.wait_ge(pe_s, u - 1 + CREDIT)
                        nc.scalar.activation(gs[0][:, og % 2].rearrange("p a b c -> p (a b c)"), bank[5][:, 0:384], cp, scale=GS_SCALE / G_SCALE).then_inc(ev_g, 1)

                    def slot(c, s, first):
                        u = U + c * OG + s
                        t1_high(u, s)
                        if not first or s >= 1:
                            r_high(u - 1, (s - 1) % OG)
                        if not last_layer and (not first or s >= 2):
                            g_copy(u - 2, (s - 2) % OG)

                    for s in range(OG):
                        slot(0, s, True)
                    with act.Fori(1, NC_) as c:
                        for s in range(OG):
                            slot(c, s, False)
                    e = U + UNITS
                    r_high(e - 1, 7)
                    if not last_layer:
                        g_copy(e - 2, 6)
                        g_copy(e - 1, 7)
                with act.Fori(0, L - 1) as l:
                    layer(l, False)
                layer(L - 1, True)
                for c in range(NC_):
                    act.wait_ge(ev_q, (L - 1) * NC_ + c + 1 + CREDIT)
                    v = acc[:, c].rearrange("p h n -> p (h n)")
                    nc.scalar.activation(v, v, ACT.Relu).then_inc(relu_d, 1)

            @block.vector
            def _(dve):
                V = nc.vector
                for s in (ev_w2, ev_b, ev_tl, ev_rl, ev_q, ev_s, ev_gl):
                    dve.sem_inc(s, CREDIT)
                V.memset(bank[7][:], 0.0)
                dve.wait_ge(p_pe, 2)
                for k in range(2):
                    last = V.tensor_copy(ss[:].rearrange("p a o k q -> p (a o) q k")[:, k:NC_:2],
                                         bank[2][0:96, 0:384].rearrange("p (s q c k) -> p c s q k", c=2, q=BQ, k=M)[:, k])
                last.then_inc(p_ev, 1)
                dve.wait_ge(ld, LOADED)
                V.tensor_scalar(bias_s64[:], bias_s[:, 0:4], float(S), None, ALU.mult)
                V.tensor_scalar(bias_1_64[:], bias_1[:], float(S), None, ALU.mult)
                V.tensor_scalar(q2c[:], eye[:, 0:Y32], q2s[:, 0:1], 1.0 / (H_SCALE * Q_SCALE), ALU.mult, ALU.mult).then_inc(q2_d, 1)
                V.tensor_reduce(p12[0:32, 2:3], bias_s[:, 0:5], mybir.AxisListType.X, ALU.add).then_inc(p_ev, 1)
                dve.wait_ge(p_pe, 3)
                V.tensor_scalar(w_img[:], bank[3][:, 0:1], H_SCALE, None, ALU.mult).then_inc(p_ev, 1)
                V.tensor_tensor(gl.rearrange("p (h n) -> p h n", h=2), grid_l.rearrange("p (h n) -> p h n", h=2),
                                bank[4][0:3, None, 0:128].broadcast_to((3, 2, 128)), ALU.mult).then_inc(p_ev, 1)
                dve.wait_ge(p_pe, 4)
                V.tensor_copy(g2[:], bank[5][:, 0:128]).then_inc(p_ev, 1)
                dve.wait_ge(zero, 2)

                def layer(l, last_layer):
                    U = l * UNITS
                    for i in range(2):
                        dve.wait_ge(pe_qb, l * 8 + 4 * i + 4)
                        if i == 1:
                            dve.wait_ge(ev_ql, l * 2 + 1)
                        V.tensor_tensor(q_tmp[:], bank[i][:].rearrange("p (a b) -> p a b", a=4), eye[:, None, :].broadcast_to((128, 4, 128)), ALU.mult).then_inc(ev_qt, 1)
                        dve.wait_ge(ev_qh, l * 2 + i + 1)
                        V.tensor_tensor(q_st[1][:, 4 * i:4 * i + 4], q_tmp[:], q_st[0][:, 4 * i:4 * i + 4], ALU.subtract).then_inc(ev_ql, 1)
                    s0 = Sp[0:32, 0, :, 0, :]
                    V.tensor_scalar(s0, s0, bias_s64[:, bass.ds(l, 1)], None, ALU.add).then_inc(bs_done, 1)
                    dve.wait_ge(bs_done, l + 1)

                    def s_update(x, h):
                        dve.wait_ge(pe_w2, l * 2 * M + 2 * x + h + 1 + CREDIT)
                        v = Sp[:, x, 8 * h:8 * h + 8].rearrange("p b k q -> p (b k q)")
                        V.tensor_tensor(v, v, bank[6][:, 0:HALF], ALU.add).then_inc(ev_w2, 1)

                    def mixed(x, h):
                        dve.wait_ge(pe_mix, l * 2 * M + 2 * x + h + 1 + CREDIT)
                        dve.wait_ge(pe_w1, l * 2 * M + 2 * x + h - 1 + CREDIT)
                        V.tensor_copy(ym[64:128, h].rearrange("p k b -> p (k b)"), bank[2 + h][64:128, 0:HALF]).then_inc(ev_b, 1)

                    def y1_copy(x, h):
                        dve.wait_ge(pe_w1, l * 2 * M + 2 * x + h + 1 + CREDIT)
                        if x >= 2:
                            dve.wait_ge(y_st[x % 2], l * 6 * 16 + (x // 2) * 16)
                        V.tensor_copy(y1[:, x % 2, :, 6 * h:6 * h + 6, :].rearrange("p b k q -> p k b q"),
                                      bank[4 + h][:, 0:HALF].rearrange("p (k b q) -> p k b q", b=NB, q=BQ)).then_inc(ev_w1, 1)
                        if x == 0 and h == 0:
                            dve.wait_ge(ev_w1, l * 2 * M + 1)
                            y0 = y1[0:32, 0, :, 0, :]
                            V.tensor_scalar(y0, y0, bias_1_64[:, bass.ds(l, 1)], None, ALU.add).then_inc(ev_db, 1)

                    for x in range(M + 1):
                        for h in range(2):
                            if x < M:
                                s_update(x, h)
                            if x >= 1:
                                mixed(x - 1, h)
                                if h == 1:
                                    y1_copy(x - 1, 0)
                            if h == 0 and x >= 2:
                                y1_copy(x - 2, 1)
                    y1_copy(M - 1, 1)

                    for h in range(2):
                        dve.wait_ge(y_high, l * 2 * NC_ + h + 1)
                        flat = lambda t: t[:, h].rearrange("p o k q -> p (o k q)")
                        V.tensor_tensor(flat(ys[1]), flat(yin), flat(ys[0]), ALU.subtract).then_inc(y_split, 1)

                    def t1_low(u, og):
                        dve.wait_ge(ev_th, u + 1 + CREDIT)
                        V.tensor_tensor(t1[1][0:112, og % 2], bank[7][0:112, :], t1[0][0:112, og % 2], ALU.subtract).then_inc(ev_tl, 1)

                    def r_low(u, og):
                        for h in range(2):
                            dve.wait_ge(ev_rh, 2 * u + h + 1 + CREDIT)
                            V.scalar_tensor_tensor(r[1][:, og % 2, h], bank[1 + h][:], 0.0, r[0][:, og % 2, h], ALU.max, ALU.subtract).then_inc(ev_rl, 1)

                    def g_low(u, og):
                        dve.wait_ge(ev_g, u + 1 + CREDIT)
                        V.scalar_tensor_tensor(gs[1][:, og % 2].rearrange("p a b c -> p (a b c)"), bank[5][:, 0:384], GS_SCALE / G_SCALE,
                                               gs[0][:, og % 2].rearrange("p a b c -> p (a b c)"), ALU.mult, ALU.subtract).then_inc(ev_gl, 1)

                    def s_copy(u, og, c_last):
                        dve.wait_ge(pe_s, u + 1 + CREDIT)
                        if og % 4 == 0:
                            dve.wait_ge(s_out[og // 4], l * NC_ * 32 + c_last * 32 + CREDIT)
                        V.tensor_scalar(ss[:, og // 4, (og % 4) * 4:(og % 4) * 4 + 4].rearrange("p o k q -> p q (o k)"),
                                        bank[6][0:96, 0:192].rearrange("p (q n) -> p q n", q=BQ), 1 / (GS_SCALE * X_SCALE), None, ALU.mult).then_inc(ev_s, 1)

                    def q_add(c):
                        dve.wait_ge(acc_ready, 2 * NC_)
                        dve.wait_ge(pe_q, l * NC_ + c + 1 + CREDIT)
                        for h in range(2):
                            v = acc[:, bass.ds(c, 1), h].rearrange("p c n -> p (c n)") if not isinstance(c, int) else acc[:, c, h]
                            last = V.tensor_tensor(v, v, bank[3 + h][:], ALU.add)
                        last.then_inc(ev_q, 1)

                    def slot(c, s, first):
                        u = U + c * OG + s
                        t1_low(u, s)
                        if not first or s >= 1:
                            r_low(u - 1, (s - 1) % OG)
                        if not first and s == 1:
                            q_add(c - 1)
                        if not last_layer and (not first or s >= 2):
                            g_low(u - 2, (s - 2) % OG)
                        if not last_layer and (not first or s >= 3):
                            s_copy(u - 3, (s - 3) % OG, c if s >= 3 else c - 1)

                    for s in range(OG):
                        slot(0, s, True)
                    with dve.Fori(1, NC_) as c:
                        for s in range(OG):
                            slot(c, s, False)
                    e = U + UNITS
                    r_low(e - 1, 7)
                    if not last_layer:
                        g_low(e - 2, 6)
                        s_copy(e - 3, 5, NC_ - 1)
                        g_low(e - 1, 7)
                        s_copy(e - 2, 6, NC_ - 1)
                        s_copy(e - 1, 7, NC_ - 1)
                    q_add(NC_ - 1)
                with dve.Fori(0, L - 1) as l:
                    layer(l, False)
                layer(L - 1, True)
                dve.wait_ge(wvo_p, 1)
                V.tensor_copy(b.wvo_h[:], bank[7][:, 0:D]).then_inc(wvo_h, 1)
                dve.wait_ge(wvo_h, 1)
                V.tensor_tensor(b.wvo_l[0:64], bank[7][0:64, 0:D], b.wvo_h[0:64], ALU.subtract).then_inc(wvo_h, 1)
                for i in range(NC_ // 2):
                    dve.wait_ge(pe_f, i + 1)
                    V.tensor_scalar(head[:, i], bank[i][:], q2b[:, 0:1], None, ALU.add).then_inc(ev_f, 1)
                for i in range(NC_ // 2):
                    dve.wait_ge(pe_f, NC_ // 2 + i + 1)
                    V.tensor_copy(tok[:, 8 * i:8 * i + 8].rearrange("p (c q) y -> p q c y", c=2),
                                  bank[4 + i][:].rearrange("p (q c y) -> p q c y", q=BQ, c=2)).then_inc(ev_f, 1)

        tokens(nc, d, tok, b, ident, bank, sem, out)


D, E, G_TILES, STEPS = 64, 8, 4, 4
GT = G_TILES * 128
T_BANKS, LG_BANKS = (0, 1, 4, 5), (2, 3, 6, 7)
PAD = 4
HID = 4
GAMMA, THETA, EPS, MIN_SUM = 0.96875, 10000.0, 1e-5, 1e-12


def token_constants():
    n = np.arange(S)
    inv_freq = (1.0 / np.float32(THETA) ** (np.arange(0, D, 2, dtype=np.float32) / np.float32(D))).astype(np.float32)
    ang = (n.astype(np.float32)[:, None] * inv_freq[None, :]).astype(np.float64)
    cos = np.repeat(np.cos(ang).T, 2, axis=0)
    sin = np.repeat(np.sin(ang).T, 2, axis=0)
    sin[0::2] *= -1.0
    diff = n[None, :] - n[:, None]
    decay = np.where(diff >= 0, np.exp(np.maximum(diff, 0) * np.log(GAMMA)), 0.0)
    causal = np.where(diff >= 0, 1.0 / np.maximum(n, 1)[None, :], 0.0)
    side = lambda m: np.kron(np.eye(2), m)
    f = lambda a: np.ascontiguousarray(a, dtype=np.float32)
    return {"rope_cos": f(np.tile(cos, (2, 1))), "rope_sin": f(np.tile(sin, (2, 1))),
            "mask0": f(side(decay)), "mask1": f(side(causal)), "ident": f(np.eye(128))}


W64 = {"wqk0": 128, "wqks0": 128, "wv0": 64, "gate_w0": E, "w1_0": E * 128, "wqk1": 128, "gate_w1": E, "w1_1": E * D}
W64_AT = {n: sum(list(W64.values())[:k]) for k, n in enumerate(W64)}
W64_N = sum(W64.values())


class Buffers:
    pass


def token_buffers(sb, area_a, area_b, area_c):
    f32, f16 = mybir.dt.float32, mybir.dt.float16
    used = [0]

    def view(area, n, p=128):
        a = area[0:p, used[0]:used[0] + n]
        used[0] += n
        return a

    two = lambda a: a.rearrange("p (j n) -> p j n", j=2)
    b = Buffers()
    b.x = view(area_a, 1024).rearrange("p (j t d) -> p j t d", j=4, t=G_TILES)
    b.v = two(view(area_a, 1024))
    b.rope_a, b.rope_b = two(view(area_a, 1024)), two(view(area_a, 1024))
    b.q_t, b.k_t = two(view(area_a, 1024, 64)), two(view(area_a, 1024, 64))
    b.att = two(view(area_a, 1024))
    b.w64 = view(area_a, W64_N)
    used[0] = 0
    b.prod = view(area_b, 2048).rearrange("p (t n) -> p t n", t=G_TILES)
    b.stats = view(area_b, 48).rearrange("p (t n) -> p t n", t=8)
    b.mv = view(area_b, 16).rearrange("p (t n) -> p t n", t=8)
    b.mean, b.rstd, b.var_eps = view(area_b, 32), view(area_b, 32), view(area_b, 32)
    b.gate, b.prob, b.top, b.wgt = (view(area_b, 256).rearrange("p (t e) -> p t e", e=E) for _ in range(4))
    b.ties = [view(area_b, 32 * (PAD + E)).rearrange("p (t e) -> p t e", e=PAD + E) for _ in range(3)]
    b.row_max, b.row_sum = view(area_b, 32), view(area_b, 32)
    b.xs = view(area_b, 2048).bitcast(f16)
    b.b2f = view(area_b, 1024, 1)
    b.w2f = [view(area_b, 512), view(area_b, 512)]
    used[0] = 0
    b.hid = view(area_c, HID * GT).rearrange("p (j n) -> p j n", j=HID)
    b.hid_h, b.hid_l = (view(area_c, HID * GT // 2).bitcast(f16).rearrange("p (j n) -> p j n", j=HID) for _ in "hl")
    b.minus_half = sb("minus_half", [128, 8])
    b.w64_h, b.w64_l = sb("w64_h", [128, W64_N], f16), sb("w64_l", [128, W64_N], f16)
    b.w2_h = [sb(f"w2_h{n}", [128, 512], f16) for n in range(2)]
    b.w2_l = [sb(f"w2_l{n}", [128, 512], f16) for n in range(2)]
    b.wvo_h, b.wvo_l = sb("wvo_h", [128, D], f16), sb("wvo_l", [128, D], f16)
    b.b2hl = sb("b2hl", [33, 2, E * D], f16)
    b.ones = sb("ones33", [33, 128], f16)
    names = {"rope_cos": [128, D], "rope_sin": [128, D], "mask0": [128, 128], "mask1": [128, 128],
             "wv1_l": [64, 128], "wo1": [64, D], "gate_b": [128, E], "b1_0": [128, E], "b1_1": [128, E // 2]}
    b.c = {n: sb("c_" + n, shape) for n, shape in names.items()}
    b.loads = [(b.c[n][:], n) for n in names] + [(b.w64, "w64"), (b.w2f[0], "w2_0"), (b.w2f[1], "w2_1"), (b.b2f, "b2")]
    return b


def tokens(nc, d, tok, b, ident, bank, sem, out):
    ALU, ACT, X_AXIS = mybir.AluOpType, mybir.ActivationFunctionType, mybir.AxisListType.X
    x, v, rope_a, rope_b, q_t, k_t, att = b.x, b.v, b.rope_a, b.rope_b, b.q_t, b.k_t, b.att
    prod, stats, mv, mean, rstd, var_eps = b.prod, b.stats, b.mv, b.mean, b.rstd, b.var_eps
    gate, prob, top, wgt, row_max, row_sum = b.gate, b.prob, b.top, b.wgt, b.row_max, b.row_sum
    xs, hid, hid_h, hid_l, minus_half, c = b.xs, b.hid, b.hid_h, b.hid_l, b.minus_half, b.c
    w64_h, w64_l, w2_h, w2_l, wvo_h, wvo_l, b2hl, ones = b.w64_h, b.w64_l, b.w2_h, b.w2_l, b.wvo_h, b.wvo_l, b.b2hl, b.ones
    ties = b.ties
    hid_bank = [bank[k] for k in (0, 1, 6, 7)]
    s = {}
    for kind, n in (("attn", 2), ("gatein", 2), ("moe", 2)):
        for i in range(n):
            s[kind + str(i)] = {m: sem(f"{kind}{i}_{m}") for m in {
                "attn": ("bn", "dev", "var", "rstd", "x", "tr", "xh", "xl", "qk", "rope_t", "q", "k", "v", "vc", "sc", "att", "ctx", "h"),
                "gatein": ("bn", "dev", "var", "rstd", "x", "tr", "xh", "xl", "lg", "lgc", "res"),
                "moe": ("hid", "high", "low", "y", "free", "sum", "h")}[kind]}
    gate_s, shifted, exp_s = sem("gate_step"), sem("logits_shifted"), sem("logits_exponentiated")
    done, stood = sem("stored"), sem("token_wait_stood_apart")
    gate_count = [0]

    def group(a, i, j):
        return a[:, bass.ds(i * 8 + 4 * j, 4)]

    def w(n, half, a=0, b=None):
        at = W64_AT[n]
        return (w64_h, w64_l)[half][:, at + a:at + (W64[n] if b is None else b)]

    def steps(eng, first, body):
        first()
        with eng.Fori(0, STEPS - 1) as i:
            body(i, False)
        body(STEPS - 1, True)

    with nc.Block() as block:
        @block.sync
        def _(sp):
            with sp.Fori(0, STEPS) as i:
                for j in range(2):
                    wait_apart(sp, s["moe1"]["h"], i * 2 + j + 1 + CREDIT, stood)
                    for bh in range(BH):
                        sp.dma_start(out[bass.ds(i * 4 + 2 * j + bh, 1)].rearrange("a q x y -> x (a q) y"),
                                     tok[64 * bh:64 * bh + 64, bass.ds(i * 8 + 4 * j, 4)]).then_inc(done, 16)
            sp.wait_ge(done, 16 * 4 * STEPS)

        @block.tensor
        def _(pe):
            mm = nc.tensor.matmul

            def transposes(m, i):
                wait_apart(pe, m["x"], i + 1, stood)
                for j in range(2):
                    if not isinstance(i, int) or i > 0:
                        wait_apart(pe, m["xl"], i * 2 + j - 1, stood)
                    for t in range(G_TILES):
                        last = nc.tensor.transpose(bank[j][0:64, t * 128:(t + 1) * 128], x[:, j, t], ident[:])
                    last.then_inc(m["tr"], 1)

            def with_tokens(o, w_h, w_l, cols):
                mm(o, w_h, cols, start=True, stop=False)
                return mm(o, w_l, cols, start=False, stop=True)

            def attention(n):
                m = s[f"attn{n}"]

                def body(i, last_step):
                    for j in range(2):
                        cols = xs[:, bass.ds(i * 1024 + 512 * j, 512)]
                        pe.wait_ge(m["xl"], i * 2 + j + 1)
                        last = with_tokens(bank[2 + j][:], w(f"wqk{n}", 0), w(f"wqk{n}", 1), cols)
                        if n == 0:
                            last = with_tokens(bank[4 + j][:], w("wqks0", 0), w("wqks0", 1), cols)
                        last.then_inc(m["qk"], 1)
                    wait_apart(pe, m["h"], i * 2 + CREDIT, stood)
                    for j in range(2):
                        for t in range(G_TILES):
                            tile = xs[:, bass.ds(i * 1024 + 512 * j + 128 * t, 128)]
                            o = bank[6 + j][:, t * D:(t + 1) * D]
                            mm(o, tile, w("wv0", 0) if n == 0 else wvo_h[:], start=True, stop=False)
                            last = mm(o, tile, w("wv0", 1) if n == 0 else wvo_l[:], start=False, stop=True)
                        last.then_inc(m["v"], 1)
                    for j in range(2):
                        pe.wait_ge(m["q"], i * 2 + j + 1)
                        pe.wait_ge(m["k"], i * 2 + j + 1)
                        for t in range(G_TILES):
                            k = slice(t * 128, (t + 1) * 128)
                            last = mm(bank[4 + j][:, k], k_t[:, j, k], q_t[:, j, k], start=True, stop=True)
                        last.then_inc(m["sc"], 1)
                    if not last_step:
                        transposes(m, i + 1)
                    for j in range(2):
                        pe.wait_ge(m["att"], i * 2 + j + 1)
                        pe.wait_ge(m["vc"], i * 2 + j + 1)
                        for t in range(G_TILES):
                            k = slice(t * 128, (t + 1) * 128)
                            last = mm(bank[6 + j][:, k], att[:, j, k], v[:, j, k], start=True, stop=True)
                        last.then_inc(m["ctx"], 1)

                steps(pe, lambda: transposes(m, 0), body)

            def gate_inputs(n):
                m = s[f"gatein{n}"]
                with pe.Fori(0, STEPS // 2) as half:
                    for k in range(4):
                        if k % 2 == 0:
                            wait_apart(pe, m["x"], half * 2 + k // 2 + 1, stood)
                        for t in range(G_TILES):
                            last = nc.tensor.transpose(bank[T_BANKS[k]][0:64, t * 128:(t + 1) * 128], x[:, k, t], ident[:])
                        last.then_inc(m["tr"], 1)
                    for k in range(4):
                        pe.wait_ge(m["xl"], half * 4 + k + 1)
                        for t in range(G_TILES):
                            tile = xs[:, bass.ds(half * 4 * GT + GT * k + 128 * t, 128)]
                            o = bank[LG_BANKS[k]][:, t * E:(t + 1) * E]
                            mm(o, tile, w(f"gate_w{n}", 0), start=True, stop=False)
                            last = mm(o, tile, w(f"gate_w{n}", 1), start=False, stop=True)
                        last.then_inc(m["lg"], 1)
                    pe.wait_ge(m["lgc"], half * 4 + 4)

            def experts(n):
                m = s[f"moe{n}"]
                H = E if n == 0 else E // 2
                W = D if n == 0 else 128
                pe.sem_inc(m["y"], CREDIT)

                def hidden(i, k):
                    pe.wait_ge(m["high"], i * 2 * H + k - HID + 1 + CREDIT)
                    e = k % H
                    w_h, w_l = (w(f"w1_{n}", half, e * 128, (e + 1) * 128) for half in range(2))
                    with_tokens(hid_bank[k % HID][:], w_h, w_l, xs[:, bass.ds(i * 1024 + GT * (k // H), GT)]).then_inc(m["hid"], 1)

                def first():
                    for k in range(HID - 1):
                        hidden(0, k)

                def body(i, last_step):
                    for k in range(2 * H):
                        j, e = k // H, k % H
                        if k + HID - 1 < 2 * H:
                            hidden(i, k + HID - 1)
                        elif not last_step:
                            hidden(i + 1, k + HID - 1 - 2 * H)
                        pe.wait_ge(m["low"], i * 2 * H + k + 1)
                        for t in range(G_TILES):
                            if e == 0:
                                pe.wait_ge(m["free"], i * 8 + j * 4 + t + 1 - 4 + CREDIT)
                                mm(bank[2 + t][:], ones[:], b2hl[:, n], start=True, stop=False)
                            o = bank[2 + t][:, e * W:(e + 1) * W]
                            for a, b in ((hid_h, w2_h), (hid_h, w2_l), (hid_l, w2_h)):
                                last = mm(o, a[:, k % HID, t * 128:(t + 1) * 128], b[n][:, e * W:(e + 1) * W], start=False, stop=(e == H - 1 and a is hid_l))
                        last.then_inc(m["y"], 1)

                steps(pe, first, body)

            attention(0)
            gate_inputs(0)
            experts(0)
            attention(1)
            gate_inputs(1)
            experts(1)

        @block.scalar
        def _(act):
            cp = ACT.Copy

            def high(m, i, banks=(0, 1)):
                for j in range(2):
                    act.wait_ge(m["tr"], i * 2 + j + 1)
                    nc.scalar.activation(xs[0:64, bass.ds(i * 1024 + 512 * j, 512)], bank[banks[j]][0:64, :], cp).then_inc(m["xh"], 1)

            def attention(n):
                m = s[f"attn{n}"]

                def body(i, last_step):
                    for j in range(2):
                        act.wait_ge(m["v"], i * 2 + j + 1)
                        nc.scalar.activation(v[:, j].rearrange("p (t a d) -> p t a d", t=G_TILES, a=2),
                                             bank[6 + j][:, 0:256].rearrange("p (t d) -> p t d", t=G_TILES)[:, :, None, :].broadcast_to((128, G_TILES, 2, D)), cp).then_inc(m["vc"], 1)
                    if not last_step:
                        high(m, i + 1)

                steps(act, lambda: high(m, 0), body)

            def gate_inputs(n):
                m = s[f"gatein{n}"]
                with act.Fori(0, STEPS // 2) as half:
                    for k in range(2):
                        high(m, half * 2 + k, T_BANKS[2 * k:2 * k + 2])

            def experts(n):
                m = s[f"moe{n}"]
                H = E if n == 0 else E // 2
                act.sem_inc(m["high"], CREDIT)
                act.wait_ge(shifted, n + 1)
                p2 = prob.rearrange("p t e -> p (t e)")
                nc.scalar.activation(p2, p2, ACT.Exp).then_inc(exp_s, 1)
                with act.Fori(0, STEPS) as i:
                    for k in range(2 * H):
                        act.wait_ge(m["hid"], i * 2 * H + k + 1)
                        act.wait_ge(m["y"], i * 2 * H + k - HID + 1 + CREDIT)
                        bias = c[f"b1_{n}"][:, k % H:k % H + 1]
                        nc.scalar.activation(hid[:, k % HID], hid_bank[k % HID][:], ACT.Gelu, bias=bias)
                        nc.scalar.activation(hid_h[:, k % HID], hid_bank[k % HID][:], ACT.Gelu, bias=bias).then_inc(m["high"], 1)

            attention(0)
            gate_inputs(0)
            experts(0)
            attention(1)
            gate_inputs(1)
            experts(1)

        @block.gpsimd
        def _(pool):
            def deviations(m, i):
                pool.wait_ge(m["var"], i + 1)
                k = bass.ds(i * 8, 8)
                nc.gpsimd.tensor_tensor(rstd[:, k], var_eps[:, k], minus_half[:], ALU.pow).then_inc(m["rstd"], 1)

            m = s["attn0"]
            for i in range(STEPS):
                deviations(m, i)

            def rotate(i):
                for j in range(2):
                    pool.wait_ge(m["rope_t"], i * 2 + j + 1)
                    nc.gpsimd.tensor_tensor(q_t[:, j], rope_a[0:64, j], rope_b[0:64, j], ALU.add).then_inc(m["q"], 1)

            rotate(0)
            with pool.Fori(1, STEPS) as i:
                rotate(i)
                deviations(s["gatein0"], i - 1)
            deviations(s["gatein0"], STEPS - 1)

            def combine(m, i, j):
                pool.wait_ge(m["free"], i * 8 + 4 * j + 4 + CREDIT)
                for k in range(3):
                    n = E * D >> (k + 1)
                    if k:
                        wait_apart(pool, m["sum"], i * 6 + 3 * j + k, stood)
                    half = prod[:, :, 0:n]
                    nc.gpsimd.tensor_tensor(half, half, prod[:, :, n:2 * n], ALU.add).then_inc(m["sum"], 1)
                wait_apart(pool, m["sum"], i * 6 + 3 * j + 3, stood)
                h = group(tok, i, j)
                nc.gpsimd.tensor_tensor(h, h, prod[:, :, 0:D], ALU.add).then_inc(m["h"], 1)

            with pool.Fori(0, STEPS) as i:
                for j in range(2):
                    combine(s["moe0"], i, j)
                deviations(s["attn1"], i)
            with pool.Fori(0, STEPS) as i:
                deviations(s["gatein1"], i)
            with pool.Fori(0, STEPS) as i:
                for j in range(2):
                    combine(s["moe1"], i, j)

        @block.vector
        def _(dve):
            V = nc.vector

            def statistics(m, i):
                for t in range(2 * G_TILES):
                    V.bn_stats(stats[:, t], tok[:, bass.ds(i * 8 + t, 1)].rearrange("p a n -> p (a n)")).then_inc(m["bn"], 1)
                wait_apart(dve, m["bn"], i * 16 + 8, stood)
                for t in range(2 * G_TILES):
                    V.bn_aggr(mv[:, t], stats[:, t]).then_inc(m["bn"], 1)
                dve.wait_ge(m["bn"], i * 16 + 16)
                k = bass.ds(i * 8, 8)
                V.tensor_copy(mean[:, k], mv[:, :, 0])
                V.tensor_scalar(var_eps[:, k], mv[:, :, 1], EPS, None, ALU.add).then_inc(m["var"], 1)
                wait_apart(dve, m["var"], i + 1, stood)

            def layernorm(m, i, slots=slice(0, 2)):
                k = bass.ds(i * 8, 8)
                wide = lambda a: a.broadcast_to((128, 8, D))
                xi = x[:, slots].rearrange("p j t d -> p (j t) d")
                V.tensor_tensor(xi, tok[:, k], wide(mean[:, k, None]), ALU.subtract).then_inc(m["dev"], 1)
                dve.wait_ge(m["dev"], i + 1)
                dve.wait_ge(m["rstd"], i + 1)
                V.tensor_tensor(xi, xi, wide(rstd[:, k, None]), ALU.mult).then_inc(m["x"], 1)

            def low(m, i, banks=(0, 1)):
                for j in range(2):
                    dve.wait_ge(m["xh"], i * 2 + j + 1)
                    cols = bass.ds(i * 1024 + 512 * j, 512)
                    V.tensor_tensor(xs[64:128, cols], bank[banks[j]][0:64, :], xs[0:64, cols], ALU.subtract).then_inc(m["xl"], 1)

            def attention(n):
                m = s[f"attn{n}"]
                dve.sem_inc(m["h"], CREDIT)

                def first():
                    layernorm(m, 0)
                    if n == 0:
                        statistics(m, 2)
                    low(m, 0)
                    if n == 1:
                        dve.wait_ge(s["moe0"]["h"], 2 * STEPS + CREDIT)
                    statistics(m, 3)

                def statistics_of(i):
                    wait_apart(dve, m["h"], i * 2 + 2 + CREDIT, stood)
                    statistics(s[f"gatein{n}"], i)

                def body(i, first_step, last_step):
                    for j in range(2):
                        dve.wait_ge(m["qk"], i * 2 + j + 1)
                        if n == 0:
                            for dst, b, table in ((rope_a, 2, "rope_cos"), (rope_b, 4, "rope_sin")):
                                last = V.tensor_tensor(dst[:, j].rearrange("p (b x) -> p b x", x=S), bank[b + j][:].rearrange("p (b x) -> p b x", x=S),
                                                       c[table][:, None, :].broadcast_to((128, 8, S)), ALU.mult)
                            last.then_inc(m["rope_t"], 1)
                            dve.wait_ge(m["rope_t"], i * 2 + j + 1)
                            V.tensor_tensor(k_t[:, j], rope_a[64:128, j], rope_b[64:128, j], ALU.add).then_inc(m["k"], 1)
                        else:
                            V.tensor_copy(q_t[:, j], bank[2 + j][0:64, :]).then_inc(m["q"], 1)
                            V.tensor_copy(k_t[:, j], bank[2 + j][64:128, :]).then_inc(m["k"], 1)
                    if not last_step:
                        dve.wait_ge(m["tr"], i * 2 + 2)
                        layernorm(m, i + 1)
                    if not first_step:
                        statistics_of(i - 1)
                    for j in range(2):
                        dve.wait_ge(m["sc"], i * 2 + j + 1)
                        sc = bank[4 + j][:].rearrange("p (t n) -> p t n", t=G_TILES)
                        mask = c[f"mask{n}"][:, None, :].broadcast_to((128, G_TILES, 128))
                        o = att[:, j].rearrange("p (t n) -> p t n", t=G_TILES)
                        if n == 0:
                            V.tensor_tensor(o, sc, mask, ALU.mult).then_inc(m["att"], 1)
                        else:
                            V.scalar_tensor_tensor(o, sc, 0.0, mask, ALU.max, ALU.mult).then_inc(m["att"], 1)
                    if not last_step:
                        low(m, i + 1)
                    for j in range(2):
                        dve.wait_ge(m["ctx"], i * 2 + j + 1)
                        h = group(tok, i, j)
                        V.tensor_tensor(h, h, bank[6 + j][:].rearrange("p (t n) -> p t n", t=G_TILES)[:, :, 0:D], ALU.add).then_inc(m["h"], 1)

                first()
                body(0, True, False)
                with dve.Fori(1, STEPS - 1) as i:
                    body(i, False, False)
                body(STEPS - 1, False, True)

            def gate_inputs(n):
                m = s[f"gatein{n}"]
                for half in range(STEPS // 2):
                    for k in range(2):
                        layernorm(m, half * 2 + k, slice(2 * k, 2 * k + 2))
                    if half == 0:
                        dve.wait_ge(s[f"attn{n}"]["h"], 2 * STEPS + CREDIT)
                        statistics(m, STEPS - 1)
                    for k in range(2):
                        i = half * 2 + k
                        if n == 1:
                            dve.wait_ge(m["x"], i + 1)
                            h = tok[:, bass.ds(i * 8, 8)]
                            V.tensor_tensor(h, h, x[:, 2 * k:2 * k + 2].rearrange("p j t d -> p (j t) d"), ALU.add).then_inc(m["res"], 1)
                        low(m, i, T_BANKS[2 * k:2 * k + 2])
                    if n == 1:
                        dve.wait_ge(m["res"], half * 2 + 2)
                    for k in range(4):
                        dve.wait_ge(m["lg"], half * 4 + k + 1)
                        lg = bank[LG_BANKS[k]][:, 0:32].rearrange("p (t e) -> p t e", e=E)
                        g = gate[:, bass.ds(half * 16 + 4 * k, 4)]
                        if n == 0:
                            V.tensor_tensor(g, lg, c["gate_b"][:, None, :].broadcast_to((128, G_TILES, E)), ALU.add).then_inc(m["lgc"], 1)
                        else:
                            V.tensor_copy(g, lg).then_inc(m["lgc"], 1)

            def gate_step(ins):
                gate_count[0] += 1
                ins.then_inc(gate_s, 1)
                dve.wait_ge(gate_s, gate_count[0])

            def wide(a):
                return a[:, :, None].broadcast_to((128, 32, E))

            def shift_logits(n):
                gate_step(V.tensor_reduce(row_max, gate, X_AXIS, ALU.max))
                V.tensor_tensor(prob, gate, wide(row_max), ALU.subtract).then_inc(shifted, 1)

            def top_two(n):
                dve.wait_ge(exp_s, n + 1)
                gate_step(V.tensor_reduce(row_sum, prob, X_AXIS, ALU.add))
                gate_step(V.reciprocal(row_sum, row_sum))
                gate_step(V.tensor_tensor(prob, prob, wide(row_sum), ALU.mult))
                for t in range(32):
                    last = V.max(top[:, t], prob[:, t])
                gate_step(last)
                second = top[:, :, 1:2].broadcast_to((128, 32, E))
                gate_step(V.tensor_tensor(wgt, prob, second, ALU.is_gt))
                gate_step(V.tensor_reduce(row_max, wgt, X_AXIS, ALU.add))
                tie, sum_a, sum_b = (t[:, :, PAD:] for t in ties)
                gate_step(V.tensor_tensor(tie, prob, second, ALU.is_equal))
                for dst, src, back in ((sum_a, ties[0], 1), (sum_b, ties[1], 2), (sum_a, ties[2], 4)):
                    gate_step(V.tensor_tensor(dst, src[:, :, PAD:], src[:, :, PAD - back:PAD - back + E], ALU.add))
                gate_step(V.tensor_tensor(sum_a, sum_a, wide(row_max), ALU.add))
                gate_step(V.scalar_tensor_tensor(tie, sum_a, 2.0, tie, ALU.is_le, ALU.mult))
                gate_step(V.tensor_tensor(wgt, wgt, tie, ALU.add))
                gate_step(V.tensor_tensor(wgt, wgt, prob, ALU.mult))
                if n == 1:
                    gate_step(V.tensor_tensor(row_sum, top[:, :, 0], top[:, :, 1], ALU.add))
                    gate_step(V.tensor_scalar(row_sum, row_sum, MIN_SUM, None, ALU.max))
                    gate_step(V.reciprocal(row_sum, row_sum))
                    gate_step(V.tensor_tensor(wgt, wgt, wide(row_sum), ALU.mult))

            def experts(n):
                m = s[f"moe{n}"]
                H = E if n == 0 else E // 2
                dve.sem_inc(m["free"], CREDIT)
                dve.sem_inc(m["h"], CREDIT)

                def statistics_of(i):
                    if n == 0:
                        wait_apart(dve, m["h"], i * 2 + 2 + CREDIT, stood)
                        statistics(s["attn1"], i)

                def body(i, first):
                    for k in range(2 * H):
                        dve.wait_ge(m["high"], i * 2 * H + k + 1 + CREDIT)
                        V.tensor_tensor(hid_l[:, k % HID], hid[:, k % HID], hid_h[:, k % HID], ALU.subtract).then_inc(m["low"], 1)
                        if k == 3 and first:
                            top_two(n)
                        if k == H:
                            combine(n, i, 0)
                        if k == 0 and not first:
                            combine(n, i - 1, 1)
                        if k == H - 1 and not first:
                            statistics_of(i - 1)

                body(0, True)
                with dve.Fori(1, STEPS) as i:
                    body(i, False)
                combine(n, STEPS - 1, 1)

            def combine(n, i, j):
                m = s[f"moe{n}"]
                H = E if n == 0 else E // 2
                dve.wait_ge(m["y"], i * 2 * H + (j + 1) * H + CREDIT)
                dve.wait_ge(m["h"], i * 2 + j + CREDIT)
                for t in range(G_TILES):
                    wt = wgt[:, bass.ds(i * 8 + 4 * j + t, 1)].rearrange("p a e -> p (a e)")
                    V.tensor_tensor(prod[:, t].rearrange("p (e d) -> p e d", e=E), bank[2 + t][:].rearrange("p (e d) -> p e d", e=E),
                                    wt[:, :, None].broadcast_to((128, E, D)), ALU.mult).then_inc(m["free"], 1)

            for t in ties:
                last = V.memset(t, 0.0)
            gate_step(last)
            for i in range(2):
                statistics(s["attn0"], i)
            attention(0)
            gate_inputs(0)
            dve.wait_ge(s["gatein0"]["lgc"], 2 * STEPS)
            shift_logits(0)
            experts(0)
            attention(1)
            gate_inputs(1)
            dve.wait_ge(s["gatein1"]["lgc"], 2 * STEPS)
            dve.wait_ge(s["gatein1"]["res"], STEPS)
            shift_logits(1)
            experts(1)


def token_layout(inp):
    f = lambda a: np.ascontiguousarray(a, dtype=np.float32)
    g = lambda n: inp[n]
    swap = np.arange(D).reshape(-1, 2)[:, ::-1].ravel()
    o = {}
    parts = {
        "wqk0": np.concatenate([g("L0_attn_W_Q"), g("L0_attn_W_K")], 1),
        "wqks0": np.concatenate([g("L0_attn_W_Q")[:, swap], g("L0_attn_W_K")[:, swap]], 1),
        "wv0": g("L0_attn_W_V"), "gate_w0": g("L0_ffn_gate_w"),
        "w1_0": g("L0_ffn_W1").transpose(1, 0, 2).reshape(D, E * 128),
        "wqk1": np.concatenate([g("L1_attn_Wq").T, g("L1_attn_Wk").T], 1),
        "gate_w1": g("L1_ffn_router_w").T, "w1_1": g("L1_ffn_w1").transpose(1, 0, 2).reshape(D, E * D)}
    o["w64"] = f(np.tile(np.concatenate([parts[n] for n in W64], 1), (2, 1)))
    o["wv1_l"] = f(np.tile(g("L1_attn_Wv"), (1, 2)))
    o["wo1"] = f(g("L1_attn_Wo").T)
    o["gate_b"] = f(np.broadcast_to(g("L0_ffn_gate_b")[None], (128, E)))
    o["b1_0"] = f(g("L0_ffn_b1").T)
    o["b1_1"] = f(g("L1_ffn_b1").reshape(E // 2, 128).T)
    o["w2_0"] = f(g("L0_ffn_W2").transpose(1, 0, 2).reshape(128, E * D))
    w2 = np.zeros((E // 2, 2, D, 2, D), np.float32)
    for k in range(2):
        w2[:, k, :, k] = g("L1_ffn_w2").reshape(E // 2, 2, D, D)[:, k]
    o["w2_1"] = f(w2.transpose(1, 2, 0, 3, 4).reshape(128, E // 2 * 128))
    o["b2"] = f(np.concatenate([g("L0_ffn_b2").reshape(1, -1), g("L1_ffn_b2").reshape(1, -1)], 1))
    return o | token_constants()


def host_layout(x, inp):
    f = lambda a: np.ascontiguousarray(a)
    p_w, p_b, fw = inp["L0_tok_p_w"], inp["L0_tok_p_b"], inp["L0_tok_fw"]
    w1, b1, w2, b2 = inp["L0_tok_w1_w"], inp["L0_tok_w1_b"], inp["L0_tok_w2_w"], inp["L0_tok_w2_b"]
    q1, q1b, q2, q2b = inp["L0_tok_q1_w"], inp["L0_tok_q1_b"], inp["L0_tok_q2_w"], inp["L0_tok_q2_b"]
    o = {}
    o["xT"] = f(x[..., 0].reshape(NC_ // 2, 2, BH, BQ, S, S).transpose(1, 5, 0, 3, 2, 4).reshape(2 * S, NC_ // 2 * COLS))
    o["x_head"] = f(x[..., 0].reshape(NC_, BH, BQ, S, 2, Y32).transpose(5, 0, 4, 2, 1, 3).reshape(Y32, NC_ * 2 * COLS))
    w_in, w_1 = np.zeros((L + 1, 4, C, 4, C), np.float32), np.zeros((L + 1, 4, C, 4, C), np.float32)
    for q in range(4):
        w_in[0, q, :3, q] = p_w.T
        w_in[1:L, q, :, q] = w2[:L - 1].transpose(0, 2, 1)
        w_1[:L, q, :, q] = w1.transpose(0, 2, 1)
    o["w_in"], o["w_1"] = w_in.reshape(-1, 128), w_1.reshape(-1, 128)
    o["bias_s"] = f(np.concatenate([p_b[None], b2]).T)
    o["bias_1"] = f(b1.T)
    w = fw.transpose(0, 1, 2, 4, 5, 6, 3)
    o["w_modes"] = f(np.stack([w, w[..., ::-1, :]], 2).reshape(L * 128, M * M * 64))
    o["w2e"] = np.zeros(((L + 1) * C, C * Y32), np.float32)
    o["w2e"][:L * C] = np.repeat(w2.reshape(L * C, C), Y32, axis=1)
    q1a = np.concatenate([q1.T, q1b[None]])
    o["q1a"] = f(np.repeat(q1a, Y32, axis=1))
    p0 = np.zeros((33, 1), np.float32)
    p0[:32] = p_w[:, 0:1]
    p12 = np.zeros((33, 3), np.float32)
    p12[:32, :2] = p_w[:, 1:3]
    p12[32, 2] = 1.0
    o["p0"], o["p12"] = p0, p12
    o["q2s"] = f(np.repeat(q2[0], Y32)[:, None])
    o["q2b"] = f(np.broadcast_to(q2b.reshape(1, 1), (128, 1)))
    return o | dft_constants() | token_layout(inp)


def kernel(**inputs):
    import concourse.bacc as bacc
    from concourse.bass_utils import run_bass_kernel_spmd as run
    inp = {k: np.asarray(v) for k, v in inputs.items()}
    arrays = host_layout(inp["x"], inp)
    nc = bacc.Bacc("TRN2", target_bir_lowering=False, num_devices=1)
    d = {n: nc.dram_tensor("in_" + n, a.shape, mybir.dt.from_np(a.dtype), kind="ExternalInput").ap() for n, a in arrays.items()}
    out = nc.dram_tensor("out", (B // BQ, BQ, S, S), mybir.dt.float32, kind="ExternalOutput").ap()
    build_program(nc, d, out)
    r = run(nc, [{"in_" + n: a for n, a in arrays.items()}], core_ids=[0])
    return np.asarray(r.results[0]["out"]).reshape(B, S, S)
```
